# Optimizing a Trainium2 kernel written in Bass

```python
import numpy as np
import jax
import jax.numpy as jnp

def _softmax(x, axis=-1):
    return jax.nn.softmax(x, axis=axis)

def _gelu(x):
    return jax.nn.gelu(x, approximate=True)

def _silu(x):
    return jax.nn.silu(x)

def _sigmoid(x):
    return jax.nn.sigmoid(x)

def _layernorm(x, axis=-1, eps=1e-05):
    m = jnp.mean(x, axis=axis, keepdims=True)
    v = jnp.var(x, axis=axis, keepdims=True)
    return (x - m) / jnp.sqrt(v + eps)

def _scatter_add(tgt, idx, src, axis=0):
    return tgt.at[idx].add(src)

def _segment_sum(src, seg, n):
    return jax.ops.segment_sum(src, seg, n)
kernel_name = 'mk_hybrid_d1_jaxref_r8_4687b9'

def setup_inputs(seed: int=0):
    np.random.seed(seed)
    _w = jnp.asarray

    def _L0_attn_a_setup():
        import jax, jax.numpy as jnp
        import numpy as np
        from jax import lax
        BLOCK_LEN = 128
        NEG_INF = -1000000000.0
        key = jax.random.key(seed)
        ks = jax.random.split(key, 8)
        N, L, Dm = (2, 1024, 512)
        W, H, dh = (128, 16, 64)
        s = lambda fan: 1.0 / np.sqrt(fan)
        return {'inputs': jax.random.normal(ks[0], (N, L, Dm), jnp.float32), 'conv_w': jax.random.normal(ks[1], (3, Dm, 3 * W), jnp.float32) * s(3 * Dm), 'conv_b': jnp.zeros((3 * W,), jnp.float32), 'wq': jax.random.normal(ks[2], (W, H, dh), jnp.float32) * s(W), 'bq': jnp.zeros((H, dh), jnp.float32), 'wk': jax.random.normal(ks[3], (W, H, dh), jnp.float32) * s(W), 'bk': jnp.zeros((H, dh), jnp.float32), 'wv': jax.random.normal(ks[4], (W, H, dh), jnp.float32) * s(W), 'bv': jnp.zeros((H, dh), jnp.float32), 'wo': jax.random.normal(ks[5], (H, dh, W), jnp.float32) * s(H * dh), 'bo': jnp.zeros((W,), jnp.float32), 'proj_w': jax.random.normal(ks[6], (W, Dm), jnp.float32) * s(W), 'proj_b': jnp.zeros((Dm,), jnp.float32)}
    _L0_attn_a_in = _L0_attn_a_setup()

    def _L0_attn_b_setup():
        import jax, jax.numpy as jnp
        import numpy as np
        SEQ, BATCH, HIDDEN = (256, 1, 512)
        NUM_HEADS, NUM_KV_HEADS, HEAD_DIM = (32, 8, 128)
        Q_PER_GROUP = NUM_HEADS // NUM_KV_HEADS
        TOTAL_PROJ = NUM_KV_HEADS * (Q_PER_GROUP + 2) * HEAD_DIM
        key = jax.random.key(seed)
        k1, k2, k3 = jax.random.split(key, 3)
        tokens = jax.random.normal(k1, (SEQ, BATCH, HIDDEN), dtype=jnp.float32)
        weight_qkv = jax.random.normal(k2, (TOTAL_PROJ, HIDDEN), dtype=jnp.float32) * (2.0 / (TOTAL_PROJ + HIDDEN)) ** 0.5
        weight_proj = jax.random.normal(k3, (HIDDEN, NUM_HEADS * HEAD_DIM), dtype=jnp.float32) * (2.0 / (HIDDEN + NUM_HEADS * HEAD_DIM)) ** 0.5
        return {'tokens': tokens, 'weight_qkv': weight_qkv, 'weight_proj': weight_proj}
    _L0_attn_b_in = _L0_attn_b_setup()

    def _L0_ffn_setup():
        import jax, jax.numpy as jnp
        import numpy as np
        NUM_EXPERTS = 16
        TOP_K = 2
        INTER = 56
        key = jax.random.key(seed)
        k1, k2, k3, k4, k5 = jax.random.split(key, 5)
        B, S, H = (4, 256, 512)
        scale = 0.02
        return {'hid': jax.random.normal(k1, (B, S, H), dtype=jnp.float32), 'gate_w': jax.random.normal(k2, (NUM_EXPERTS, H), dtype=jnp.float32) * scale, 'u': jax.random.normal(k3, (NUM_EXPERTS * INTER, H), dtype=jnp.float32) * scale, 'g': jax.random.normal(k4, (NUM_EXPERTS * INTER, H), dtype=jnp.float32) * scale, 'd': jax.random.normal(k5, (H, NUM_EXPERTS * INTER), dtype=jnp.float32) * scale}
    _L0_ffn_in = _L0_ffn_setup()
    _d = {'L0_attn_a_inputs': _L0_attn_a_in['inputs'], 'L0_attn_a_conv_w': _L0_attn_a_in['conv_w'], 'L0_attn_a_conv_b': _L0_attn_a_in['conv_b'], 'L0_attn_a_wq': _L0_attn_a_in['wq'], 'L0_attn_a_bq': _L0_attn_a_in['bq'], 'L0_attn_a_wk': _L0_attn_a_in['wk'], 'L0_attn_a_bk': _L0_attn_a_in['bk'], 'L0_attn_a_wv': _L0_attn_a_in['wv'], 'L0_attn_a_bv': _L0_attn_a_in['bv'], 'L0_attn_a_wo': _L0_attn_a_in['wo'], 'L0_attn_a_bo': _L0_attn_a_in['bo'], 'L0_attn_a_proj_w': _L0_attn_a_in['proj_w'], 'L0_attn_a_proj_b': _L0_attn_a_in['proj_b'], 'L0_attn_b_weight_qkv': _L0_attn_b_in['weight_qkv'], 'L0_attn_b_weight_proj': _L0_attn_b_in['weight_proj'], 'L0_ffn_gate_w': _L0_ffn_in['gate_w'], 'L0_ffn_u': _L0_ffn_in['u'], 'L0_ffn_g': _L0_ffn_in['g'], 'L0_ffn_d': _L0_ffn_in['d']}
    _x0 = _d['L0_attn_a_inputs']
    _d['L0_attn_a_inputs'] = jax.random.normal(jax.random.fold_in(jax.random.key(seed), 1), (2, 1024, 512), dtype=_x0.dtype)
    del _x0
    return _d

def reference(L0_attn_a_inputs, L0_attn_a_conv_w, L0_attn_a_conv_b, L0_attn_a_wq, L0_attn_a_bq, L0_attn_a_wk, L0_attn_a_bk, L0_attn_a_wv, L0_attn_a_bv, L0_attn_a_wo, L0_attn_a_bo, L0_attn_a_proj_w, L0_attn_a_proj_b, L0_attn_b_weight_qkv, L0_attn_b_weight_proj, L0_ffn_gate_w, L0_ffn_u, L0_ffn_g, L0_ffn_d):

    def _L0_attn_a_ref(inputs, conv_w, conv_b, wq, bq, wk, bk, wv, bv, wo, bo, proj_w, proj_b):
        import jax, jax.numpy as jnp
        import numpy as np
        from jax import lax
        BLOCK_LEN = 128
        NEG_INF = -1000000000.0
        N, L, Dm = inputs.shape
        x = lax.conv_general_dilated(inputs, conv_w, window_strides=(1,), padding='SAME', dimension_numbers=('NWC', 'WIO', 'NWC')) + conv_b
        q, k, v = jnp.split(x, 3, axis=-1)
        W_ = q.shape[-1]
        nb = L // BLOCK_LEN
        q = q.reshape(N * nb, BLOCK_LEN, W_)
        k = k.reshape(N * nb, BLOCK_LEN, W_)
        v = v.reshape(N * nb, BLOCK_LEN, W_)
        dh = wq.shape[-1]
        qh = jnp.einsum('btd,dhe->bthe', q, wq) + bq
        kh = jnp.einsum('btd,dhe->bthe', k, wk) + bk
        vh = jnp.einsum('btd,dhe->bthe', v, wv) + bv
        scale = 1.0 / jnp.sqrt(jnp.asarray(dh, qh.dtype))
        scores = jnp.einsum('bqhe,bkhe->bhqk', qh * scale, kh)
        causal = jnp.tril(jnp.ones((BLOCK_LEN, BLOCK_LEN), bool))
        scores = jnp.where(causal, scores, NEG_INF)
        p = jax.nn.softmax(scores, axis=-1)
        o = jnp.einsum('bhqk,bkhe->bqhe', p, vh)
        o = jnp.einsum('bqhe,hed->bqd', o, wo) + bo
        o = o.reshape(N, L, W_)
        return o @ proj_w + proj_b

    def _L0_attn_b_ref(tokens, weight_qkv, weight_proj):
        import jax, jax.numpy as jnp
        import numpy as np
        SEQ, BATCH, HIDDEN = (256, 1, 512)
        NUM_HEADS, NUM_KV_HEADS, HEAD_DIM = (32, 8, 128)
        Q_PER_GROUP = NUM_HEADS // NUM_KV_HEADS
        TOTAL_PROJ = NUM_KV_HEADS * (Q_PER_GROUP + 2) * HEAD_DIM
        S, B, H = tokens.shape
        scale = 1.0 / HEAD_DIM ** 0.5
        qkv = jnp.einsum('sbh,ph->sbp', tokens, weight_qkv)
        qkv = qkv.reshape(S, B, NUM_KV_HEADS, Q_PER_GROUP + 2, HEAD_DIM)
        q = qkv[:, :, :, :Q_PER_GROUP, :].reshape(S, B, NUM_HEADS, HEAD_DIM)
        k = qkv[:, :, :, Q_PER_GROUP, :]
        v = qkv[:, :, :, Q_PER_GROUP + 1, :]
        k = jnp.repeat(k, Q_PER_GROUP, axis=2)
        v = jnp.repeat(v, Q_PER_GROUP, axis=2)
        q = q.transpose(1, 2, 0, 3)
        k = k.transpose(1, 2, 0, 3)
        v = v.transpose(1, 2, 0, 3)
        scores = jnp.einsum('bhsd,bhtd->bhst', q, k) * scale
        causal = jnp.tril(jnp.ones((S, S), dtype=bool))
        scores = jnp.where(causal, scores, jnp.finfo(scores.dtype).min)
        attn = jax.nn.softmax(scores, axis=-1)
        out = jnp.einsum('bhst,bhtd->bhsd', attn, v)
        out = out.transpose(2, 0, 1, 3).reshape(S, B, NUM_HEADS * HEAD_DIM)
        return jnp.einsum('sbe,he->sbh', out, weight_proj)

    def _L0_ffn_ref(hid, gate_w, u, g, d):
        import jax, jax.numpy as jnp
        import numpy as np
        NUM_EXPERTS = 16
        TOP_K = 2
        INTER = 56
        B, S, H = hid.shape
        x = hid.reshape(-1, H)
        bs = x.shape[0]
        logits = x @ gate_w.T
        probs = jax.nn.softmax(logits.astype(jnp.float32), axis=-1)
        vals, idx = jax.lax.top_k(probs, TOP_K)
        vals = vals / jnp.sum(vals, axis=-1, keepdims=True)
        rows = jnp.arange(bs)[:, None]
        w = jnp.zeros((bs, NUM_EXPERTS), dtype=jnp.float32).at[rows, idx].set(vals)
        w = w.astype(x.dtype)
        gate_out = (x @ g.T).reshape(bs, NUM_EXPERTS, INTER)
        up_out = (x @ u.T).reshape(bs, NUM_EXPERTS, INTER)
        h = jax.nn.silu(gate_out) * up_out
        d_r = d.reshape(H, NUM_EXPERTS, INTER)
        out = jnp.einsum('bei,hei,be->bh', h, d_r, w)
        return out.reshape(B, S, H)
    x = L0_attn_a_inputs
    x = x + _L0_attn_a_ref(_layernorm(x, axis=-1), L0_attn_a_conv_w, L0_attn_a_conv_b, L0_attn_a_wq, L0_attn_a_bq, L0_attn_a_wk, L0_attn_a_bk, L0_attn_a_wv, L0_attn_a_bv, L0_attn_a_wo, L0_attn_a_bo, L0_attn_a_proj_w, L0_attn_a_proj_b)
    x = x + _L0_ffn_ref(_layernorm(x, axis=-1), L0_ffn_gate_w, L0_ffn_u, L0_ffn_g, L0_ffn_d)
    x = x + _L0_attn_b_ref(_layernorm(x, axis=-1), L0_attn_b_weight_qkv, L0_attn_b_weight_proj)
    x = x + _L0_ffn_ref(_layernorm(x, axis=-1), L0_ffn_gate_w, L0_ffn_u, L0_ffn_g, L0_ffn_d)
    return x

_drawn_inputs = setup_inputs


def setup_inputs(seed=0):
    import zlib

    import numpy as np

    out = dict(_drawn_inputs(seed))
    spreads = {'L0_attn_a_conv_b': (0.0, 0.1),
     'L0_attn_a_bq': (0.0, 0.372),
     'L0_attn_a_bk': (0.0, 0.8),
     'L0_attn_a_bv': (0.0, 0.1),
     'L0_attn_a_bo': (0.0, 0.1),
     'L0_attn_a_proj_b': (0.0, 0.1)}
    factors = {'L0_ffn_gate_w': 3.243, 'L0_ffn_u': 3.026, 'L0_ffn_g': 3.082, 'L0_ffn_d': 3.024}
    for name, (base, spread) in spreads.items():
        noise = np.random.default_rng([zlib.crc32(name.encode()), seed]).standard_normal(out[name].shape)
        drawn = base * np.exp(spread * noise) if base else spread * noise
        out[name] = jnp.asarray(drawn.astype(out[name].dtype))
    for name, factor in factors.items():
        out[name] = (out[name] * factor).astype(out[name].dtype)
    return out
```

```python
from contextlib import ExitStack

import concourse.bass as bass
from concourse import mybir

F32 = mybir.dt.float32
F32R = mybir.dt.float32r
BF16 = mybir.dt.bfloat16
ACT = mybir.ActivationFunctionType
ALU = mybir.AluOpType
AX_X = mybir.AxisListType.X

P = 128
SEQS, LEN, DM = 2, 1024, 512
TOK = SEQS * LEN
TILES = TOK // P
KT = DM // P
GROUP = 512
GT = GROUP // P
GROUPS = TOK // GROUP
ST = LEN // P
EPS = 1e-5

TAPS, W, HA, EA = 3, 128, 16, 64
PADDED = LEN + TAPS - 1
HEAD_TILES = HA * EA // P
HPS = 4
BLOCK_STEPS = HA // HPS
STEPS = GT * BLOCK_STEPS
SCALE_A = EA ** -0.5
MASKED = -1e30

HB, KVB, EB = 32, 8, 128
QPG = HB // KVB
ROWS_G = (QPG + 2) * EB
SCALE_B = EB ** -0.5

EXPERTS, INTER = 16, 56
FF = EXPERTS * INTER
FT = FF // P
FFN_CHUNKS = 3 * KT
G_AT, U_AT, D_AT = 0, KT, 2 * KT

ds = bass.ds


def heads_of(step):
    return [8 * (step // 2) + 2 * m + step % 2 for m in range(HPS)]


def product3(pe, out, w_hi, w_lo, x_hi, x_lo, first, last):
    pe.matmul(out, w_hi, x_hi, start=first, stop=False)
    pe.matmul(out, w_hi, x_lo, start=False, stop=False)
    return pe.matmul(out, w_lo, x_hi, start=False, stop=last)


def wait_on_cell(eng, cell, sem, value):
    eng.wait_ge(sem, value)
    eng.tensor_tensor(cell[:, 0:1], cell[:, 1:2], cell[:, 1:2], ALU.mult)


def pool_copy(pool, out, src, zero):
    return pool.tensor_tensor(out, src, zero, ALU.add)


def take_hi(act, hi, src):
    return act.activation(hi, src, ACT.Copy)


def take_lo(eng, lo, src, hi):
    return eng.tensor_tensor(lo, src, hi.bitcast(F32), ALU.subtract)



def conv_stage(nc, psum, sem, x_sb, ident, qkvT, prefetch, dram):
    with ExitStack() as ctx:
        def buf(name, shape, dt=F32):
            return ctx.enter_context(nc.sbuf_tensor("c_" + name, shape, dt))

        xnT_hi = buf("xnT_hi", [P, KT, SEQS * PADDED], F32R)
        xnT_lo = buf("xnT_lo", [P, KT, SEQS * PADDED], F32R)
        w_raw = buf("w_raw", [P, KT, 3 * W])
        w_hi = buf("w_hi", [P, TAPS * KT, 3 * W], F32R)
        w_lo = buf("w_lo", [P, TAPS * KT, 3 * W], F32R)
        conv_b = buf("b", [P, 3])
        eps = buf("eps", [P, 1])
        stats = buf("stats", [P, ST, 6])
        mv = buf("mv", [P, ST, 2])
        std = buf("std", [P, ST])
        rstd = buf("rstd", [P, ST])
        xn = buf("xn", [P, 2, DM])

        x_in, w_in, b_in = sem("c_x_in"), sem("c_w_in"), sem("c_b_in")
        eps_set, pads, cell_set = sem("c_eps_set"), sem("c_pads"), sem("c_cell_set")
        cell = buf("cell", [P, 2])
        w_hi_ready, w_lo_ready = sem("c_w_hi_ready"), sem("c_w_lo_ready")
        stats_done, var_ready, std_ready, rstd_ready = (sem("c_" + s) for s in ("stats", "var", "std", "rstd"))
        xn_ready, turned = sem("c_xn_ready"), sem("c_turned")
        hi_ready, lo_ready = sem("c_hi_ready"), sem("c_lo_ready")
        conv_done, conv_out = sem("c_conv_done"), sem("c_conv_out")
        turn_ps = [psum[:, b, :].rearrange("p (k n) -> p k n", k=KT) for b in (0, 1)]
        conv_ps = [psum[:, b, :] for b in (2, 3)]
        UNITS = 3 * LEN // GROUP

        block = ctx.enter_context(nc.Block())

        @block.sync
        def _(sp):
            xv = dram["x"].rearrange("(t p) n -> p t n", p=P)
            for h in range(2):
                sp.dma_start(x_sb[:, 4 * h:4 * h + 4, :], xv[:, 4 * h:4 * h + 4, :]).then_inc(x_in, 16)
            sp.dma_start(ident[:, :], dram["ident"]).then_inc(b_in, 16)
            sp.dma_start(conv_b[:, :], dram["conv_b"]).then_inc(b_in, 16)
            for t in range(TAPS):
                if t:
                    sp.wait_ge(w_lo_ready, t)
                sp.dma_start(w_raw[:, :, :], dram["conv_w"][:, KT * t:KT * (t + 1), :]).then_inc(w_in, 16)
            sp.wait_ge(x_in, 32)
            for h in range(2, 4):
                sp.dma_start(x_sb[:, 4 * h:4 * h + 4, :], xv[:, 4 * h:4 * h + 4, :]).then_inc(x_in, 16)
            for dst, src in prefetch["loads"]:
                sp.dma_start(dst, src).then_inc(prefetch["in"], 16)

        @block.gpsimd
        def _(pool):
            pool.memset(eps[:, :], EPS).then_inc(eps_set, 1)
            for t in (xnT_hi, xnT_lo):
                ends = t[:, :, :].bitcast(F32).rearrange("p k (s n) -> p k s n", s=SEQS)
                for col in (0, PADDED - 1):
                    pool.memset(ends[:, :, :, col:col + 1], 0.0).then_inc(pads, 1)
            for t in range(TAPS):
                s = slice(KT * t, KT * (t + 1))
                pool.wait_ge(w_in, 16 * (t + 1))
                pool.tensor_copy(w_hi[:, s, :], w_raw[:, :, :]).then_inc(w_hi_ready, 1)
                pool.wait_ge(w_hi_ready, t + 1)
                take_lo(pool, w_lo[:, s, :], w_raw[:, :, :], w_hi[:, s, :]).then_inc(w_lo_ready, 1)

        @block.vector
        def _(dve):
            dve.memset(cell[:, :], 0.0).then_inc(cell_set, 1)
            dve.wait_ge(cell_set, 1)
            with dve.Fori(0, SEQS) as n:
                dve.wait_ge(x_in, 32 * n + 32)
                for t in range(ST):
                    dve.bn_stats(stats[:, t, :], x_sb[:, ds(n * ST + t, 1), :]).then_inc(stats_done, 1)
                wait_on_cell(dve, cell, stats_done, n * ST + ST)
                for t in range(ST):
                    dve.bn_aggr(mv[:, t, :], stats[:, t, :]).then_inc(var_ready, 1)
                dve.wait_ge(std_ready, n + 1)
                dve.reciprocal(rstd[:, :], std[:, :]).then_inc(rstd_ready, 1)
                dve.wait_ge(rstd_ready, n + 1)

                def norm(t):
                    if t >= 2:
                        dve.wait_ge(turned, n * ST + t - 1)
                    dve.tensor_scalar(xn[:, t % 2, :], x_sb[:, ds(n * ST + t, 1), :], mv[:, t, 0:1],
                                      rstd[:, t:t + 1], ALU.subtract, ALU.mult).then_inc(xn_ready, 1)

                norm(0)
                for t in range(ST):
                    if t + 1 < ST:
                        norm(t + 1)
                    dve.wait_ge(hi_ready, n * ST + t + 1)
                    at = n * PADDED + 1 + t * P
                    take_lo(dve, xnT_lo[:, :, ds(at, P)], turn_ps[t % 2], xnT_hi[:, :, ds(at, P)]).then_inc(lo_ready, 1)

        @block.scalar
        def _(act):
            act.wait_ge(eps_set, 1)
            act.wait_ge(b_in, 32)
            with act.Fori(0, SEQS) as n:
                act.wait_ge(var_ready, n * ST + ST)
                act.activation(std[:, :], mv[:, :, 1], ACT.Sqrt, bias=eps[:, 0:1]).then_inc(std_ready, 1)
                for t in range(ST):
                    act.wait_ge(turned, n * ST + t + 1)
                    take_hi(act, xnT_hi[:, :, ds(n * PADDED + 1 + t * P, P)], turn_ps[t % 2]).then_inc(hi_ready, 1)
                for c in range(UNITS):
                    o, half = c // 2, c % 2
                    act.wait_ge(conv_done, n * UNITS + c + 1)
                    act.activation(qkvT[:, o, ds(n * LEN + half * GROUP, GROUP)], conv_ps[c % 2], ACT.Identity,
                                   bias=conv_b[:, o:o + 1]).then_inc(conv_out, 1)

        @block.tensor
        def _(pe):
            pe.wait_ge(b_in, 32)
            pe.wait_ge(pads, 4)
            with pe.Fori(0, SEQS) as n:
                for t in range(ST):
                    pe.wait_ge(xn_ready, n * ST + t + 1)
                    if t >= 2:
                        pe.wait_ge(lo_ready, n * ST + t - 1)
                    for k in range(KT):
                        ins = pe.transpose(turn_ps[t % 2][:, k, :], xn[:, t % 2, k * P:(k + 1) * P], ident[:, :])
                    ins.then_inc(turned, 1)
                pe.wait_ge(lo_ready, n * ST + ST)
                for c in range(UNITS):
                    o, half = c // 2, c % 2
                    if c >= 2:
                        pe.wait_ge(conv_out, n * UNITS + c - 1)
                    for tap in range(TAPS):
                        if c == 0:
                            pe.wait_ge(w_lo_ready, tap + 1)
                        for k in range(KT):
                            at = n * PADDED + half * GROUP + tap
                            kk, cols = tap * KT + k, slice(o * W, (o + 1) * W)
                            ins = product3(pe, conv_ps[c % 2], w_hi[:, kk, cols], w_lo[:, kk, cols],
                                           xnT_hi[:, k, ds(at, GROUP)], xnT_lo[:, k, ds(at, GROUP)],
                                           kk == 0, kk == TAPS * KT - 1)
                    ins.then_inc(conv_done, 1)
                pe.wait_ge(conv_out, n * UNITS + UNITS)



def attention_a_stage(nc, psum, sem, x_sb, ident, qkvT, pre, dram):
    with ExitStack() as ctx:
        def buf(name, shape, dt=F32):
            return ctx.enter_context(nc.sbuf_tensor("a_" + name, shape, dt))

        wqk_hi = buf("wqk_hi", [P, 2, HA * EA], F32R)
        wqk_lo = buf("wqk_lo", [P, 2, HA * EA], F32R)
        vo_hi = buf("vo_hi", [P, BLOCK_STEPS, HPS * W], F32R)
        vo_lo = buf("vo_lo", [P, BLOCK_STEPS, HPS * W], F32R)
        obias = buf("obias", [P, 1])
        mask16 = buf("mask16", [P, HPS * P], BF16)
        ident16 = buf("ident16", [P, P], BF16)
        s_hi = buf("split_hi", [P, 3, GROUP], F32R)
        s_lo = buf("split_lo", [P, 3, GROUP], F32R)
        qh = buf("qh", [P, HEAD_TILES, GROUP])
        kh = buf("kh", [P, HEAD_TILES, GROUP])
        vo = buf("vo", [P, 4, HPS * W])
        mx = buf("mx", [P, 2, HPS])
        prob = buf("prob", [P, 4, HPS, P])
        sums = buf("sums", [P, 2, HPS])
        rsum = buf("rsum", [P, 2, HPS])
        probT = buf("probT", [P, 2, HPS * P])
        oT = buf("oT", [P, 2, P])

        names = ("w_hi w_lo vo_made vo_hi vo_lo bias_made bias_ready consts hi lo vhi vlo projected qh kh scored "
                 "max_ready sub_done exp_done sum_ready rsum_ready normed vo_done vo_ready probs_turned probT_ready "
                 "pv_done oT_ready y_done y_added pb_added")
        s = {n: sem("a_" + n) for n in names.split()}

        block = ctx.enter_context(nc.Block())
        score_ps = [psum[:, b, :] for b in (0, 1)]
        proj_ps = [psum[:, b, :] for b in (2, 3)]
        turn_ps = [psum[:, b, :] for b in (4, 5)]
        out_ps = [psum[:, b, :] for b in (6, 7)]
        N_PROJ = 2 * HEAD_TILES
        DRAIN = 4
        proj_at = {STEPS + d: range(d * N_PROJ // DRAIN, (d + 1) * N_PROJ // DRAIN) for d in range(DRAIN)}

        def is_block_end(u):
            return u % BLOCK_STEPS == BLOCK_STEPS - 1

        @block.scalar
        def _(act):
            act.wait_ge(pre["in"], pre["total"])
            act.activation(ident16[:, :], ident[:, :], ACT.Copy).then_inc(s["consts"], 1)
            act.activation(mask16[:, :], pre["mask"][:, :], ACT.Copy).then_inc(s["consts"], 1)
            for w in range(2):
                take_hi(act, wqk_hi[:, w, :], pre["wqk"][:, w, :]).then_inc(s["w_hi"], 1)
            for c in range(BLOCK_STEPS):
                act.wait_ge(s["vo_made"], c + 1)
                take_hi(act, vo_hi[:, c, :], psum[:, c, :]).then_inc(s["vo_hi"], 1)
            act.wait_ge(s["bias_made"], 1)
            act.activation(obias[:, :], psum[:, 4, 0:1], ACT.Identity, bias=pre["bo"][:, 0:1]).then_inc(s["bias_ready"], 1)

            def split(i, o):
                src = qkvT[:, o, ds(i * GROUP, GROUP)]
                take_hi(act, s_hi[:, o, :], src).then_inc(s["vhi"] if o == 2 else s["hi"], 1)

            def q_out(i, n):
                t = n // 2
                act.wait_ge(s["projected"], N_PROJ * i + n + 1)
                act.activation(qh[:, t, :], proj_ps[0], ACT.Identity, bias=pre["bq"][:, t:t + 1]).then_inc(s["qh"], 1)

            def group(i, last):
                for u in range(STEPS + DRAIN):
                    if u < STEPS:
                        act.wait_ge(s["sub_done"], STEPS * i + u + 1)
                        act.activation(prob[:, u % 4, :, :], prob[:, u % 4, :, :], ACT.Exp, scale=SCALE_A).then_inc(s["exp_done"], 1)
                        act.wait_ge(s["vo_done"], STEPS * i + u + 1)
                        if u >= 4:
                            act.wait_ge(s["pv_done"], STEPS * i + u - 3)
                        act.activation(vo[:, u % 4, :], proj_ps[u % 2], ACT.Copy).then_inc(s["vo_ready"], 1)
                    if 2 <= u < STEPS + 2:
                        t = u - 2
                        act.wait_ge(s["probs_turned"], STEPS * i + t + 1)
                        if t >= 2:
                            act.wait_ge(s["pv_done"], STEPS * i + t - 1)
                        act.activation(probT[:, t % 2, :], turn_ps[t % 2], ACT.Copy).then_inc(s["probT_ready"], 1)
                    if u == STEPS - 3 and not last:
                        split(i + 1, 0)
                        split(i + 1, 1)
                    if u == STEPS + 1 and not last:
                        act.wait_ge(s["vo_done"], STEPS * i + STEPS)
                        split(i + 1, 2)
                    if u >= 3 and is_block_end(u - 3):
                        b = (u - 3) // BLOCK_STEPS
                        act.wait_ge(s["pv_done"], STEPS * i + u - 2)
                        if b >= 2:
                            act.wait_ge(s["y_done"], GT * i + b - 1)
                        act.activation(oT[:, b % 2, :], out_ps[b % 2][:, 0:P], ACT.Identity,
                                       bias=obias[:, 0:1]).then_inc(s["oT_ready"], 1)
                    if u in proj_at and not last:
                        for n in proj_at[u]:
                            if n % 2 == 0:
                                q_out(i + 1, n)

            for o in range(3):
                split(0, o)
            for n in range(0, N_PROJ, 2):
                q_out(0, n)
            with act.Fori(0, GROUPS - 1) as i:
                group(i, False)
            group(GROUPS - 1, True)

        @block.vector
        def _(dve):
            dve.wait_ge(pre["in"], pre["total"])
            for w in range(2):
                dve.wait_ge(s["w_hi"], w + 1)
                take_lo(dve, wqk_lo[:, w, :], pre["wqk"][:, w, :], wqk_hi[:, w, :]).then_inc(s["w_lo"], 1)
            for c in range(BLOCK_STEPS):
                dve.wait_ge(s["vo_hi"], c + 1)
                take_lo(dve, vo_lo[:, c, :], psum[:, c, :], vo_hi[:, c, :]).then_inc(s["vo_lo"], 1)

            def split(i, o):
                dve.wait_ge(s["vhi"] if o == 2 else s["hi"], i + 1 if o == 2 else 2 * i + o + 1)
                src = qkvT[:, o, ds(i * GROUP, GROUP)]
                take_lo(dve, s_lo[:, o, :], src, s_hi[:, o, :]).then_inc(s["vlo"] if o == 2 else s["lo"], 1)

            def k_out(i, n):
                t = n // 2
                dve.wait_ge(s["projected"], N_PROJ * i + n + 1)
                dve.tensor_scalar(kh[:, t, :], proj_ps[1], pre["bk"][:, t:t + 1], None, ALU.add).then_inc(s["kh"], 1)

            def group(i, last):
                for u in range(STEPS + DRAIN + 1):
                    if u < STEPS:
                        scores = score_ps[u % 2].rearrange("p (h k) -> p h k", h=HPS)
                        dve.wait_ge(s["scored"], STEPS * i + u + 1)
                        dve.tensor_reduce(mx[:, u % 2, :], scores, AX_X, ALU.max).then_inc(s["max_ready"], 1)
                        if u >= 4:
                            dve.wait_ge(s["probs_turned"], STEPS * i + u - 3)
                        dve.wait_ge(s["max_ready"], STEPS * i + u + 1)
                        dve.tensor_tensor(prob[:, u % 4, :, :], scores, mx[:, u % 2, :].unsqueeze(2).broadcast_to([P, HPS, P]),
                                          ALU.subtract).then_inc(s["sub_done"], 1)
                    if 1 <= u < STEPS + 1:
                        t = u - 1
                        dve.wait_ge(s["exp_done"], STEPS * i + t + 1)
                        dve.tensor_reduce(sums[:, t % 2, :], prob[:, t % 4, :, :], AX_X, ALU.add).then_inc(s["sum_ready"], 1)
                        dve.wait_ge(s["sum_ready"], STEPS * i + t + 1)
                        if t >= 2:
                            dve.wait_ge(s["normed"], STEPS * i + t - 1)
                        dve.reciprocal(rsum[:, t % 2, :], sums[:, t % 2, :]).then_inc(s["rsum_ready"], 1)
                    if u == STEPS - 2 and not last:
                        split(i + 1, 0)
                        split(i + 1, 1)
                    if u == STEPS + 1 and not last:
                        split(i + 1, 2)
                    if u in proj_at and not last:
                        for n in proj_at[u]:
                            if n % 2:
                                k_out(i + 1, n)
                    if u >= 5 and is_block_end(u - 5):
                        b = (u - 5) // BLOCK_STEPS
                        dve.wait_ge(s["y_done"], GT * i + b + 1)
                        if b == 0:
                            dve.wait_ge(s["pb_added"], i + 1)
                        xt = x_sb[:, ds(GT * i + b, 1), :]
                        dve.tensor_tensor(xt, xt, out_ps[b % 2].unsqueeze(1), ALU.add).then_inc(s["y_added"], 1)

            for o in range(3):
                split(0, o)
            for n in range(1, N_PROJ, 2):
                k_out(0, n)
            with dve.Fori(0, GROUPS - 1) as i:
                group(i, False)
            group(GROUPS - 1, True)

        @block.gpsimd
        def _(pool):
            pool.wait_ge(pre["in"], pre["total"])
            with pool.Fori(0, GROUPS) as i:
                xg = x_sb[:, ds(GT * i, GT), :]
                pool.tensor_tensor(xg, xg, pre["proj_b"][:, :].unsqueeze(1).broadcast_to([P, GT, DM]), ALU.add).then_inc(s["pb_added"], 1)
                for u in range(STEPS):
                    pool.wait_ge(s["rsum_ready"], STEPS * i + u + 1)
                    p = prob[:, u % 4, :, :]
                    pool.tensor_tensor(p, p, rsum[:, u % 2, :].unsqueeze(2).broadcast_to([P, HPS, P]), ALU.mult).then_inc(s["normed"], 1)

        @block.tensor
        def _(pe):
            pe.wait_ge(pre["in"], pre["total"])
            for c in range(BLOCK_STEPS):
                for m, h in enumerate(heads_of(c)):
                    rows = slice(EA * (h % 2), EA * (h % 2) + EA)
                    ins = pe.matmul(psum[:, c, m * W:(m + 1) * W], pre["wvT"][rows, h // 2, :], pre["wo"][rows, h // 2, :],
                                    start=True, stop=True)
                ins.then_inc(s["vo_made"], 1)
            for t in range(HEAD_TILES):
                ins = pe.matmul(psum[:, 4, 0:1], pre["wo"][:, t, :], pre["bv"][:, t:t + 1],
                                start=t == 0, stop=t == HEAD_TILES - 1)
            ins.then_inc(s["bias_made"], 1)
            pe.wait_ge(s["vo_lo"], BLOCK_STEPS)
            pe.wait_ge(s["bias_ready"], 1)
            pe.wait_ge(s["w_lo"], 2)
            pe.wait_ge(s["consts"], 2)

            def project(i, n):
                w, t = n % 2, n // 2
                if n < 2:
                    pe.wait_ge(s["lo"], 2 * i + w + 1)
                elif w == 0:
                    pe.wait_ge(s["qh"], HEAD_TILES * i + t)
                else:
                    pe.wait_ge(s["kh"], HEAD_TILES * i + t)
                cols = slice(t * P, (t + 1) * P)
                product3(pe, proj_ps[w], wqk_hi[:, w, cols], wqk_lo[:, w, cols], s_hi[:, w, :], s_lo[:, w, :],
                         True, True).then_inc(s["projected"], 1)

            def group(i, last):
                for u in range(STEPS + DRAIN + 1):
                    if u < STEPS:
                        b, c = u // BLOCK_STEPS, u % BLOCK_STEPS
                        cols = slice(b * P, (b + 1) * P)
                        if u == 0:
                            pe.wait_ge(s["qh"], HEAD_TILES * i + HEAD_TILES)
                            pe.wait_ge(s["kh"], HEAD_TILES * i + HEAD_TILES)
                            pe.wait_ge(s["vlo"], i + 1)
                        else:
                            if u >= 2:
                                pe.wait_ge(s["sub_done"], STEPS * i + u - 1)
                                pe.wait_ge(s["vo_ready"], STEPS * i + u - 1)
                        pe.matmul(score_ps[u % 2], ident16[:, :], mask16[:, :], start=True, stop=False, skip_group_check=True)
                        for m, h in enumerate(heads_of(c)):
                            rows = slice(EA * (h % 2), EA * (h % 2) + EA)
                            ins = pe.matmul(score_ps[u % 2][:, m * P:(m + 1) * P], qh[rows, h // 2, cols], kh[rows, h // 2, cols],
                                            start=False, stop=m == HPS - 1, skip_group_check=True)
                        ins.then_inc(s["scored"], 1)
                        product3(pe, proj_ps[u % 2], s_hi[:, 2, cols], s_lo[:, 2, cols], vo_hi[:, c, :], vo_lo[:, c, :],
                                 True, True).then_inc(s["vo_done"], 1)
                    if 2 <= u < STEPS + 2:
                        t = u - 2
                        pe.wait_ge(s["normed"], STEPS * i + t + 1)
                        if t >= 2:
                            pe.wait_ge(s["probT_ready"], STEPS * i + t - 1)
                        for m in range(HPS):
                            ins = pe.transpose(turn_ps[t % 2][:, m * P:(m + 1) * P], prob[:, t % 4, m, :], ident[:, :])
                        ins.then_inc(s["probs_turned"], 1)
                    if 3 <= u < STEPS + 3:
                        t = u - 3
                        b, c = t // BLOCK_STEPS, t % BLOCK_STEPS
                        pe.wait_ge(s["probT_ready"], STEPS * i + t + 1)
                        pe.wait_ge(s["vo_ready"], STEPS * i + t + 1)
                        if c == 0 and b >= 2:
                            pe.wait_ge(s["y_added"], GT * i + b - 1)
                        for m in range(HPS):
                            ins = pe.matmul(out_ps[b % 2][:, 0:P], vo[:, t % 4, m * W:(m + 1) * W], probT[:, t % 2, m * P:(m + 1) * P],
                                            start=c == 0 and m == 0, stop=c == BLOCK_STEPS - 1 and m == HPS - 1)
                        ins.then_inc(s["pv_done"], 1)
                    if u in proj_at and not last:
                        if u == STEPS:
                            pe.wait_ge(s["vo_ready"], STEPS * i + STEPS)
                        for n in proj_at[u]:
                            project(i + 1, n)
                    if u >= 4 and is_block_end(u - 4):
                        b = (u - 4) // BLOCK_STEPS
                        pe.wait_ge(s["oT_ready"], GT * i + b + 1)
                        pe.matmul(out_ps[b % 2], oT[:, b % 2, :], pre["proj_w"][:, :], start=True, stop=True).then_inc(s["y_done"], 1)
                pe.wait_ge(s["y_added"], GT * i + GT)

            for n in range(N_PROJ):
                project(0, n)
            with pe.Fori(0, GROUPS - 1) as i:
                group(i, False)
            group(GROUPS - 1, True)



FFN_SEMS = ("c_in cell consts eps stats var std rstd xn turned hi lo logits routed routed2 shifted exped rstep w wT_turned wT "
            "g_done u_done w_done silu up hid h_hi h_lo d_done y_added out w_hi w_lo chunk_in0 chunk_in1").split()


def ffn_stage(nc, psum, s, x_sb, ident, dram, run, out):
    tag = f"f{run}_"
    FIRST, LAST = GROUPS * run, GROUPS * run + GROUPS - 1
    CHUNKS_BEFORE = FFN_CHUNKS * run

    def tile(i, t):
        return ds(GT * (i - FIRST) + t, 1)

    with ExitStack() as ctx:
        def buf(name, shape, dt=F32):
            return ctx.enter_context(nc.sbuf_tensor(tag + name, shape, dt))

        w_raw = buf("w_raw", [P, 2, FF])
        w_hi = buf("w_hi", [P, FFN_CHUNKS, FF], F32R)
        w_lo = buf("w_lo", [P, FFN_CHUNKS, FF], F32R)
        r_raw = buf("r_raw", [P, KT, EXPERTS])
        r_hi = buf("r_hi", [P, KT, EXPERTS], F32R)
        r_lo = buf("r_lo", [P, KT, EXPERTS], F32R)
        spread_raw = buf("spread_raw", [2 * EXPERTS, FF])
        spread = buf("spread", [2 * EXPERTS, FF], F32R)
        rank = buf("rank", [P, EXPERTS])
        cell = buf("cell", [P, 2])
        eps = buf("eps", [P, 1])
        stats = buf("stats", [P, GT, 6])
        mv = buf("mv", [P, GT, 2])
        std = buf("std", [P, GT])
        rstd = buf("rstd", [P, GT])
        xn = buf("xn", [P, GT, DM])
        xT_hi = buf("xT_hi", [P, KT, GROUP], F32R)
        xT_lo = buf("xT_lo", [P, KT, GROUP], F32R)
        row = buf("row", [P, 3, GT])
        lg = buf("lg", [P, 6, GT, EXPERTS])
        wsplit = buf("wsplit", [P, GT, 2 * EXPERTS])
        wT = buf("wT", [2 * EXPERTS, GROUP], F32R)
        silu = buf("silu", [P, 2, GROUP])
        up = buf("up", [P, 2, GROUP])
        hid = buf("hid", [P, 2, GROUP])
        hT_hi = buf("hT_hi", [P, 3, GROUP], F32R)
        hT_lo = buf("hT_lo", [P, 3, GROUP], F32R)

        chunk_in = [s["chunk_in0"], s["chunk_in1"]]
        y_ps = [psum[:, b, :] for b in range(GT)]
        g_ps, u_ps, w_ps, m_ps = (psum[:, GT + b, :] for b in range(4))
        turn_ps = [m_ps, w_ps]
        d_hi = w_hi[:, D_AT:, :].rearrange("p a b -> p (a b)")
        d_lo = w_lo[:, D_AT:, :].rearrange("p a b -> p (a b)")

        block = ctx.enter_context(nc.Block())

        @block.sync
        def _(sp):
            for dst, src in ((r_raw, "gate_w"), (spread_raw, "spread"), (rank, "rank")):
                sp.dma_start(dst[:], dram[src]).then_inc(s["c_in"], 16)
            for c in range(FFN_CHUNKS):
                if c >= 2:
                    sp.wait_ge(s["w_lo"], CHUNKS_BEFORE + c - 1)
                sp.dma_start(w_raw[:, c % 2, :], dram["ffn_w"][:, c, :]).then_inc(chunk_in[c % 2], 16)
            if out is not None:
                with sp.Fori(FIRST, LAST + 1) as i:
                    sp.wait_ge(s["y_added"], GT * i + GT)
                    group = ds(GT * (i - FIRST), GT)
                    sp.dma_start(out.rearrange("(t p) n -> p t n", p=P)[:, group, :], x_sb[:, group, :]).then_inc(s["out"], 16)
                sp.wait_ge(s["out"], 16 * GROUPS)

        @block.gpsimd
        def _(pool):
            pool.memset(eps[:, :], EPS).then_inc(s["eps"], 1)
            for c in range(FFN_CHUNKS):
                pool.wait_ge(s["w_hi"], CHUNKS_BEFORE + c + 1)
                take_lo(pool, w_lo[:, c, :], w_raw[:, c % 2, :], w_hi[:, c, :]).then_inc(s["w_lo"], 1)
            with pool.Fori(FIRST, LAST + 1) as i:
                for j in range(FT):
                    pool.wait_ge(s["h_hi"], FT * i + j + 1)
                    take_lo(pool, hT_lo[:, j % 3, :], hid[:, j % 2, :], hT_hi[:, j % 3, :]).then_inc(s["h_lo"], 1)

        @block.scalar
        def _(act):
            act.wait_ge(s["c_in"], 48 * (run + 1))
            act.wait_ge(s["eps"], run + 1)
            take_hi(act, r_hi[:, :, :], r_raw[:, :, :]).then_inc(s["consts"], 1)
            act.activation(spread[:, :], spread_raw[:, :], ACT.Copy).then_inc(s["consts"], 1)

            def root(i):
                act.wait_ge(s["var"], GT * i + GT)
                act.activation(std[:, :], mv[:, :, 1], ACT.Sqrt, bias=eps[:, 0:1]).then_inc(s["std"], 1)

            def turn(i, t):
                act.wait_ge(s["turned"], GT * i + t + 1)
                take_hi(act, xT_hi[:, :, t * P:(t + 1) * P],
                        turn_ps[t % 2].rearrange("p (k n) -> p k n", k=KT)).then_inc(s["hi"], 1)

            def route(i):
                act.wait_ge(s["shifted"], i + 1)
                act.activation(lg[:, 1, :, :], lg[:, 0, :, :], ACT.Exp).then_inc(s["exped"], 1)

            def gate(i, j):
                act.wait_ge(s["g_done"], FT * i + j + 1)
                if j >= 2:
                    act.wait_ge(s["up"], FT * i + j - 1)
                act.activation(silu[:, j % 2, :], g_ps, ACT.Silu).then_inc(s["silu"], 1)

            def high(i, j):
                act.wait_ge(s["hid"], FT * i + j + 1)
                if j >= 3:
                    act.wait_ge(s["d_done"], FT * i + j - 2)
                take_hi(act, hT_hi[:, j % 3, :], hid[:, j % 2, :]).then_inc(s["h_hi"], 1)

            def main(i, last):
                for j in range(FT + 1):
                    if j < FT:
                        gate(i, j)
                    if j == 1:
                        act.wait_ge(s["wT_turned"], i + 1)
                        act.activation(wT[:, :], m_ps[0:2 * EXPERTS, :], ACT.Copy).then_inc(s["wT"], 1)
                    if j >= 1:
                        high(i, j - 1)
                    if j == 3 and not last:
                        root(i + 1)
                if not last:
                    for t in range(GT):
                        turn(i + 1, t)
                    route(i + 1)

            root(FIRST)
            for c in range(FFN_CHUNKS):
                act.wait_ge(chunk_in[c % 2], 16 * ((CHUNKS_BEFORE + c) // 2 + 1))
                take_hi(act, w_hi[:, c, :], w_raw[:, c % 2, :]).then_inc(s["w_hi"], 1)
                if c == 3:
                    for t in range(GT):
                        turn(FIRST, t)
                    route(FIRST)
            with act.Fori(FIRST, LAST) as i:
                main(i, False)
            main(LAST, True)

        @block.vector
        def _(dve):
            dve.memset(cell[:, :], 0.0).then_inc(s["cell"], 1)
            dve.wait_ge(s["cell"], run + 1)
            dve.wait_ge(s["c_in"], 48 * (run + 1))
            dve.wait_ge(s["consts"], 3 * run + 1)
            take_lo(dve, r_lo[:, :, :], r_raw[:, :, :], r_hi[:, :, :]).then_inc(s["consts"], 1)

            def stats_of(i):
                for t in range(GT):
                    dve.bn_stats(stats[:, t, :], x_sb[:, tile(i, t), :]).then_inc(s["stats"], 1)
                wait_on_cell(dve, cell, s["stats"], GT * i + GT)
                for t in range(GT):
                    dve.bn_aggr(mv[:, t, :], stats[:, t, :]).then_inc(s["var"], 1)

            def norm(i):
                dve.wait_ge(s["std"], i + 1)
                dve.reciprocal(rstd[:, :], std[:, :]).then_inc(s["rstd"], 1)
                dve.wait_ge(s["rstd"], i + 1)
                for t in range(GT):
                    dve.tensor_scalar(xn[:, t, :], x_sb[:, tile(i, t), :], mv[:, t, 0:1], rstd[:, t:t + 1],
                                      ALU.subtract, ALU.mult).then_inc(s["xn"], 1)

            def low(i, t):
                dve.wait_ge(s["hi"], GT * i + t + 1)
                cols = slice(t * P, (t + 1) * P)
                take_lo(dve, xT_lo[:, :, cols], turn_ps[t % 2].rearrange("p (k n) -> p k n", k=KT),
                        xT_hi[:, :, cols]).then_inc(s["lo"], 1)

            R_STEPS = 16

            def route(i):
                at = [0]

                def done(ins):
                    at[0] += 1
                    ins.then_inc(s["rstep"], 1)
                    dve.wait_ge(s["rstep"], R_STEPS * i + at[0])

                def wide(r):
                    return r.unsqueeze(2).broadcast_to([P, GT, EXPERTS])

                ranks = rank[:, :].unsqueeze(1).broadcast_to([P, GT, EXPERTS])
                logits = m_ps[:, 0:GT * EXPERTS].rearrange("p (t e) -> p t e", t=GT)
                a, e, c, one1, one2, left = (lg[:, k, :, :] for k in range(6))
                m, first, second = (row[:, k, :] for k in range(3))
                dve.wait_ge(s["logits"], i + 1)
                done(dve.tensor_reduce(m, logits, AX_X, ALU.max))
                dve.tensor_tensor(a, logits, wide(m), ALU.subtract).then_inc(s["shifted"], 1)
                dve.wait_ge(s["exped"], i + 1)
                done(dve.tensor_reduce(m, e, AX_X, ALU.add))
                done(dve.reciprocal(m, m))
                done(dve.tensor_tensor(a, e, wide(m), ALU.mult))
                for held, one, best in ((a, one1, first), (left, one2, second)):
                    done(dve.tensor_reduce(best, held, AX_X, ALU.max))
                    done(dve.tensor_tensor(c, held, wide(best), ALU.is_equal))
                    done(dve.tensor_tensor(c, c, ranks, ALU.mult))
                    done(dve.tensor_reduce(m, c, AX_X, ALU.max))
                    dve.tensor_tensor(one, ranks, wide(m), ALU.is_equal).then_inc(s["routed"], 1)
                    if one is one1:
                        dve.wait_ge(s["routed"], 2 * i + 1)
                        done(dve.scalar_tensor_tensor(left, one1, -2.0, a, ALU.mult, ALU.add))
                done(dve.tensor_tensor(first, first, second, ALU.add))
                done(dve.reciprocal(first, first))
                dve.wait_ge(s["routed"], 2 * i + 2)
                done(dve.tensor_tensor(one1, one1, one2, ALU.add))
                assert at[0] == R_STEPS
                dve.tensor_tensor(a, a, one1, ALU.mult).then_inc(s["routed2"], 1)
                dve.wait_ge(s["routed2"], 3 * i + 1)
                dve.tensor_tensor(a, a, wide(first), ALU.mult).then_inc(s["routed2"], 1)
                dve.wait_ge(s["routed2"], 3 * i + 2)
                dve.tensor_copy(wsplit[:, :, 0:EXPERTS].bitcast(F32R), a).then_inc(s["routed2"], 1)
                dve.wait_ge(s["routed2"], 3 * i + 3)
                dve.tensor_tensor(wsplit[:, :, EXPERTS:], a, wsplit[:, :, 0:EXPERTS], ALU.subtract).then_inc(s["w"], 1)

            def main(i, last):
                for j in range(FT):
                    dve.wait_ge(s["silu"], FT * i + j + 1)
                    dve.wait_ge(s["u_done"], FT * i + j + 1)
                    dve.tensor_tensor(up[:, j % 2, :], silu[:, j % 2, :], u_ps, ALU.mult).then_inc(s["up"], 1)
                    dve.wait_ge(s["w_done"], FT * i + j + 1)
                    if j >= 2:
                        dve.wait_ge(s["h_lo"], FT * i + j - 1)
                    dve.wait_ge(s["up"], FT * i + j + 1)
                    dve.tensor_tensor(hid[:, j % 2, :], up[:, j % 2, :], w_ps, ALU.mult).then_inc(s["hid"], 1)
                    if not last:
                        if j == 1:
                            stats_of(i + 1)
                        if j == 4:
                            norm(i + 1)
                if not last:
                    for t in range(GT):
                        low(i + 1, t)
                    route(i + 1)
                dve.wait_ge(s["d_done"], FT * i + FT)
                for t in range(GT):
                    xt = x_sb[:, tile(i, t), :]
                    dve.tensor_tensor(xt, xt, y_ps[t].unsqueeze(1), ALU.add).then_inc(s["y_added"], 1)

            stats_of(FIRST)
            norm(FIRST)
            for t in range(GT):
                low(FIRST, t)
            route(FIRST)
            with dve.Fori(FIRST, LAST) as i:
                main(i, False)
            main(LAST, True)

        @block.tensor
        def _(pe):
            def turn(i, t, first=False):
                pe.wait_ge(s["xn"], GT * i + t + 1)
                if t == 0 and not first:
                    pe.wait_ge(s["hid"], FT * i)
                if t >= 2:
                    pe.wait_ge(s["lo"], GT * i + t - 1)
                for k in range(KT):
                    ins = pe.transpose(turn_ps[t % 2][:, k * P:(k + 1) * P], xn[:, t, k * P:(k + 1) * P], ident[:, :])
                ins.then_inc(s["turned"], 1)

            def logits(i):
                pe.wait_ge(s["lo"], GT * i + GT)
                for t in range(GT):
                    for k in range(KT):
                        ins = product3(pe, m_ps[:, t * EXPERTS:(t + 1) * EXPERTS], xT_hi[:, k, t * P:(t + 1) * P],
                                       xT_lo[:, k, t * P:(t + 1) * P], r_hi[:, k, :], r_lo[:, k, :], k == 0, k == KT - 1)
                ins.then_inc(s["logits"], 1)

            def hidden(out, at, j, name):
                for k in range(KT):
                    cols = slice(j * P, (j + 1) * P)
                    ins = product3(pe, out, w_hi[:, at + k, cols], w_lo[:, at + k, cols], xT_hi[:, k, :], xT_lo[:, k, :],
                                   k == 0, k == KT - 1)
                ins.then_inc(s[name], 1)

            def down(i, j):
                pe.wait_ge(s["h_lo"], FT * i + j + 1)
                rows = slice(j * DM, (j + 1) * DM)
                for t in range(GT):
                    cols = slice(t * P, (t + 1) * P)
                    ins = product3(pe, y_ps[t], hT_hi[:, j % 3, cols], hT_lo[:, j % 3, cols], d_hi[:, rows], d_lo[:, rows],
                                   j == 0, j == FT - 1)
                ins.then_inc(s["d_done"], 1)

            def main(i, last, first=False):
                for j in range(FT):
                    if j:
                        pe.wait_ge(s["silu"], FT * i + j)
                    if first and j == 0:
                        pe.wait_ge(s["w_lo"], CHUNKS_BEFORE + KT)
                    hidden(g_ps, G_AT, j, "g_done")
                    if j == 1:
                        expert_weights(i)
                    if j:
                        pe.wait_ge(s["up"], FT * i + j)
                    if first and j == 0:
                        pe.wait_ge(s["w_lo"], CHUNKS_BEFORE + 2 * KT)
                    hidden(u_ps, U_AT, j, "u_done")
                    if j == 1:
                        pe.wait_ge(s["wT"], i + 1)
                        spread_weights(0)
                    if j >= 1:
                        pe.wait_ge(s["hid"], FT * i + j)
                        spread_weights(j)
                    if first and j == 2:
                        pe.wait_ge(s["w_lo"], CHUNKS_BEFORE + 3 * KT)
                    if j >= 2:
                        down(i, j - 2)
                if last:
                    down(i, FT - 2)
                    down(i, FT - 1)
                else:
                    turn(i + 1, 0)
                    turn(i + 1, 1)
                    down(i, FT - 2)
                    turn(i + 1, 2)
                    turn(i + 1, 3)
                    down(i, FT - 1)
                    logits(i + 1)

            def expert_weights(i):
                pe.wait_ge(s["w"], i + 1)
                for t in range(GT):
                    ins = pe.transpose(m_ps[0:2 * EXPERTS, t * P:(t + 1) * P], wsplit[:, t, :], ident[:, :])
                ins.then_inc(s["wT_turned"], 1)

            def spread_weights(j):
                pe.matmul(w_ps, spread[:, j * P:(j + 1) * P], wT[:, :], start=True, stop=True).then_inc(s["w_done"], 1)

            pe.wait_ge(s["consts"], 3 * run + 3)
            for t in range(GT):
                turn(FIRST, t, True)
            logits(FIRST)
            with pe.Fori(FIRST, LAST) as i:
                main(i, False, True)
            main(LAST, True)



def attention_b_stage(nc, psum, sem, x_sb, ident, dram):
    with ExitStack() as ctx:
        xT_hi = ctx.enter_context(nc.sbuf_tensor("b_xT_hi", [P, KT, LEN], F32R))
        xT_lo = ctx.enter_context(nc.sbuf_tensor("b_xT_lo", [P, KT, LEN], F32R))
        dT_hi = ctx.enter_context(nc.sbuf_tensor("b_dT_hi", [P, KT, LEN], F32R))
        dT_lo = ctx.enter_context(nc.sbuf_tensor("b_dT_lo", [P, KT, LEN], F32R))
        direct_part(nc, psum, sem, x_sb, ident, xT_hi, xT_lo, dT_hi, dT_lo, dram)
        head_part(nc, psum, sem, x_sb, xT_hi, xT_lo, dT_hi, dT_lo, dram)


def direct_part(nc, psum, sem, x_sb, ident, xT_hi, xT_lo, dT_hi, dT_lo, dram):
    with ExitStack() as ctx:
        def buf(name, shape, dt=F32):
            return ctx.enter_context(nc.sbuf_tensor("m_" + name, shape, dt))

        wv = buf("wv", [P, 2, DM])
        wp = buf("wp", [P, 2, QPG, DM])
        wsum = buf("wsum", [P, 2, DM])
        cell = buf("cell", [P, 2])
        zero16 = buf("zero16", [P, DM], BF16)
        M_hi = buf("M_hi", [P, KT, DM], F32R)
        M_lo = buf("M_lo", [P, KT, DM], F32R)
        eps = buf("eps", [P, 1])
        stats = buf("stats", [P, TILES, 6])
        mv = buf("mv", [P, TILES, 2])
        std = buf("std", [P, TILES])
        rstd = buf("rstd", [P, TILES])
        xn = buf("xn", [P, 2, 3, DM])
        t_hi = buf("t_hi", [P, 2, 2, KT, P], F32R)
        t_lo = buf("t_lo", [P, 2, 2, KT, P], F32R)
        names = ("set wsum1 wsum M_done M_made M_hi M_lo stats var std rstd xn dx turned hi lo copied y_done y_added")
        s = {n: sem("m_" + n) for n in names.split()}
        w_in = [sem(f"m_w_in{k}") for k in range(2)]
        PAIRS = LEN // P
        XN0, XN1, DX = range(3)
        turn_ps = [psum[:, b, :].rearrange("p (k n) -> p k n", k=KT) for b in range(3)]

        block = ctx.enter_context(nc.Block())

        @block.sync
        def _(sp):
            def load(g, k):
                sp.dma_start(wv[:, k, :], dram["wv"][:, ds(g, 1), :]).then_inc(w_in[k], 16)
                sp.dma_start(wp[:, k, :, :], dram["wpT"][ds(g, 1), :, :, :].rearrange("a p q n -> (a p) q n")).then_inc(w_in[k], 16)

            for k in range(2):
                load(k, k)
            with sp.Fori(1, KVB // 2) as j:
                for k in range(2):
                    sp.wait_ge(s["M_done"], 2 * j + k - 1)
                    load(2 * j + k, k)

        @block.gpsimd
        def _(pool):
            pool.memset(eps[:, :], EPS).then_inc(s["set"], 1)
            pool.memset(zero16[:, :], 0.0).then_inc(s["set"], 1)
            pool.memset(cell[:, :], 0.0).then_inc(s["set"], 1)
            pool.wait_ge(s["set"], 3)
            with pool.Fori(0, KVB // 2) as j:
                for k in range(2):
                    pool.wait_ge(w_in[k], 32 * j + 32)
                    pool.tensor_tensor(wp[:, k, 0:2, :], wp[:, k, 0:2, :], wp[:, k, 2:4, :], ALU.add).then_inc(s["wsum1"], 1)
                    pool.wait_ge(s["wsum1"], 2 * j + k + 1)
                    pool.tensor_tensor(wsum[:, k, :], wp[:, k, 0, :], wp[:, k, 1, :], ALU.add).then_inc(s["wsum"], 1)

            def diff(t, k):
                pool.wait_ge(s["xn"], 2 * t + 2)
                pool.tensor_tensor(xn[:, k, DX, :], xn[:, k, XN0, :], xn[:, k, XN1, :], ALU.subtract).then_inc(s["dx"], 1)

            def copies(t, k):
                pool.wait_ge(s["lo"], 3 * t + 3)
                zero = cell[:, 0:1].unsqueeze(2).broadcast_to([P, KT, P])
                pool_copy(pool, xT_hi[:, :, ds(t * P, P)], t_hi[:, k, 1, :, :].bitcast(F32), zero).then_inc(s["copied"], 1)
                pool_copy(pool, xT_lo[:, :, ds(t * P, P)], t_lo[:, k, 1, :, :].bitcast(F32), zero).then_inc(s["copied"], 1)

            diff(0, 0)
            diff(1, 1)
            copies(0, 0)

            def unit(t, k, n_diff, n_copy):
                if n_diff:
                    diff(t + 2, k)
                if n_copy:
                    copies(t + 1, 1 - k)

            with pool.Fori(0, PAIRS // 2 - 1) as j:
                unit(2 * j, 0, True, True)
                unit(2 * j + 1, 1, True, True)
            unit(PAIRS - 2, 0, False, True)

        @block.scalar
        def _(act):
            act.wait_ge(s["set"], 3)
            act.wait_ge(s["var"], TILES)
            act.activation(std[:, :], mv[:, :, 1], ACT.Sqrt, bias=eps[:, 0:1]).then_inc(s["std"], 1)

            def high(t, k):
                for a in range(3):
                    act.wait_ge(s["turned"], 3 * t + a + 1)
                    if a == 2:
                        take_hi(act, dT_hi[:, :, ds(t * P, P)], turn_ps[a]).then_inc(s["hi"], 1)
                    else:
                        take_hi(act, t_hi[:, k, a, :, :], turn_ps[a]).then_inc(s["hi"], 1)

            high(0, 0)
            act.wait_ge(s["M_made"], 1)
            for c in range(KT):
                take_hi(act, M_hi[:, c, :], psum[:, 4 + c, :]).then_inc(s["M_hi"], 1)
            with act.Fori(0, PAIRS // 2 - 1) as j:
                high(2 * j + 1, 1)
                act.wait_ge(s["copied"], 4 * j + 2)
                high(2 * j + 2, 0)
                act.wait_ge(s["copied"], 4 * j + 4)
            high(PAIRS - 1, 1)

        @block.vector
        def _(dve):
            for t in range(TILES):
                dve.bn_stats(stats[:, t, :], x_sb[:, t, :]).then_inc(s["stats"], 1)
            dve.wait_ge(s["stats"], TILES)
            for t in range(TILES):
                dve.bn_aggr(mv[:, t, :], stats[:, t, :]).then_inc(s["var"], 1)
            dve.wait_ge(s["std"], 1)
            dve.reciprocal(rstd[:, :], std[:, :]).then_inc(s["rstd"], 1)
            dve.wait_ge(s["rstd"], 1)

            def norm(t, k, first=False):
                if not first:
                    dve.wait_ge(s["turned"], 3 * t - 3)
                for a in range(2):
                    at = t + PAIRS * a
                    dve.tensor_scalar(xn[:, k, a, :], x_sb[:, ds(at, 1), :], mv[:, ds(at, 1), 0:1].squeeze(1),
                                      rstd[:, ds(at, 1)], ALU.subtract, ALU.mult).then_inc(s["xn"], 1)

            def low(t, k):
                for a in range(3):
                    dve.wait_ge(s["hi"], 3 * t + a + 1)
                    if a == 2:
                        cols = ds(t * P, P)
                        take_lo(dve, dT_lo[:, :, cols], turn_ps[a], dT_hi[:, :, cols]).then_inc(s["lo"], 1)
                    else:
                        take_lo(dve, t_lo[:, k, a, :, :], turn_ps[a], t_hi[:, k, a, :, :]).then_inc(s["lo"], 1)

            norm(0, 0, True)
            norm(1, 1, True)
            low(0, 0)
            for c in range(KT):
                dve.wait_ge(s["M_hi"], c + 1)
                take_lo(dve, M_lo[:, c, :], psum[:, 4 + c, :], M_hi[:, c, :]).then_inc(s["M_lo"], 1)

            def unit(t, k, n_norm, n_low):
                if n_norm:
                    norm(t + 2, k)
                if n_low:
                    low(t + 1, 1 - k)
                for a in range(2):
                    dve.wait_ge(s["y_done"], 2 * t + a + 1)
                    xt = x_sb[:, ds(t + PAIRS * a, 1), :]
                    dve.tensor_tensor(xt, xt, psum[:, 4 + 2 * k + a, :].unsqueeze(1), ALU.add).then_inc(s["y_added"], 1)

            with dve.Fori(0, PAIRS // 2 - 1) as j:
                unit(2 * j, 0, True, True)
                unit(2 * j + 1, 1, True, True)
            unit(PAIRS - 2, 0, False, True)
            unit(PAIRS - 1, 1, False, False)

        @block.tensor
        def _(pe):
            pe.wait_ge(s["set"], 3)
            for c in range(KT):
                pe.matmul(psum[:, 4 + c, :], zero16[:, 0:P], zero16[:, :], start=True, stop=False, skip_group_check=True)
            with pe.Fori(0, KVB // 2) as j:
                for k in range(2):
                    pe.wait_ge(s["wsum"], 2 * j + k + 1)
                    for c in range(KT):
                        ins = pe.matmul(psum[:, 4 + c, :], wv[:, k, c * P:(c + 1) * P], wsum[:, k, :],
                                        start=False, stop=False, skip_group_check=True)
                    ins.then_inc(s["M_done"], 1)
            for c in range(KT):
                ins = pe.matmul(psum[:, 4 + c, :], zero16[:, 0:P], zero16[:, :], start=False, stop=True, skip_group_check=True)
            ins.then_inc(s["M_made"], 1)

            def turn(t, k, first=False):
                for a in range(3):
                    if a == 2:
                        pe.wait_ge(s["dx"], t + 1)
                    else:
                        pe.wait_ge(s["xn"], 2 * t + a + 1)
                    if not first:
                        pe.wait_ge(s["lo"], 3 * t - 2 + a)
                    for c in range(KT):
                        ins = pe.transpose(turn_ps[a][:, c, :], xn[:, k, a, c * P:(c + 1) * P], ident[:, :])
                    ins.then_inc(s["turned"], 1)

            def unit(t, k, n_turn):
                if n_turn:
                    turn(t + 1, 1 - k)
                pe.wait_ge(s["lo"], 3 * t + 3)
                for a in range(2):
                    for c in range(KT):
                        ins = product3(pe, psum[:, 4 + 2 * k + a, :], t_hi[:, k, a, c, :], t_lo[:, k, a, c, :],
                                       M_hi[:, c, :], M_lo[:, c, :], c == 0, c == KT - 1)
                    ins.then_inc(s["y_done"], 1)

            turn(0, 0, True)
            pe.wait_ge(s["M_lo"], KT)
            with pe.Fori(0, PAIRS // 2 - 1) as j:
                unit(2 * j, 0, True)
                unit(2 * j + 1, 1, True)
                pe.wait_ge(s["y_added"], 4 * j + 4)
            unit(PAIRS - 2, 0, True)
            unit(PAIRS - 1, 1, False)


def head_part(nc, psum, sem, x_sb, xT_hi, xT_lo, dT_hi, dT_lo, dram):
    with ExitStack() as ctx:
        def buf(name, shape, dt=F32):
            return ctx.enter_context(nc.sbuf_tensor("h_" + name, shape, dt))

        PIECES = 2 + 2 * QPG
        RING = PIECES // 2
        K_AT, V_AT, Q_AT, O_AT = 0, 1, 2, 2 + QPG
        CHUNKS = LEN // GROUP
        UNITS = CHUNKS * QPG
        raw = buf("raw", [P, RING, DM])
        w_hi = buf("w_hi", [P, PIECES, DM], F32R)
        w_lo = buf("w_lo", [P, PIECES, DM], F32R)
        ones = buf("ones", [P, P], F32R)
        ones_f = buf("ones_f", [P, P])
        cell = buf("cell", [P, 2])
        dk = buf("dk", [P, CHUNKS, GROUP])
        dv = buf("dv", [P, CHUNKS, GROUP])
        prod = buf("prod", [P, GROUP])
        prod_hi = buf("prod_hi", [P, 2, GROUP], F32R)
        prod_lo = buf("prod_lo", [P, 2, GROUP], F32R)
        prob = buf("prob", [P, GROUP])
        pv = buf("pv", [P, GROUP])
        pv_hi = buf("pv_hi", [P, QPG, GROUP], F32R)
        pv_lo = buf("pv_lo", [P, QPG, GROUP], F32R)
        names = "set ones w_hi w_lo dk_done dk dv_done dv q_done prod prod_hi prod_lo summed prob pv pv_hi pv_lo y_done y_added"
        s = {n: sem("h_" + n) for n in names.split()}
        piece_in = [sem(f"h_piece_in{k}") for k in range(RING)]

        block = ctx.enter_context(nc.Block())

        @block.sync
        def _(sp):
            def load(g, first):
                for p in range(PIECES):
                    if not (first and p < RING):
                        sp.wait_ge(s["w_lo"], PIECES * g + p - RING + 1)
                    sp.dma_start(raw[:, p % RING, :], dram["wB"][ds(g * PIECES + p, 1), :, :].rearrange("a p n -> (a p) n"))\
                      .then_inc(piece_in[p % RING], 16)

            load(0, True)
            with sp.Fori(1, KVB) as g:
                load(g, False)

        @block.gpsimd
        def _(pool):
            pool.memset(ones_f[:, :], 1.0).then_inc(s["set"], 1)
            pool.memset(cell[:, :], 0.0).then_inc(s["set"], 1)
            pool.wait_ge(s["set"], 2)

            def split(g, first):
                for p in range(PIECES):
                    if not first:
                        if p == K_AT:
                            pool.wait_ge(s["dk_done"], CHUNKS * g)
                        elif p == V_AT:
                            pool.wait_ge(s["dv_done"], CHUNKS * g)
                        elif p < O_AT:
                            pool.wait_ge(s["q_done"], UNITS * g - QPG + (p - Q_AT) + 1)
                        else:
                            pool.wait_ge(s["y_done"], UNITS * g)
                    pool.wait_ge(piece_in[p % RING], 16 * (2 * g + p // RING + 1))
                    pool_copy(pool, w_hi[:, p, :], raw[:, p % RING, :], cell[:, 0:1].broadcast_to([P, DM])).then_inc(s["w_hi"], 1)
                    pool.wait_ge(s["w_hi"], PIECES * g + p + 1)
                    take_lo(pool, w_lo[:, p, :], raw[:, p % RING, :], w_hi[:, p, :]).then_inc(s["w_lo"], 1)

            split(0, True)
            with pool.Fori(1, KVB) as g:
                split(g, False)

        @block.scalar
        def _(act):
            act.wait_ge(s["set"], 2)
            act.activation(ones[:, :], ones_f[:, :], ACT.Copy).then_inc(s["ones"], 1)

            def prob_of(u, k, r):
                act.wait_ge(s["summed"], u + 1)
                act.activation(prob[:, :], psum[:, 4 + k, :], ACT.Sigmoid, scale=SCALE_B).then_inc(s["prob"], 1)
                act.wait_ge(s["pv"], u + 1)
                take_hi(act, pv_hi[:, r, :], pv[:, :]).then_inc(s["pv_hi"], 1)

            def prod_of(u, k):
                act.wait_ge(s["prod"], u + 1)
                take_hi(act, prod_hi[:, k, :], prod[:, :]).then_inc(s["prod_hi"], 1)

            def group(g, first):
                for c in range(CHUNKS):
                    for r in range(QPG):
                        u = UNITS * g + QPG * c + r
                        prev = not (first and c == 0 and r == 0)
                        if r == 0:
                            act.wait_ge(s["dk_done"], CHUNKS * g + c + 1)
                            act.activation(dk[:, c, :], psum[:, 0, :], ACT.Copy).then_inc(s["dk"], 1)
                            if prev:
                                prob_of(u - 1, 1, QPG - 1)
                            act.wait_ge(s["dv_done"], CHUNKS * g + c + 1)
                            act.activation(dv[:, c, :], psum[:, 1, :], ACT.Copy).then_inc(s["dv"], 1)
                            prod_of(u, 0)
                        else:
                            prod_of(u, r % 2)
                            prob_of(u - 1, (r - 1) % 2, r - 1)

            group(0, True)
            with act.Fori(1, KVB) as g:
                group(g, False)
            prob_of(UNITS * KVB - 1, 1, QPG - 1)

        @block.vector
        def _(dve):
            def pv_of(u, c, k, r, begin=False):
                if not begin:
                    dve.wait_ge(s["pv_lo"], u)
                dve.wait_ge(s["prob"], u + 1)
                dve.tensor_tensor(pv[:, :], prob[:, :], dv[:, c, :], ALU.mult).then_inc(s["pv"], 1)
                dve.wait_ge(s["pv_hi"], u + 1)
                take_lo(dve, pv_lo[:, r, :], pv[:, :], pv_hi[:, r, :]).then_inc(s["pv_lo"], 1)

            def prod_of(u, c, k, begin=False):
                if not begin:
                    dve.wait_ge(s["prod_lo"], u)
                dve.wait_ge(s["q_done"], u + 1)
                dve.tensor_tensor(prod[:, :], psum[:, 2 + k, :], dk[:, c, :], ALU.mult).then_inc(s["prod"], 1)
                dve.wait_ge(s["prod_hi"], u + 1)
                take_lo(dve, prod_lo[:, k, :], prod[:, :], prod_hi[:, k, :]).then_inc(s["prod_lo"], 1)

            def add(chunk, c):
                for t in range(GT):
                    dve.wait_ge(s["y_done"], GT * chunk + t + 1)
                    xt = x_sb[:, ST + GT * c + t, :]
                    dve.tensor_tensor(xt, xt, psum[:, 6 + t % 2, :], ALU.add).then_inc(s["y_added"], 1)

            def group(g, first):
                for c in range(CHUNKS):
                    for r in range(QPG):
                        u = UNITS * g + QPG * c + r
                        prev = not (first and c == 0)
                        if r == 0:
                            if prev:
                                pv_of(u - 1, 1 - c, 1, QPG - 1)
                            dve.wait_ge(s["dk"], CHUNKS * g + c + 1)
                            prod_of(u, c, 0, not prev)
                        else:
                            prod_of(u, c, r % 2)
                            if r == 1 and prev:
                                add(CHUNKS * g + c - 1, 1 - c)
                            if r == 1:
                                dve.wait_ge(s["dv"], CHUNKS * g + c + 1)
                            pv_of(u - 1, c, (r - 1) % 2, r - 1, not prev and r == 1)

            group(0, True)
            with dve.Fori(1, KVB) as g:
                group(g, False)
            pv_of(UNITS * KVB - 1, CHUNKS - 1, 1, QPG - 1)
            add(CHUNKS * KVB - 1, CHUNKS - 1)

        @block.tensor
        def _(pe):
            pe.wait_ge(s["ones"], 1)

            def product(g, p, out, m_hi, m_lo, c, name):
                pe.wait_ge(s["w_lo"], PIECES * g + p + 1)
                cols = slice(c * GROUP, (c + 1) * GROUP)
                for k in range(KT):
                    w = slice(k * P, (k + 1) * P)
                    ins = product3(pe, out, w_hi[:, p, w], w_lo[:, p, w], m_hi[:, k, cols], m_lo[:, k, cols], k == 0, k == KT - 1)
                ins.then_inc(s[name], 1)

            def score(u, k, may_wait=True):
                pe.wait_ge(s["prod_lo"], u + 1)
                if may_wait:
                    pe.wait_ge(s["prob"], u - 1)
                pe.matmul(psum[:, 4 + k, :], ones[:, :], prod_hi[:, k, :], start=True, stop=False)
                pe.matmul(psum[:, 4 + k, :], ones[:, :], prod_lo[:, k, :], start=False, stop=True).then_inc(s["summed"], 1)

            def project(chunk, first):
                pe.wait_ge(s["pv_lo"], QPG * chunk + QPG)
                for t in range(GT):
                    if not (first and t < 2):
                        pe.wait_ge(s["y_added"], GT * chunk + t - 1)
                    cols = slice(t * P, (t + 1) * P)
                    for r in range(QPG):
                        ins = product3(pe, psum[:, 6 + t % 2, :], pv_hi[:, r, cols], pv_lo[:, r, cols],
                                       w_hi[:, O_AT + r, :], w_lo[:, O_AT + r, :], r == 0, r == QPG - 1)
                    ins.then_inc(s["y_done"], 1)

            def group(g, first):
                for c in range(CHUNKS):
                    for r in range(QPG):
                        u = UNITS * g + QPG * c + r
                        begin = first and c == 0
                        if r == 0:
                            if not begin:
                                pe.wait_ge(s["dk"], CHUNKS * g + c)
                            product(g, K_AT, psum[:, 0, :], dT_hi, dT_lo, c, "dk_done")
                            if not begin:
                                score(u - 1, 1)
                                pe.wait_ge(s["dv"], CHUNKS * g + c)
                            product(g, V_AT, psum[:, 1, :], dT_hi, dT_lo, c, "dv_done")
                        if not (begin and r < 2):
                            pe.wait_ge(s["prod"], u - 1)
                        product(g, Q_AT + r, psum[:, 2 + r % 2, :], xT_hi, xT_lo, c, "q_done")
                        if r == 1 and not begin:
                            if c == 1:
                                pe.wait_ge(s["w_lo"], PIECES * g + PIECES)
                            project(CHUNKS * g + c - 1, first and c == 1)
                        if r:
                            score(u - 1, (r - 1) % 2, not (begin and r < 3))

            group(0, True)
            with pe.Fori(1, KVB) as g:
                group(g, False)
            score(UNITS * KVB - 1, 1)
            project(CHUNKS * KVB - 1, False)



def layer(nc, dram, out):
    with ExitStack() as ctx:
        x_sb = ctx.enter_context(nc.sbuf_tensor("x_sb", [P, TILES, DM], F32))
        ident = ctx.enter_context(nc.sbuf_tensor("ident", [P, P], F32))
        psum = ctx.enter_context(nc.psum_tensor("psum", [P, 8, 512], F32))

        def sem(name):
            return ctx.enter_context(nc.semaphore(name))

        with ExitStack() as first:
            def buf(name, shape, dt=F32):
                return first.enter_context(nc.sbuf_tensor(name, shape, dt))

            qkvT = buf("qkvT", [P, 3, TOK])
            pre = {
                "wqk": buf("p_wqk", [P, 2, HA * EA]), "wvT": buf("p_wvT", [P, HEAD_TILES, W]),
                "wo": buf("p_wo", [P, HEAD_TILES, W]), "bq": buf("p_bq", [P, HEAD_TILES]),
                "bk": buf("p_bk", [P, HEAD_TILES]), "bv": buf("p_bv", [P, HEAD_TILES]), "bo": buf("p_bo", [P, 1]),
                "proj_w": buf("p_proj_w", [P, DM]), "proj_b": buf("p_proj_b", [P, DM]), "mask": buf("p_mask", [P, HPS * P]),
            }
            loads = [(pre[n][:], dram[n]) for n in pre]
            pre["loads"], pre["total"], pre["in"] = loads, 16 * len(loads), sem("p_in")
            conv_stage(nc, psum, sem, x_sb, ident, qkvT, pre, dram)
            attention_a_stage(nc, psum, sem, x_sb, ident, qkvT, pre, dram)
        ffn_sems = {n: sem("f_" + n) for n in FFN_SEMS}
        ffn_stage(nc, psum, ffn_sems, x_sb, ident, dram, 0, None)
        attention_b_stage(nc, psum, sem, x_sb, ident, dram)
        ffn_stage(nc, psum, ffn_sems, x_sb, ident, dram, 1, out)



def kernel(L0_attn_a_inputs, L0_attn_a_conv_w, L0_attn_a_conv_b, L0_attn_a_wq, L0_attn_a_bq, L0_attn_a_wk, L0_attn_a_bk,
           L0_attn_a_wv, L0_attn_a_bv, L0_attn_a_wo, L0_attn_a_bo, L0_attn_a_proj_w, L0_attn_a_proj_b,
           L0_attn_b_weight_qkv, L0_attn_b_weight_proj, L0_ffn_gate_w, L0_ffn_u, L0_ffn_g, L0_ffn_d):
    import numpy as np
    import concourse.bacc as bacc
    from concourse.bass_utils import run_bass_kernel_spmd

    def rows(a, n):
        return a.reshape(n, P, -1).transpose(1, 0, 2)

    def column(a):
        return a.reshape(-1, P).T

    wqkv = np.asarray(L0_attn_b_weight_qkv)
    wqkv_g = wqkv.reshape(KVB, ROWS_G // EB, EB, KT, P)
    pieces = wqkv_g.transpose(0, 1, 4, 3, 2).reshape(KVB, ROWS_G // EB, P, KT * EB)
    wprojT = np.asarray(L0_attn_b_weight_proj).T.reshape(KVB, QPG, EB, DM)
    order = [QPG, QPG + 1, *range(QPG)]
    spread = np.zeros((2 * EXPERTS, FF), np.float32)
    for e in range(EXPERTS):
        spread[e, e * INTER:(e + 1) * INTER] = 1
        spread[EXPERTS + e, e * INTER:(e + 1) * INTER] = 1
    arrays = {
        "x": np.asarray(L0_attn_a_inputs).reshape(TOK, DM),
        "conv_w": rows(np.asarray(L0_attn_a_conv_w).reshape(TAPS * DM, 3 * W), TAPS * KT),
        "conv_b": column(np.asarray(L0_attn_a_conv_b)),
        "wqk": np.stack([np.asarray(L0_attn_a_wq).reshape(W, HA * EA), np.asarray(L0_attn_a_wk).reshape(W, HA * EA)], 1),
        "wvT": rows(np.asarray(L0_attn_a_wv).reshape(W, HA * EA).T, HEAD_TILES),
        "wo": rows(np.asarray(L0_attn_a_wo).reshape(HA * EA, W), HEAD_TILES),
        "bq": column(np.asarray(L0_attn_a_bq)), "bk": column(np.asarray(L0_attn_a_bk)),
        "bv": column(np.asarray(L0_attn_a_bv)), "bo": column(np.asarray(L0_attn_a_bo)),
        "proj_w": np.asarray(L0_attn_a_proj_w),
        "proj_b": np.broadcast_to(np.asarray(L0_attn_a_proj_b)[None, :], (P, DM)),
        "mask": np.tile(np.triu(np.full((P, P), MASKED, np.float32), 1), (1, HPS)),
        "ident": np.eye(P, dtype=np.float32),
        "gate_w": rows(np.asarray(L0_ffn_gate_w).T, KT),
        "ffn_w": np.concatenate([rows(np.asarray(L0_ffn_g).T, KT), rows(np.asarray(L0_ffn_u).T, KT),
                                 rows(np.asarray(L0_ffn_d).T, FT).reshape(P, KT, FF)], 1),
        "spread": spread,
        "rank": np.tile(np.arange(EXPERTS, 0, -1, dtype=np.float32), (P, 1)),
        "wB": np.concatenate([pieces[:, order], wprojT], 1).reshape(KVB * (2 + 2 * QPG), P, DM),
        "wv": wqkv.reshape(KVB, QPG + 2, EB, DM)[:, QPG + 1].transpose(1, 0, 2),
        "wpT": wprojT.transpose(0, 2, 1, 3),
    }
    nc = bacc.Bacc("TRN2", target_bir_lowering=False, num_devices=1)
    dram, sent = {}, {}
    for name, a in arrays.items():
        a = np.ascontiguousarray(a)
        sent["in_" + name] = a
        dram[name] = nc.dram_tensor("in_" + name, a.shape, mybir.dt.from_np(a.dtype), kind="ExternalInput").ap()
    out = nc.dram_tensor("out", (TOK, DM), F32, kind="ExternalOutput").ap()
    layer(nc, dram, out)
    r = run_bass_kernel_spmd(nc, [sent], core_ids=[0])
    return r.results[0]["out"].reshape(SEQS, LEN, DM)
```

```python
from contextlib import ExitStack

import concourse.bass as bass
from concourse import mybir

F32 = mybir.dt.float32
F32R = mybir.dt.float32r
BF16 = mybir.dt.bfloat16
ACT = mybir.ActivationFunctionType
ALU = mybir.AluOpType
AX_X = mybir.AxisListType.X

P = 128
SEQS, LEN, DM = 2, 1024, 512
TOK = SEQS * LEN
TILES = TOK // P
KT = DM // P
GROUP = 512
GT = GROUP // P
GROUPS = TOK // GROUP
ST = LEN // P
EPS = 1e-5

TAPS, W, HA, EA = 3, 128, 16, 64
PADDED = LEN + TAPS - 1
HEAD_TILES = HA * EA // P
HPS = 4
BLOCK_STEPS = HA // HPS
STEPS = GT * BLOCK_STEPS
SCALE_A = EA ** -0.5
MASKED = -1e30

HB, KVB, EB = 32, 8, 128
QPG = HB // KVB
ROWS_G = (QPG + 2) * EB
SCALE_B = EB ** -0.5
PIECES_B = 2 + 2 * QPG
RING_B = PIECES_B // 2

EXPERTS, INTER = 16, 56
FF = EXPERTS * INTER
FT = FF // P

ds = bass.ds


def heads_of(step):
    return [8 * (step // 2) + 2 * m + step % 2 for m in range(HPS)]


def product3(pe, out, w_hi, w_lo, x_hi, x_lo, first, last):
    pe.matmul(out, w_hi, x_hi, start=first, stop=False)
    pe.matmul(out, w_hi, x_lo, start=False, stop=False)
    return pe.matmul(out, w_lo, x_hi, start=False, stop=last)


def wait_on_cell(eng, cell, sem, value):
    eng.wait_ge(sem, value)
    eng.tensor_tensor(cell[:, 0:1], cell[:, 1:2], cell[:, 1:2], ALU.mult)


def pool_copy(pool, out, src, zero):
    return pool.tensor_tensor(out, src, zero, ALU.add)


def take_hi(act, hi, src):
    return act.activation(hi, src, ACT.Copy)


def take_lo(eng, lo, src, hi):
    return eng.tensor_tensor(lo, src, hi.bitcast(F32), ALU.subtract)



def conv_stage(nc, psum, sem, x_sb, ident, qkvT, prefetch, entry, dram):
    with ExitStack() as ctx:
        def buf(name, shape, dt=F32):
            return ctx.enter_context(nc.sbuf_tensor("c_" + name, shape, dt))

        xnT_hi = buf("xnT_hi", [P, KT, SEQS * PADDED], F32R)
        xnT_lo = buf("xnT_lo", [P, KT, SEQS * PADDED], F32R)
        both = entry.raw[:, :, :, :].rearrange("p a b n -> p a (b n)")
        w_raw = [both[:, t, 0:KT * 3 * W].rearrange("p (k w) -> p k w", k=KT) for t in range(2)]
        w_raw.append(buf("w_raw", [P, KT, 3 * W])[:, :, :])
        warm = buf("warm", [P, 1])
        w_hi = buf("w_hi", [P, TAPS * KT, 3 * W], F32R)
        w_lo = buf("w_lo", [P, TAPS * KT, 3 * W], F32R)
        conv_b = buf("b", [P, 3])
        eps = buf("eps", [P, 1])
        stats = buf("stats", [P, TILES, 6])
        mv = buf("mv", [P, TILES, 2])
        std = buf("std", [P, TILES])
        rstd = buf("rstd", [P, TILES])
        xn = entry.xn

        names = ("warmed b_in eps_set pads w_hi_ready w_lo_ready stats var std rstd xn turned hi lo conv_done conv_out")
        s = {n: sem("c_" + n) for n in names.split()}
        x_in = [sem(f"c_x_in{g}") for g in range(GROUPS)]
        w_in = [sem(f"c_w_in{t}") for t in range(TAPS)]
        turn_ps = [psum[:, b, :].rearrange("p (k n) -> p k n", k=KT) for b in (0, 1)]
        conv_ps = [psum[:, b, :] for b in (2, 3)]

        units = [(n, half, o) for n in range(SEQS) for half in range(2) for o in range(3)]
        tiles_for = {(0, 0): GT + 1, (0, 1): ST, (1, 0): ST + GT + 1, (1, 1): TILES}
        AHEAD, AFTER = GT + 1, 2

        def at(t):
            return (t // ST) * PADDED + 1 + (t % ST) * P

        block = ctx.enter_context(nc.Block())

        @block.sync
        def _(sp):
            xv = dram["x"].rearrange("(t p) n -> p t n", p=P)

            def load_x(g):
                sp.dma_start(x_sb[:, GT * g:GT * (g + 1), :], xv[:, GT * g:GT * (g + 1), :]).then_inc(x_in[g], 16)

            def load_w(t):
                sp.dma_start(w_raw[t], dram["conv_w"][:, KT * t:KT * (t + 1), :]).then_inc(w_in[t], 16)

            load_x(0)
            sp.dma_start(ident[:, :], dram["ident"]).then_inc(s["b_in"], 16)
            sp.dma_start(conv_b[:, :], dram["conv_b"]).then_inc(s["b_in"], 16)
            load_w(0)
            load_x(1)
            load_w(1)
            load_w(2)
            load_x(2)
            load_x(3)
            for dst, src in prefetch["loads"]:
                sp.dma_start(dst, src).then_inc(prefetch["in"], 16)

        @block.gpsimd
        def _(pool):
            pool.memset(eps[:, :], EPS).then_inc(s["eps_set"], 1)
            entry.clear(pool)
            for t in (xnT_hi, xnT_lo):
                ends = t[:, :, :].bitcast(F32).rearrange("p k (s n) -> p k s n", s=SEQS)
                for col in (0, PADDED - 1):
                    pool.memset(ends[:, :, :, col:col + 1], 0.0).then_inc(s["pads"], 1)
            for t in range(TAPS):
                taps = slice(KT * t, KT * (t + 1))
                pool.wait_ge(s["w_hi_ready"], t + 1)
                take_lo(pool, w_lo[:, taps, :], w_raw[t], w_hi[:, taps, :]).then_inc(s["w_lo_ready"], 1)

        @block.vector
        def _(dve):
            def stats_of(g):
                dve.wait_ge(x_in[g], 16)
                for t in range(GT * g, GT * g + GT):
                    dve.bn_stats(stats[:, t, :], x_sb[:, t, :]).then_inc(s["stats"], 1)
                dve.wait_ge(s["stats"], GT * g + GT)
                for t in range(GT * g, GT * g + GT):
                    dve.bn_aggr(mv[:, t, :], stats[:, t, :]).then_inc(s["var"], 1)

            def norm(t):
                if t % GT == 0:
                    g = t // GT
                    cols = slice(t, t + GT)
                    dve.wait_ge(s["std"], g + 1)
                    dve.reciprocal(rstd[:, cols], std[:, cols]).then_inc(s["rstd"], 1)
                    dve.wait_ge(s["rstd"], g + 1)
                if t >= 2:
                    dve.wait_ge(s["turned"], t - 1)
                dve.tensor_scalar(xn[:, t % 2, :], x_sb[:, t, :], mv[:, t, 0:1], rstd[:, t:t + 1],
                                  ALU.subtract, ALU.mult).then_inc(s["xn"], 1)

            stats_of(0)
            norm(0)
            for t in range(TILES):
                if t % GT == 1 and t // GT + 1 < GROUPS:
                    stats_of(t // GT + 1)
                if t + 1 < TILES:
                    norm(t + 1)
                dve.wait_ge(s["hi"], t + 1)
                cols = slice(at(t), at(t) + P)
                take_lo(dve, xnT_lo[:, :, cols], turn_ps[t % 2], xnT_hi[:, :, cols]).then_inc(s["lo"], 1)

        @block.scalar
        def _(act):
            act.wait_ge(s["eps_set"], 1)
            act.activation(warm[:, :], eps[:, :], ACT.Sqrt).then_inc(s["warmed"], 1)
            act.wait_ge(s["b_in"], 32)

            def root(g):
                act.wait_ge(s["var"], GT * g + GT)
                cols = slice(GT * g, GT * g + GT)
                act.activation(std[:, cols], mv[:, cols, 1], ACT.Sqrt, bias=eps[:, 0:1]).then_inc(s["std"], 1)

            def high(t):
                act.wait_ge(s["turned"], t + 1)
                take_hi(act, xnT_hi[:, :, at(t):at(t) + P], turn_ps[t % 2]).then_inc(s["hi"], 1)
                if t % GT == 1 and t // GT + 1 < GROUPS:
                    root(t // GT + 1)

            def high_w(t):
                act.wait_ge(w_in[t], 16)
                take_hi(act, w_hi[:, KT * t:KT * (t + 1), :], w_raw[t]).then_inc(s["w_hi_ready"], 1)

            root(0)
            high(0)
            high(1)
            high_w(0)
            high(2)
            high(3)
            high_w(1)
            high(4)
            high_w(2)
            for c, (n, half, o) in enumerate(units):
                act.wait_ge(s["conv_done"], c + 1)
                first = n * LEN + half * GROUP
                act.activation(qkvT[:, o, first:first + GROUP], conv_ps[c % 2], ACT.Identity,
                               bias=conv_b[:, o:o + 1]).then_inc(s["conv_out"], 1)
                for t in range(AHEAD + AFTER * c, min(AHEAD + AFTER * (c + 1), TILES)):
                    high(t)

        @block.tensor
        def _(pe):
            pe.wait_ge(s["b_in"], 32)
            pe.wait_ge(s["pads"], 4)

            def turn(t):
                pe.wait_ge(s["xn"], t + 1)
                if t >= 2:
                    pe.wait_ge(s["lo"], t - 1)
                for k in range(KT):
                    ins = pe.transpose(turn_ps[t % 2][:, k, :], xn[:, t % 2, k * P:(k + 1) * P], ident[:, :])
                ins.then_inc(s["turned"], 1)

            for t in range(AHEAD):
                turn(t)
            for c, (n, half, o) in enumerate(units):
                pe.wait_ge(s["lo"], tiles_for[n, half])
                if c >= 2:
                    pe.wait_ge(s["conv_out"], c - 1)
                for tap in range(TAPS):
                    if c == 0:
                        pe.wait_ge(s["w_lo_ready"], tap + 1)
                    for k in range(KT):
                        first = n * PADDED + half * GROUP + tap
                        kk, cols = tap * KT + k, slice(o * W, (o + 1) * W)
                        ins = product3(pe, conv_ps[c % 2], w_hi[:, kk, cols], w_lo[:, kk, cols],
                                       xnT_hi[:, k, first:first + GROUP], xnT_lo[:, k, first:first + GROUP],
                                       kk == 0, kk == TAPS * KT - 1)
                ins.then_inc(s["conv_done"], 1)
                for t in range(AHEAD + AFTER * c, min(AHEAD + AFTER * (c + 1), TILES)):
                    turn(t)



def attention_a_stage(nc, psum, sem, x_sb, ident, qkvT, pre, entry, dram):
    with ExitStack() as ctx:
        def buf(name, shape, dt=F32):
            return ctx.enter_context(nc.sbuf_tensor("a_" + name, shape, dt))

        wqk_hi = buf("wqk_hi", [P, 2, HA * EA], F32R)
        wqk_lo = buf("wqk_lo", [P, 2, HA * EA], F32R)
        vo_hi = buf("vo_hi", [P, BLOCK_STEPS, HPS * W], F32R)
        vo_lo = buf("vo_lo", [P, BLOCK_STEPS, HPS * W], F32R)
        obias = buf("obias", [P, 1])
        mask16 = buf("mask16", [P, HPS * P], BF16)
        ident16 = buf("ident16", [P, P], BF16)
        s_hi = buf("split_hi", [P, 3, GROUP], F32R)
        s_lo = buf("split_lo", [P, 3, GROUP], F32R)
        qh = buf("qh", [P, HEAD_TILES, GROUP])
        kh = buf("kh", [P, HEAD_TILES, GROUP])
        vo = buf("vo", [P, 4, HPS * W])
        mx = buf("mx", [P, 2, HPS])
        prob = buf("prob", [P, 4, HPS, P])
        sums = buf("sums", [P, 2, HPS])
        rsum = buf("rsum", [P, 2, HPS])
        probT = buf("probT", [P, 2, HPS * P])
        oT = buf("oT", [P, 2, P])

        names = ("w_hi w_lo vo_made vo_hi vo_lo bias_made bias_ready consts hi lo vhi vlo projected qh kh scored "
                 "max_ready sub_done exp_done sum_ready rsum_ready normed vo_done vo_ready probs_turned probT_ready "
                 "pv_done oT_ready y_done y_added pb_added")
        s = {n: sem("a_" + n) for n in names.split()}

        block = ctx.enter_context(nc.Block())

        @block.sync
        def _(sp):
            for j in range(2):
                entry.load_piece(sp, 0, j)

        score_ps = [psum[:, b, :] for b in (0, 1)]
        vo_ps = [psum[:, b, :] for b in (2, 3)]
        turn_ps = [psum[:, b, :] for b in (4, 5)]
        out_ps = [psum[:, b, :] for b in (6, 7)]
        N_PROJ = 2 * HEAD_TILES
        TURN = 3
        PV, Y = TURN + 1, TURN + 2
        DRAIN = Y
        proj_at = {STEPS + d: range(4 * d, 4 * d + 4) for d in range(N_PROJ // 4)}

        def proj_ps(n):
            return (vo_ps, score_ps)[n % 2][n // 2 % 2]

        def is_block_end(u):
            return u % BLOCK_STEPS == BLOCK_STEPS - 1

        @block.scalar
        def _(act):
            act.wait_ge(pre["in"], pre["total"])
            act.activation(ident16[:, :], ident[:, :], ACT.Copy).then_inc(s["consts"], 1)
            act.activation(mask16[:, :], pre["mask"][:, :], ACT.Copy).then_inc(s["consts"], 1)
            for w in range(2):
                take_hi(act, wqk_hi[:, w, :], pre["wqk"][:, w, :]).then_inc(s["w_hi"], 1)
            for c in range(BLOCK_STEPS):
                act.wait_ge(s["vo_made"], c + 1)
                take_hi(act, vo_hi[:, c, :], psum[:, c, :]).then_inc(s["vo_hi"], 1)
            act.wait_ge(s["bias_made"], 1)
            act.activation(obias[:, :], psum[:, 4, 0:1], ACT.Identity, bias=pre["bo"][:, 0:1]).then_inc(s["bias_ready"], 1)

            def split(i, o):
                src = qkvT[:, o, ds(i * GROUP, GROUP)]
                take_hi(act, s_hi[:, o, :], src).then_inc(s["vhi"] if o == 2 else s["hi"], 1)

            def q_out(i, n):
                t = n // 2
                act.wait_ge(s["projected"], N_PROJ * i + n + 1)
                act.activation(qh[:, t, :], proj_ps(n), ACT.Identity, bias=pre["bq"][:, t:t + 1]).then_inc(s["qh"], 1)

            def group(i, last):
                for u in range(STEPS + DRAIN):
                    if u < STEPS:
                        act.wait_ge(s["sub_done"], STEPS * i + u + 1)
                        act.activation(prob[:, u % 4, :, :], prob[:, u % 4, :, :], ACT.Exp, scale=SCALE_A).then_inc(s["exp_done"], 1)
                        act.wait_ge(s["vo_done"], STEPS * i + u + 1)
                        if u >= 4:
                            act.wait_ge(s["pv_done"], STEPS * i + u - 3)
                        act.activation(vo[:, u % 4, :], vo_ps[u % 2], ACT.Copy).then_inc(s["vo_ready"], 1)
                    if u in proj_at and not last:
                        q_out(i + 1, proj_at[u][0])
                    if TURN <= u < STEPS + TURN:
                        t = u - TURN
                        act.wait_ge(s["probs_turned"], STEPS * i + t + 1)
                        if t >= 2:
                            act.wait_ge(s["pv_done"], STEPS * i + t - 1)
                        act.activation(probT[:, t % 2, :], turn_ps[t % 2], ACT.Copy).then_inc(s["probT_ready"], 1)
                    if u == STEPS - 3 and not last:
                        split(i + 1, 0)
                        split(i + 1, 1)
                    if u == STEPS + 1 and not last:
                        act.wait_ge(s["vo_done"], STEPS * i + STEPS)
                        split(i + 1, 2)
                    if u >= PV and is_block_end(u - PV):
                        b = (u - PV) // BLOCK_STEPS
                        act.wait_ge(s["pv_done"], STEPS * i + u - PV + 1)
                        if b >= 2:
                            act.wait_ge(s["y_done"], GT * i + b - 1)
                        act.activation(oT[:, b % 2, :], out_ps[b % 2][:, 0:P], ACT.Identity,
                                       bias=obias[:, 0:1]).then_inc(s["oT_ready"], 1)
                    if u in proj_at and not last:
                        q_out(i + 1, proj_at[u][2])
                    if u == 4 and last:
                        entry.root(act, 0)

            for o in range(3):
                split(0, o)
            for n in range(0, N_PROJ, 2):
                q_out(0, n)
            with act.Fori(0, GROUPS - 1) as i:
                group(i, False)
            group(GROUPS - 1, True)

        @block.vector
        def _(dve):
            dve.wait_ge(pre["in"], pre["total"])
            for w in range(2):
                dve.wait_ge(s["w_hi"], w + 1)
                take_lo(dve, wqk_lo[:, w, :], pre["wqk"][:, w, :], wqk_hi[:, w, :]).then_inc(s["w_lo"], 1)
            for c in range(BLOCK_STEPS):
                dve.wait_ge(s["vo_hi"], c + 1)
                take_lo(dve, vo_lo[:, c, :], psum[:, c, :], vo_hi[:, c, :]).then_inc(s["vo_lo"], 1)

            def split(i, o):
                dve.wait_ge(s["vhi"] if o == 2 else s["hi"], i + 1 if o == 2 else 2 * i + o + 1)
                src = qkvT[:, o, ds(i * GROUP, GROUP)]
                take_lo(dve, s_lo[:, o, :], src, s_hi[:, o, :]).then_inc(s["vlo"] if o == 2 else s["lo"], 1)

            def k_out(i, n):
                t = n // 2
                dve.wait_ge(s["projected"], N_PROJ * i + n + 1)
                dve.tensor_scalar(kh[:, t, :], proj_ps(n), pre["bk"][:, t:t + 1], None, ALU.add).then_inc(s["kh"], 1)

            def group(i, last):
                for u in range(STEPS + DRAIN + 1):
                    if u < STEPS:
                        scores = score_ps[u % 2].rearrange("p (h k) -> p h k", h=HPS)
                        dve.wait_ge(s["scored"], STEPS * i + u + 1)
                        dve.tensor_reduce(mx[:, u % 2, :], scores, AX_X, ALU.max).then_inc(s["max_ready"], 1)
                        if u >= 4:
                            dve.wait_ge(s["probs_turned"], STEPS * i + u - 3)
                        dve.wait_ge(s["max_ready"], STEPS * i + u + 1)
                        dve.tensor_tensor(prob[:, u % 4, :, :], scores, mx[:, u % 2, :].unsqueeze(2).broadcast_to([P, HPS, P]),
                                          ALU.subtract).then_inc(s["sub_done"], 1)
                    if 1 <= u < STEPS + 1:
                        t = u - 1
                        dve.wait_ge(s["exp_done"], STEPS * i + t + 1)
                        dve.tensor_reduce(sums[:, t % 2, :], prob[:, t % 4, :, :], AX_X, ALU.add).then_inc(s["sum_ready"], 1)
                        dve.wait_ge(s["sum_ready"], STEPS * i + t + 1)
                        if t >= 2:
                            dve.wait_ge(s["normed"], STEPS * i + t - 1)
                        dve.reciprocal(rsum[:, t % 2, :], sums[:, t % 2, :]).then_inc(s["rsum_ready"], 1)
                    if u == STEPS - 2 and not last:
                        split(i + 1, 0)
                        split(i + 1, 1)
                    if u == STEPS + 1 and not last:
                        split(i + 1, 2)
                    if u in proj_at and not last:
                        k_out(i + 1, proj_at[u][1])
                        k_out(i + 1, proj_at[u][3])
                    if last and u == 2:
                        entry.take_stats(dve, 0, 0)
                    if last and u == 7:
                        entry.norm(dve, 0, 0)
                    if u > Y and is_block_end(u - Y - 1):
                        b = (u - Y - 1) // BLOCK_STEPS
                        dve.wait_ge(s["y_done"], GT * i + b + 1)
                        if b == 0:
                            dve.wait_ge(s["pb_added"], i + 1)
                        xt = x_sb[:, ds(GT * i + b, 1), :]
                        dve.tensor_tensor(xt, xt, out_ps[b % 2].unsqueeze(1), ALU.add).then_inc(s["y_added"], 1)
                dve.wait_ge(s["y_added"], GT * i + GT)

            for o in range(3):
                split(0, o)
            for n in range(1, N_PROJ, 2):
                k_out(0, n)
            with dve.Fori(0, GROUPS - 1) as i:
                group(i, False)
            group(GROUPS - 1, True)

        @block.gpsimd
        def _(pool):
            pool.wait_ge(pre["in"], pre["total"])
            with pool.Fori(0, GROUPS) as i:
                xg = x_sb[:, ds(GT * i, GT), :]
                pool.tensor_tensor(xg, xg, pre["proj_b"][:, :].unsqueeze(1).broadcast_to([P, GT, DM]), ALU.add).then_inc(s["pb_added"], 1)
                for u in range(STEPS):
                    pool.wait_ge(s["rsum_ready"], STEPS * i + u + 1)
                    p = prob[:, u % 4, :, :]
                    pool.tensor_tensor(p, p, rsum[:, u % 2, :].unsqueeze(2).broadcast_to([P, HPS, P]), ALU.mult).then_inc(s["normed"], 1)

        @block.tensor
        def _(pe):
            pe.wait_ge(pre["in"], pre["total"])
            for c in range(BLOCK_STEPS):
                for m, h in enumerate(heads_of(c)):
                    rows = slice(EA * (h % 2), EA * (h % 2) + EA)
                    ins = pe.matmul(psum[:, c, m * W:(m + 1) * W], pre["wvT"][rows, h // 2, :], pre["wo"][rows, h // 2, :],
                                    start=True, stop=True)
                ins.then_inc(s["vo_made"], 1)
            for t in range(HEAD_TILES):
                ins = pe.matmul(psum[:, 4, 0:1], pre["wo"][:, t, :], pre["bv"][:, t:t + 1],
                                start=t == 0, stop=t == HEAD_TILES - 1)
            ins.then_inc(s["bias_made"], 1)
            pe.wait_ge(s["vo_lo"], BLOCK_STEPS)
            pe.wait_ge(s["bias_ready"], 1)
            pe.wait_ge(s["w_lo"], 2)
            pe.wait_ge(s["consts"], 2)

            def project(i, n):
                w, t = n % 2, n // 2
                if n < 2:
                    pe.wait_ge(s["lo"], 2 * i + w + 1)
                elif n >= 4:
                    pe.wait_ge(s["kh"] if w else s["qh"], HEAD_TILES * i + t - 1)
                cols = slice(t * P, (t + 1) * P)
                product3(pe, proj_ps(n), wqk_hi[:, w, cols], wqk_lo[:, w, cols], s_hi[:, w, :], s_lo[:, w, :],
                         True, True).then_inc(s["projected"], 1)

            def group(i, last):
                for u in range(STEPS + DRAIN + 1):
                    if u < STEPS:
                        b, c = u // BLOCK_STEPS, u % BLOCK_STEPS
                        cols = slice(b * P, (b + 1) * P)
                        if u == 0:
                            pe.wait_ge(s["qh"], HEAD_TILES * i + HEAD_TILES)
                            pe.wait_ge(s["kh"], HEAD_TILES * i + HEAD_TILES)
                            pe.wait_ge(s["vlo"], i + 1)
                        else:
                            if u >= 2:
                                pe.wait_ge(s["sub_done"], STEPS * i + u - 1)
                                pe.wait_ge(s["vo_ready"], STEPS * i + u - 1)
                        pe.matmul(score_ps[u % 2], ident16[:, :], mask16[:, :], start=True, stop=False, skip_group_check=True)
                        for m, h in enumerate(heads_of(c)):
                            rows = slice(EA * (h % 2), EA * (h % 2) + EA)
                            ins = pe.matmul(score_ps[u % 2][:, m * P:(m + 1) * P], qh[rows, h // 2, cols], kh[rows, h // 2, cols],
                                            start=False, stop=m == HPS - 1, skip_group_check=True)
                        ins.then_inc(s["scored"], 1)
                        product3(pe, vo_ps[u % 2], s_hi[:, 2, cols], s_lo[:, 2, cols], vo_hi[:, c, :], vo_lo[:, c, :],
                                 True, True).then_inc(s["vo_done"], 1)
                    if u in proj_at and not last:
                        if u == STEPS:
                            pe.wait_ge(s["vo_ready"], STEPS * i + STEPS - 1)
                            pe.wait_ge(s["sub_done"], STEPS * i + STEPS - 1)
                        project(i + 1, proj_at[u][0])
                        project(i + 1, proj_at[u][1])
                    if TURN <= u < STEPS + TURN:
                        t = u - TURN
                        pe.wait_ge(s["normed"], STEPS * i + t + 1)
                        if t >= 2:
                            pe.wait_ge(s["probT_ready"], STEPS * i + t - 1)
                        for m in range(HPS):
                            ins = pe.transpose(turn_ps[t % 2][:, m * P:(m + 1) * P], prob[:, t % 4, m, :], ident[:, :])
                        ins.then_inc(s["probs_turned"], 1)
                    if PV <= u < STEPS + PV:
                        t = u - PV
                        b, c = t // BLOCK_STEPS, t % BLOCK_STEPS
                        pe.wait_ge(s["probT_ready"], STEPS * i + t + 1)
                        pe.wait_ge(s["vo_ready"], STEPS * i + t + 1)
                        if c == 0 and b >= 2:
                            pe.wait_ge(s["y_added"], GT * i + b - 1)
                        for m in range(HPS):
                            ins = pe.matmul(out_ps[b % 2][:, 0:P], vo[:, t % 4, m * W:(m + 1) * W], probT[:, t % 2, m * P:(m + 1) * P],
                                            start=c == 0 and m == 0, stop=c == BLOCK_STEPS - 1 and m == HPS - 1)
                        ins.then_inc(s["pv_done"], 1)
                    if u in proj_at and not last:
                        if u == STEPS:
                            pe.wait_ge(s["vo_ready"], STEPS * i + STEPS)
                            pe.wait_ge(s["sub_done"], STEPS * i + STEPS)
                        project(i + 1, proj_at[u][2])
                        project(i + 1, proj_at[u][3])
                    if u >= Y and is_block_end(u - Y):
                        b = (u - Y) // BLOCK_STEPS
                        pe.wait_ge(s["oT_ready"], GT * i + b + 1)
                        pe.matmul(out_ps[b % 2], oT[:, b % 2, :], pre["proj_w"][:, :], start=True, stop=True).then_inc(s["y_done"], 1)

            for n in range(N_PROJ):
                project(0, n)
            with pe.Fori(0, GROUPS - 1) as i:
                group(i, False)
            group(GROUPS - 1, True)



class FfnEntry:

    SEMS = ("set c_in consts eps stats var std rstd xn turned hi lo logitsT lgT logits routed routed2 shifted exped rstep "
            "w wT_turned wT g_done u_done w_done silu up hid h_hi h_lo d_done y_added out w_hi w_lo piece_in0 piece_in1 "
            "wp_in wsum1 wsum").split()
    USES = (FT + 1) // 2, FT // 2

    def __init__(self, buf, sem, x_sb, dram):
        self.s = {n: sem("f_" + n) for n in self.SEMS}
        self.x_sb, self.dram = x_sb, dram
        self.raw = buf("f_raw", [P, 2, 3, DM])
        self.eps = buf("f_eps", [P, 1])
        self.cell = buf("f_cell", [P, 2])
        self.stats = buf("f_stats", [P, GT, 6])
        self.mv = buf("f_mv", [P, GT, 2])
        self.std = buf("f_std", [P, GT])
        self.rstd = buf("f_rstd", [P, GT])
        self.xn = buf("f_xn", [P, GT, DM])

    def tile(self, i, t):
        return self.x_sb[:, ds(GT * i + t, 1), :]

    def landed(self, run, j):
        return self.s[f"piece_in{j % 2}"], 16 * (self.USES[j % 2] * run + j // 2 + 1)

    def load_piece(self, sp, run, j):
        sp.dma_start(self.raw[:, j % 2, :, :], self.dram["ffn_w"][:, j, :, :]).then_inc(self.landed(run, j)[0], 16)

    def clear(self, pool):
        pool.memset(self.eps[:, :], EPS).then_inc(self.s["set"], 1)
        pool.memset(self.cell[:, :], 0.0).then_inc(self.s["set"], 1)

    def take_stats(self, dve, i, at):
        for t in range(GT):
            dve.bn_stats(self.stats[:, t, :], self.tile(at, t)).then_inc(self.s["stats"], 1)
        wait_on_cell(dve, self.cell, self.s["stats"], GT * i + GT)
        for t in range(GT):
            dve.bn_aggr(self.mv[:, t, :], self.stats[:, t, :]).then_inc(self.s["var"], 1)

    def root(self, act, i):
        act.wait_ge(self.s["var"], GT * i + GT)
        act.activation(self.std[:, :], self.mv[:, :, 1], ACT.Sqrt, bias=self.eps[:, 0:1]).then_inc(self.s["std"], 1)

    def norm(self, dve, i, at):
        dve.wait_ge(self.s["std"], i + 1)
        dve.reciprocal(self.rstd[:, :], self.std[:, :]).then_inc(self.s["rstd"], 1)
        dve.wait_ge(self.s["rstd"], i + 1)
        for t in range(GT):
            dve.tensor_scalar(self.xn[:, t, :], self.tile(at, t), self.mv[:, t, 0:1], self.rstd[:, t:t + 1],
                              ALU.subtract, ALU.mult).then_inc(self.s["xn"], 1)


def ffn_stage(nc, psum, entry, ident, dram, run, out, wsum):
    s, raw, xn, x_sb = entry.s, entry.raw, entry.xn, entry.x_sb
    FIRST, LAST = GROUPS * run, GROUPS * run + GROUPS - 1
    PARTS = 3
    W_BEFORE = PARTS * FT * run
    G_PART, U_PART, D_PART = range(PARTS)
    with ExitStack() as ctx:
        def buf(name, shape, dt=F32):
            return ctx.enter_context(nc.sbuf_tensor(f"f{run}_{name}", shape, dt))

        w_hi = buf("w_hi", [P, FT, PARTS, DM], F32R)
        w_lo = buf("w_lo", [P, FT, PARTS, DM], F32R)
        r_raw = buf("r_raw", [P, KT, EXPERTS])
        r_hi = buf("r_hi", [P, KT, P], F32R)
        r_lo = buf("r_lo", [P, KT, P], F32R)
        spread = buf("spread", [2 * EXPERTS, FF], F32R)
        rank = buf("rank", [P, EXPERTS])
        xT_hi = buf("xT_hi", [P, KT, GROUP], F32R)
        xT_lo = buf("xT_lo", [P, KT, GROUP], F32R)
        lgT = buf("lgT", [P, GROUP])
        row = buf("row", [P, 3, GT])
        lg = buf("lg", [P, 6, GT, EXPERTS])
        wsplit = buf("wsplit", [P, GT, 2 * EXPERTS])
        wT = buf("wT", [2 * EXPERTS, GROUP], F32R)
        silu = buf("silu", [P, 2, GROUP])
        up = buf("up", [P, 2, GROUP])
        hid = buf("hid", [P, 2, GROUP])
        hT_hi = buf("hT_hi", [P, 3, GROUP], F32R)
        hT_lo = buf("hT_lo", [P, 3, GROUP], F32R)
        spread_raw = silu[0:2 * EXPERTS, :, :].rearrange("e a n -> e (a n)")[:, 0:FF]

        y_ps = [psum[:, b, :] for b in range(GT)]
        g_ps, u_ps, w_ps, m_ps = (psum[:, GT + b, :] for b in range(4))
        turn_ps = [m_ps, w_ps]

        block = ctx.enter_context(nc.Block())

        @block.sync
        def _(sp):
            for dst, src in ((r_raw[:, :, :], "gate_w"), (spread_raw, "spread"), (rank[:, :], "rank")):
                sp.dma_start(dst, dram[src]).then_inc(s["c_in"], 16)
            for j in range(2, FT):
                sp.wait_ge(s["w_lo"], W_BEFORE + PARTS * (j - 1))
                entry.load_piece(sp, run, j)
            if wsum is not None:
                sp.wait_ge(s["w_lo"], W_BEFORE + PARTS * FT)
                wp = raw[:, :, :, :].rearrange("p a b n -> p (a b) n")[:, 0:QPG, :]
                sp.dma_start(wp, dram["wpT"][0, :, :, :]).then_inc(s["wp_in"], 16)
                with sp.Fori(1, KVB) as g:
                    sp.wait_ge(s["wsum"], g)
                    sp.dma_start(wp, dram["wpT"][ds(g, 1), :, :, :].rearrange("a p q n -> (a p) q n")).then_inc(s["wp_in"], 16)
            if out is not None:
                with sp.Fori(FIRST, LAST + 1) as i:
                    sp.wait_ge(s["y_added"], GT * i + GT)
                    group = ds(GT * (i - FIRST), GT)
                    sp.dma_start(out.rearrange("(t p) n -> p t n", p=P)[:, group, :], x_sb[:, group, :]).then_inc(s["out"], 16)
                sp.wait_ge(s["out"], 16 * GROUPS)

        @block.gpsimd
        def _(pool):
            def low_w(j):
                for part in range(PARTS):
                    pool.wait_ge(s["w_hi"], W_BEFORE + PARTS * j + part + 1)
                    take_lo(pool, w_lo[:, j, part, :], raw[:, j % 2, part, :], w_hi[:, j, part, :]).then_inc(s["w_lo"], 1)

            def head_sum(g):
                wp = raw[:, :, :, :].rearrange("p a b n -> p (a b) n")
                pool.wait_ge(s["wp_in"], 16 * g + 16)
                pool.tensor_tensor(wp[:, 0:2, :], wp[:, 0:2, :], wp[:, 2:4, :], ALU.add).then_inc(s["wsum1"], 1)
                pool.wait_ge(s["wsum1"], g + 1)
                pool.tensor_tensor(wsum[:, ds(g, 1), :], wp[:, 0:1, :], wp[:, 1:2, :], ALU.add).then_inc(s["wsum"], 1)

            def group(i, first=False, sums=()):
                for j in range(FT):
                    if first and j + 2 < FT:
                        low_w(j + 2)
                    pool.wait_ge(s["h_hi"], FT * i + j + 1)
                    take_lo(pool, hT_lo[:, j % 3, :], hid[:, j % 2, :], hT_hi[:, j % 3, :]).then_inc(s["h_lo"], 1)
                    if wsum is not None and j in sums:
                        head_sum(3 * (i - 1) + sums.index(j))

            for r in (r_hi, r_lo):
                pool.memset(r[:, :, :].bitcast(F32), 0.0).then_inc(s["consts"], 1)
            low_w(0)
            low_w(1)
            group(FIRST, first=True)
            with pool.Fori(FIRST + 1, LAST) as i:
                group(i, sums=(1, 3, 5))
            group(LAST, sums=(1, 3))

        CONSTS = 5 * run

        @block.scalar
        def _(act):
            def high_w(j):
                act.wait_ge(*entry.landed(run, j))
                for part in range(PARTS):
                    take_hi(act, w_hi[:, j, part, :], raw[:, j % 2, part, :]).then_inc(s["w_hi"], 1)

            def turn(i, t):
                act.wait_ge(s["turned"], GT * i + t + 1)
                take_hi(act, xT_hi[:, :, t * P:(t + 1) * P],
                        turn_ps[t % 2].rearrange("p (k n) -> p k n", k=KT)).then_inc(s["hi"], 1)

            def route(i):
                act.wait_ge(s["logitsT"], i + 1)
                act.activation(lgT[:, :], m_ps, ACT.Copy).then_inc(s["lgT"], 1)
                act.wait_ge(s["shifted"], i + 1)
                act.activation(lg[:, 1, :, :], lg[:, 0, :, :], ACT.Exp).then_inc(s["exped"], 1)

            def gate(i, j):
                act.wait_ge(s["g_done"], FT * i + j + 1)
                if j >= 2:
                    act.wait_ge(s["up"], FT * i + j - 1)
                act.activation(silu[:, j % 2, :], g_ps, ACT.Silu).then_inc(s["silu"], 1)

            def high(i, j):
                act.wait_ge(s["hid"], FT * i + j + 1)
                if j >= 3:
                    act.wait_ge(s["d_done"], FT * i + j - 2)
                take_hi(act, hT_hi[:, j % 3, :], hid[:, j % 2, :]).then_inc(s["h_hi"], 1)

            def main(i, last=False, first=False):
                for j in range(FT + 1):
                    if first and j + 2 < FT:
                        high_w(j + 2)
                    if j < FT:
                        gate(i, j)
                    if j == 1:
                        act.wait_ge(s["wT_turned"], i + 1)
                        act.activation(wT[:, :], m_ps[0:2 * EXPERTS, :], ACT.Copy).then_inc(s["wT"], 1)
                    if j >= 1:
                        high(i, j - 1)
                    if j == 3 and not last:
                        entry.root(act, i + 1)
                if not last:
                    for t in range(GT):
                        turn(i + 1, t)
                    route(i + 1)

            for t in range(2):
                turn(FIRST, t)
            act.wait_ge(s["consts"], CONSTS + 2)
            act.wait_ge(s["c_in"], 48 * (run + 1))
            take_hi(act, r_hi[:, :, 0:EXPERTS], r_raw[:, :, :]).then_inc(s["consts"], 1)
            act.activation(spread[:, :], spread_raw, ACT.Copy).then_inc(s["consts"], 1)
            for t in range(2, GT):
                turn(FIRST, t)
            high_w(0)
            route(FIRST)
            high_w(1)
            main(FIRST, first=True)
            with act.Fori(FIRST + 1, LAST) as i:
                main(i)
            main(LAST, last=True)

        @block.vector
        def _(dve):
            def low(i, t):
                dve.wait_ge(s["hi"], GT * i + t + 1)
                cols = slice(t * P, (t + 1) * P)
                take_lo(dve, xT_lo[:, :, cols], turn_ps[t % 2].rearrange("p (k n) -> p k n", k=KT),
                        xT_hi[:, :, cols]).then_inc(s["lo"], 1)

            def gate_up(i, j):
                dve.wait_ge(s["silu"], FT * i + j + 1)
                dve.wait_ge(s["u_done"], FT * i + j + 1)
                dve.tensor_tensor(up[:, j % 2, :], silu[:, j % 2, :], u_ps, ALU.mult).then_inc(s["up"], 1)

            def weigh(i, j):
                dve.wait_ge(s["w_done"], FT * i + j + 1)
                if j >= 2:
                    dve.wait_ge(s["h_lo"], FT * i + j - 1)
                dve.wait_ge(s["up"], FT * i + j + 1)
                dve.tensor_tensor(hid[:, j % 2, :], up[:, j % 2, :], w_ps, ALU.mult).then_inc(s["hid"], 1)

            R_STEPS = 16

            def route(i):
                at = [0]

                def done(ins):
                    at[0] += 1
                    ins.then_inc(s["rstep"], 1)
                    dve.wait_ge(s["rstep"], R_STEPS * i + at[0])

                def wide(r):
                    return r.unsqueeze(2).broadcast_to([P, GT, EXPERTS])

                ranks = rank[:, :].unsqueeze(1).broadcast_to([P, GT, EXPERTS])
                logits = w_ps.rearrange("p (t e) -> p t e", t=GT)[:, :, 0:EXPERTS]
                a, e, c, one1, one2, left = (lg[:, k, :, :] for k in range(6))
                m, first, second = (row[:, k, :] for k in range(3))
                dve.wait_ge(s["logits"], i + 1)
                done(dve.tensor_reduce(m, logits, AX_X, ALU.max))
                dve.tensor_tensor(a, logits, wide(m), ALU.subtract).then_inc(s["shifted"], 1)
                dve.wait_ge(s["exped"], i + 1)
                done(dve.tensor_reduce(m, e, AX_X, ALU.add))
                done(dve.reciprocal(m, m))
                done(dve.tensor_tensor(a, e, wide(m), ALU.mult))
                for held, one, best in ((a, one1, first), (left, one2, second)):
                    done(dve.tensor_reduce(best, held, AX_X, ALU.max))
                    done(dve.tensor_tensor(c, held, wide(best), ALU.is_equal))
                    done(dve.tensor_tensor(c, c, ranks, ALU.mult))
                    done(dve.tensor_reduce(m, c, AX_X, ALU.max))
                    dve.tensor_tensor(one, ranks, wide(m), ALU.is_equal).then_inc(s["routed"], 1)
                    if one is one1:
                        dve.wait_ge(s["routed"], 2 * i + 1)
                        done(dve.scalar_tensor_tensor(left, one1, -2.0, a, ALU.mult, ALU.add))
                        gate_up(i, 0)
                done(dve.tensor_tensor(first, first, second, ALU.add))
                done(dve.reciprocal(first, first))
                dve.wait_ge(s["routed"], 2 * i + 2)
                done(dve.tensor_tensor(one1, one1, one2, ALU.add))
                assert at[0] == R_STEPS
                dve.tensor_tensor(a, a, one1, ALU.mult).then_inc(s["routed2"], 1)
                dve.wait_ge(s["routed2"], 3 * i + 1)
                dve.tensor_tensor(a, a, wide(first), ALU.mult).then_inc(s["routed2"], 1)
                dve.wait_ge(s["routed2"], 3 * i + 2)
                dve.tensor_copy(wsplit[:, :, 0:EXPERTS].bitcast(F32R), a).then_inc(s["routed2"], 1)
                dve.wait_ge(s["routed2"], 3 * i + 3)
                dve.tensor_tensor(wsplit[:, :, EXPERTS:], a, wsplit[:, :, 0:EXPERTS], ALU.subtract).then_inc(s["w"], 1)

            def add(i):
                dve.wait_ge(s["d_done"], FT * i + FT)
                for t in range(GT):
                    xt = entry.tile(i - FIRST, t)
                    dve.tensor_tensor(xt, xt, y_ps[t].unsqueeze(1), ALU.add).then_inc(s["y_added"], 1)

            def main(i, last=False):
                gate_up(i, 1)
                weigh(i, 0)
                for j in range(2, FT):
                    weigh(i, j - 1)
                    gate_up(i, j)
                    if j == 2 and not last:
                        entry.take_stats(dve, i + 1, i + 1 - FIRST)
                    if j == 4 and not last:
                        entry.norm(dve, i + 1, i + 1 - FIRST)
                weigh(i, FT - 1)
                if not last:
                    for t in range(GT):
                        low(i + 1, t)
                add(i)
                if not last:
                    route(i + 1)

            for t in range(2):
                low(FIRST, t)
            dve.wait_ge(s["consts"], CONSTS + 4)
            take_lo(dve, r_lo[:, :, 0:EXPERTS], r_raw[:, :, :], r_hi[:, :, 0:EXPERTS]).then_inc(s["consts"], 1)
            for t in range(2, GT):
                low(FIRST, t)
            route(FIRST)
            main(FIRST)
            with dve.Fori(FIRST + 1, LAST) as i:
                main(i)
            main(LAST, last=True)

        @block.tensor
        def _(pe):
            def turn(i, t, first=False):
                pe.wait_ge(s["xn"], GT * i + t + 1)
                if t == 0 and not first:
                    pe.wait_ge(s["hid"], FT * i)
                if t >= 2:
                    pe.wait_ge(s["lo"], GT * i + t - 1)
                for k in range(KT):
                    ins = pe.transpose(turn_ps[t % 2][:, k * P:(k + 1) * P], xn[:, t, k * P:(k + 1) * P], ident[:, :])
                ins.then_inc(s["turned"], 1)

            def router(i):
                pe.wait_ge(s["lo"], GT * i + GT)
                for k in range(KT):
                    ins = product3(pe, m_ps, r_hi[:, k, :], r_lo[:, k, :], xT_hi[:, k, :], xT_lo[:, k, :], k == 0, k == KT - 1)
                ins.then_inc(s["logitsT"], 1)

            def turn_logits(i):
                pe.wait_ge(s["lgT"], i + 1)
                for t in range(GT):
                    ins = pe.transpose(w_ps[:, t * P:(t + 1) * P], lgT[:, t * P:(t + 1) * P], ident[:, :])
                ins.then_inc(s["logits"], 1)

            def hidden(out, part, j, name):
                pe.wait_ge(s["w_lo"], W_BEFORE + PARTS * j + part + 1)
                for k in range(KT):
                    cols = slice(k * P, (k + 1) * P)
                    ins = product3(pe, out, w_hi[:, j, part, cols], w_lo[:, j, part, cols], xT_hi[:, k, :], xT_lo[:, k, :],
                                   k == 0, k == KT - 1)
                ins.then_inc(s[name], 1)

            def down(i, j):
                pe.wait_ge(s["w_lo"], W_BEFORE + PARTS * j + D_PART + 1)
                pe.wait_ge(s["h_lo"], FT * i + j + 1)
                for t in range(GT):
                    cols = slice(t * P, (t + 1) * P)
                    ins = product3(pe, y_ps[t], hT_hi[:, j % 3, cols], hT_lo[:, j % 3, cols],
                                   w_hi[:, j, D_PART, :], w_lo[:, j, D_PART, :], j == 0, j == FT - 1)
                ins.then_inc(s["d_done"], 1)

            def expert_weights(i):
                pe.wait_ge(s["w"], i + 1)
                for t in range(GT):
                    ins = pe.transpose(m_ps[0:2 * EXPERTS, t * P:(t + 1) * P], wsplit[:, t, :], ident[:, :])
                ins.then_inc(s["wT_turned"], 1)

            def spread_weights(i, j):
                if j:
                    pe.wait_ge(s["hid"], FT * i + j)
                else:
                    pe.wait_ge(s["wT"], i + 1)
                pe.matmul(w_ps, spread[:, j * P:(j + 1) * P], wT[:, :], start=True, stop=True).then_inc(s["w_done"], 1)

            def main(i, last=False):
                for j in range(FT):
                    if j:
                        pe.wait_ge(s["silu"], FT * i + j)
                    hidden(g_ps, G_PART, j, "g_done")
                    if j == 0:
                        turn_logits(i)
                    if j >= 2:
                        spread_weights(i, j - 1)
                    if j:
                        pe.wait_ge(s["up"], FT * i + j)
                    hidden(u_ps, U_PART, j, "u_done")
                    if j == 1:
                        expert_weights(i)
                        spread_weights(i, 0)
                    if j >= 2:
                        if j == FT - 1:
                            spread_weights(i, j)
                        down(i, j - 2)
                if last:
                    down(i, FT - 2)
                    down(i, FT - 1)
                else:
                    turn(i + 1, 0)
                    turn(i + 1, 1)
                    down(i, FT - 2)
                    turn(i + 1, 2)
                    turn(i + 1, 3)
                    down(i, FT - 1)
                    router(i + 1)

            for t in range(GT):
                turn(FIRST, t, True)
            pe.wait_ge(s["consts"], CONSTS + 5)
            router(FIRST)
            with pe.Fori(FIRST, LAST) as i:
                main(i)
            main(LAST, last=True)



def attention_b_stage(nc, psum, sem, x_sb, ident, wsum, entry, dram):
    with ExitStack() as ctx:
        def pair(name):
            return [ctx.enter_context(nc.sbuf_tensor(f"b_{name}_{part}", [P, KT, LEN], F32R)) for part in ("hi", "lo")]

        xT, dT = pair("xT"), pair("dT")
        raw = ctx.enter_context(nc.sbuf_tensor("b_raw", [P, RING_B, DM], F32))
        piece_in = [sem(f"b_piece_in{k}") for k in range(RING_B)]
        direct_part(nc, psum, sem, x_sb, ident, xT, dT, wsum, raw, piece_in, entry, dram)
        head_part(nc, psum, sem, x_sb, xT, dT, wsum, raw, piece_in, entry, dram)


def load_piece_b(sp, raw, piece_in, dram, g, p):
    src = dram["wB"][ds(g * PIECES_B + p, 1), :, :].rearrange("a p n -> (a p) n")
    sp.dma_start(raw[:, p % RING_B, :], src).then_inc(piece_in[p % RING_B], 16)


def direct_part(nc, psum, sem, x_sb, ident, xT, dT, wsum, raw, piece_in, entry, dram):
    with ExitStack() as ctx:
        def buf(name, shape, dt=F32):
            return ctx.enter_context(nc.sbuf_tensor("m_" + name, shape, dt))

        wv = buf("wv", [P, 2, DM])
        zero16 = buf("zero16", [P, DM], BF16)
        M_hi = buf("M_hi", [P, KT, DM], F32R)
        M_lo = buf("M_lo", [P, KT, DM], F32R)
        x0T = buf("x0T_hi", [P, KT, LEN], F32R), buf("x0T_lo", [P, KT, LEN], F32R)
        stats = buf("stats", [P, TILES, 6])
        mv = buf("mv", [P, TILES, 2])
        std = buf("std", [P, TILES])
        rstd = buf("rstd", [P, TILES])
        xn = entry.raw
        names = "set M_done M_made M_hi M_lo stats var std rstd xn dx turned hi lo y_done y_added"
        s = {n: sem("m_" + n) for n in names.split()}
        w_in = [sem(f"m_w_in{k}") for k in range(2)]
        XN0, XN1, DX = range(3)
        turn_ps = [psum[:, b, :].rearrange("p (k n) -> p k n", k=KT) for b in range(3)]
        M_ps = [psum[:, 4 + c, :] for c in range(KT)]
        Y_BANKS = 4
        into = (x0T, xT, dT)

        block = ctx.enter_context(nc.Block())

        @block.sync
        def _(sp):
            def load(g, k):
                sp.dma_start(wv[:, k, :], dram["wv"][:, ds(g, 1), :]).then_inc(w_in[k], 16)

            for k in range(2):
                load(k, k)
            for p in range(RING_B):
                load_piece_b(sp, raw, piece_in, dram, 0, p)
            with sp.Fori(1, KVB // 2) as j:
                for k in range(2):
                    sp.wait_ge(s["M_done"], 2 * j + k - 1)
                    load(2 * j + k, k)

        def pairs(eng, unit):
            unit(0, 0, True)
            unit(1, 1, True)
            with eng.Fori(1, ST // 2) as j:
                unit(2 * j, 0, False)
                unit(2 * j + 1, 1, False)

        @block.gpsimd
        def _(pool):
            pool.memset(zero16[:, :], 0.0).then_inc(s["set"], 1)

            def diff(t, k, first):
                pool.wait_ge(s["xn"], 2 * t + 2)
                pool.tensor_tensor(xn[:, k, DX, :], xn[:, k, XN0, :], xn[:, k, XN1, :], ALU.subtract).then_inc(s["dx"], 1)

            pairs(pool, diff)

        @block.scalar
        def _(act):
            act.wait_ge(s["var"], TILES)
            act.activation(std[:, :], mv[:, :, 1], ACT.Sqrt, bias=entry.eps[:, 0:1]).then_inc(s["std"], 1)

            def high(t, k, first):
                for a in range(3):
                    act.wait_ge(s["turned"], 3 * t + a + 1)
                    take_hi(act, into[a][0][:, :, ds(t * P, P)], turn_ps[a]).then_inc(s["hi"], 1)

            pairs(act, high)
            act.wait_ge(s["M_made"], 1)
            for c in range(KT):
                take_hi(act, M_hi[:, c, :], M_ps[c]).then_inc(s["M_hi"], 1)

        @block.vector
        def _(dve):
            for t in range(TILES):
                dve.bn_stats(stats[:, t, :], x_sb[:, t, :]).then_inc(s["stats"], 1)
            dve.wait_ge(s["stats"], TILES)
            for t in range(TILES):
                dve.bn_aggr(mv[:, t, :], stats[:, t, :]).then_inc(s["var"], 1)
            dve.wait_ge(s["std"], 1)
            dve.reciprocal(rstd[:, :], std[:, :]).then_inc(s["rstd"], 1)
            dve.wait_ge(s["rstd"], 1)

            def norm(t, k, first):
                if not first:
                    dve.wait_ge(s["turned"], 3 * t - 3)
                for a in range(2):
                    at = t + ST * a
                    dve.tensor_scalar(xn[:, k, a, :], x_sb[:, ds(at, 1), :], mv[:, ds(at, 1), 0:1].squeeze(1),
                                      rstd[:, ds(at, 1)], ALU.subtract, ALU.mult).then_inc(s["xn"], 1)

            def low(t):
                for a in range(3):
                    dve.wait_ge(s["hi"], 3 * t + a + 1)
                    cols = ds(t * P, P)
                    take_lo(dve, into[a][1][:, :, cols], turn_ps[a], into[a][0][:, :, cols]).then_inc(s["lo"], 1)

            norm(0, 0, True)
            norm(1, 1, True)
            low(0)
            with dve.Fori(1, ST // 2) as j:
                norm(2 * j, 0, False)
                low(2 * j - 1)
                norm(2 * j + 1, 1, False)
                low(2 * j)
            low(ST - 1)
            for c in range(KT):
                dve.wait_ge(s["M_hi"], c + 1)
                take_lo(dve, M_lo[:, c, :], M_ps[c], M_hi[:, c, :]).then_inc(s["M_lo"], 1)
            for t in range(TILES):
                dve.wait_ge(s["y_done"], t + 1)
                dve.tensor_tensor(x_sb[:, t, :], x_sb[:, t, :], psum[:, t % Y_BANKS, :], ALU.add).then_inc(s["y_added"], 1)

        @block.tensor
        def _(pe):
            pe.wait_ge(s["set"], 1)
            for c in range(KT):
                pe.matmul(M_ps[c], zero16[:, 0:P], zero16[:, :], start=True, stop=False, skip_group_check=True)

            def unit(t, k, first):
                pe.wait_ge(w_in[k], 16 * t + 16 if first and t == 0 else 8 * t + 16 - 8 * k)
                for c in range(KT):
                    ins = pe.matmul(M_ps[c], wv[:, k, c * P:(c + 1) * P], wsum[:, ds(t, 1), :].squeeze(1),
                                    start=False, stop=False, skip_group_check=True)
                ins.then_inc(s["M_done"], 1)
                for a in range(3):
                    if a == DX:
                        pe.wait_ge(s["dx"], t + 1)
                    else:
                        pe.wait_ge(s["xn"], 2 * t + a + 1)
                    if not (first and k == 0):
                        pe.wait_ge(s["lo"], 3 * t - 2 + a)
                    for c in range(KT):
                        ins = pe.transpose(turn_ps[a][:, c, :], xn[:, k, a, c * P:(c + 1) * P], ident[:, :])
                    ins.then_inc(s["turned"], 1)

            pairs(pe, unit)
            for c in range(KT):
                ins = pe.matmul(M_ps[c], zero16[:, 0:P], zero16[:, :], start=False, stop=True, skip_group_check=True)
            ins.then_inc(s["M_made"], 1)
            pe.wait_ge(s["lo"], 3 * ST)
            for t in range(TILES):
                hi, lo = (x0T, xT)[t // ST]
                cols = slice((t % ST) * P, (t % ST + 1) * P)
                if t >= Y_BANKS:
                    pe.wait_ge(s["y_added"], t - Y_BANKS + 1)
                for c in range(KT):
                    if t == 0:
                        pe.wait_ge(s["M_lo"], c + 1)
                    ins = product3(pe, psum[:, t % Y_BANKS, :], hi[:, c, cols], lo[:, c, cols], M_hi[:, c, :], M_lo[:, c, :],
                                   c == 0, c == KT - 1)
                ins.then_inc(s["y_done"], 1)


def head_part(nc, psum, sem, x_sb, xT, dT, spare, raw, piece_in, entry, dram):
    xT_hi, xT_lo = xT
    dT_hi, dT_lo = dT
    with ExitStack() as ctx:
        def buf(name, shape, dt=F32):
            return ctx.enter_context(nc.sbuf_tensor("h_" + name, shape, dt))

        PIECES, RING = PIECES_B, RING_B
        K_AT, V_AT, Q_AT, O_AT = 0, 1, 2, 2 + QPG
        CHUNKS = LEN // GROUP
        UNITS = CHUNKS * QPG
        w_hi = buf("w_hi", [P, PIECES, DM], F32R)
        w_lo = buf("w_lo", [P, PIECES, DM], F32R)
        ones = buf("ones", [P, P], F32R)
        dk, dv = spare[:, 0:CHUNKS, :], spare[:, CHUNKS:2 * CHUNKS, :]
        prod, prob, pv = (spare[:, 2 * CHUNKS + n, :] for n in range(3))
        ones_f, cell = spare[:, 2 * CHUNKS + 3, 0:P], spare[:, 2 * CHUNKS + 3, P:P + 2]
        prod_hi = buf("prod_hi", [P, 2, GROUP], F32R)
        prod_lo = buf("prod_lo", [P, 2, GROUP], F32R)
        pv_hi = buf("pv_hi", [P, QPG, GROUP], F32R)
        pv_lo = buf("pv_lo", [P, QPG, GROUP], F32R)
        names = "set ones w_hi w_lo dk_done dk dv_done dv q_done prod prod_hi prod_lo summed prob pv pv_hi pv_lo y_done y_added"
        s = {n: sem("h_" + n) for n in names.split()}

        block = ctx.enter_context(nc.Block())

        @block.sync
        def _(sp):
            def load(g, first):
                for p in range(RING if first else 0, PIECES):
                    sp.wait_ge(s["w_lo"], PIECES * g + p - RING + 1)
                    load_piece_b(sp, raw, piece_in, dram, g, p)

            load(0, True)
            with sp.Fori(1, KVB) as g:
                load(g, False)
            for j in range(2):
                entry.load_piece(sp, 1, j)

        @block.gpsimd
        def _(pool):
            pool.memset(ones_f[:, :], 1.0).then_inc(s["set"], 1)
            pool.memset(cell[:, :], 0.0).then_inc(s["set"], 1)
            pool.wait_ge(s["set"], 2)

            def split(g, first):
                for p in range(PIECES):
                    if not first:
                        if p == K_AT:
                            pool.wait_ge(s["dk_done"], CHUNKS * g)
                        elif p == V_AT:
                            pool.wait_ge(s["dv_done"], CHUNKS * g)
                        elif p < O_AT:
                            pool.wait_ge(s["q_done"], UNITS * g - QPG + (p - Q_AT) + 1)
                        else:
                            pool.wait_ge(s["y_done"], UNITS * g)
                    pool.wait_ge(piece_in[p % RING], 16 * (2 * g + p // RING + 1))
                    pool_copy(pool, w_hi[:, p, :], raw[:, p % RING, :], cell[:, 0:1].broadcast_to([P, DM])).then_inc(s["w_hi"], 1)
                    pool.wait_ge(s["w_hi"], PIECES * g + p + 1)
                    take_lo(pool, w_lo[:, p, :], raw[:, p % RING, :], w_hi[:, p, :]).then_inc(s["w_lo"], 1)

            split(0, True)
            with pool.Fori(1, KVB) as g:
                split(g, False)

        @block.scalar
        def _(act):
            act.wait_ge(s["set"], 2)
            act.activation(ones[:, :], ones_f[:, :], ACT.Copy).then_inc(s["ones"], 1)
            entry.root(act, GROUPS)

            def prob_of(u, k, r):
                act.wait_ge(s["summed"], u + 1)
                act.activation(prob[:, :], psum[:, 4 + k, :], ACT.Sigmoid, scale=SCALE_B).then_inc(s["prob"], 1)
                act.wait_ge(s["pv"], u + 1)
                take_hi(act, pv_hi[:, r, :], pv[:, :]).then_inc(s["pv_hi"], 1)

            def prod_of(u, k):
                act.wait_ge(s["prod"], u + 1)
                take_hi(act, prod_hi[:, k, :], prod[:, :]).then_inc(s["prod_hi"], 1)

            def group(g, first):
                for c in range(CHUNKS):
                    for r in range(QPG):
                        u = UNITS * g + QPG * c + r
                        prev = not (first and c == 0 and r == 0)
                        if r == 0:
                            act.wait_ge(s["dk_done"], CHUNKS * g + c + 1)
                            act.activation(dk[:, c, :], psum[:, 0, :], ACT.Copy).then_inc(s["dk"], 1)
                            if prev:
                                prob_of(u - 1, 1, QPG - 1)
                            act.wait_ge(s["dv_done"], CHUNKS * g + c + 1)
                            act.activation(dv[:, c, :], psum[:, 1, :], ACT.Copy).then_inc(s["dv"], 1)
                            prod_of(u, 0)
                        else:
                            prod_of(u, r % 2)
                            prob_of(u - 1, (r - 1) % 2, r - 1)

            group(0, True)
            with act.Fori(1, KVB) as g:
                group(g, False)
            prob_of(UNITS * KVB - 1, 1, QPG - 1)

        @block.vector
        def _(dve):
            def pv_of(u, c, k, r, begin=False):
                if not begin:
                    dve.wait_ge(s["pv_lo"], u)
                dve.wait_ge(s["prob"], u + 1)
                dve.tensor_tensor(pv[:, :], prob[:, :], dv[:, c, :], ALU.mult).then_inc(s["pv"], 1)
                dve.wait_ge(s["pv_hi"], u + 1)
                take_lo(dve, pv_lo[:, r, :], pv[:, :], pv_hi[:, r, :]).then_inc(s["pv_lo"], 1)

            def prod_of(u, c, k, begin=False):
                if not begin:
                    dve.wait_ge(s["prod_lo"], u)
                dve.wait_ge(s["q_done"], u + 1)
                dve.tensor_tensor(prod[:, :], psum[:, 2 + k, :], dk[:, c, :], ALU.mult).then_inc(s["prod"], 1)
                dve.wait_ge(s["prod_hi"], u + 1)
                take_lo(dve, prod_lo[:, k, :], prod[:, :], prod_hi[:, k, :]).then_inc(s["prod_lo"], 1)

            def add(chunk, c):
                for t in range(GT):
                    dve.wait_ge(s["y_done"], GT * chunk + t + 1)
                    xt = x_sb[:, ST + GT * c + t, :]
                    dve.tensor_tensor(xt, xt, psum[:, 6 + t % 2, :], ALU.add).then_inc(s["y_added"], 1)

            def group(g, first):
                for c in range(CHUNKS):
                    for r in range(QPG):
                        u = UNITS * g + QPG * c + r
                        prev = not (first and c == 0)
                        if r == 0:
                            if prev:
                                pv_of(u - 1, 1 - c, 1, QPG - 1)
                            dve.wait_ge(s["dk"], CHUNKS * g + c + 1)
                            prod_of(u, c, 0, not prev)
                        else:
                            prod_of(u, c, r % 2)
                            if r == 1 and prev:
                                add(CHUNKS * g + c - 1, 1 - c)
                            if r == 1:
                                dve.wait_ge(s["dv"], CHUNKS * g + c + 1)
                            pv_of(u - 1, c, (r - 1) % 2, r - 1, not prev and r == 1)

            entry.take_stats(dve, GROUPS, 0)
            entry.norm(dve, GROUPS, 0)
            group(0, True)
            with dve.Fori(1, KVB) as g:
                group(g, False)
            pv_of(UNITS * KVB - 1, CHUNKS - 1, 1, QPG - 1)
            add(CHUNKS * KVB - 1, CHUNKS - 1)

        @block.tensor
        def _(pe):
            pe.wait_ge(s["ones"], 1)

            def product(g, p, out, m_hi, m_lo, c, name):
                pe.wait_ge(s["w_lo"], PIECES * g + p + 1)
                cols = slice(c * GROUP, (c + 1) * GROUP)
                for k in range(KT):
                    w = slice(k * P, (k + 1) * P)
                    ins = product3(pe, out, w_hi[:, p, w], w_lo[:, p, w], m_hi[:, k, cols], m_lo[:, k, cols], k == 0, k == KT - 1)
                ins.then_inc(s[name], 1)

            def score(u, k, may_wait=True):
                pe.wait_ge(s["prod_lo"], u + 1)
                if may_wait:
                    pe.wait_ge(s["prob"], u - 1)
                pe.matmul(psum[:, 4 + k, :], ones[:, :], prod_hi[:, k, :], start=True, stop=False)
                pe.matmul(psum[:, 4 + k, :], ones[:, :], prod_lo[:, k, :], start=False, stop=True).then_inc(s["summed"], 1)

            def project(chunk, first):
                pe.wait_ge(s["pv_lo"], QPG * chunk + QPG)
                for t in range(GT):
                    if not (first and t < 2):
                        pe.wait_ge(s["y_added"], GT * chunk + t - 1)
                    cols = slice(t * P, (t + 1) * P)
                    for r in range(QPG):
                        ins = product3(pe, psum[:, 6 + t % 2, :], pv_hi[:, r, cols], pv_lo[:, r, cols],
                                       w_hi[:, O_AT + r, :], w_lo[:, O_AT + r, :], r == 0, r == QPG - 1)
                    ins.then_inc(s["y_done"], 1)

            def group(g, first):
                for c in range(CHUNKS):
                    for r in range(QPG):
                        u = UNITS * g + QPG * c + r
                        begin = first and c == 0
                        if r == 0:
                            if not begin:
                                pe.wait_ge(s["dk"], CHUNKS * g + c)
                            product(g, K_AT, psum[:, 0, :], dT_hi, dT_lo, c, "dk_done")
                            if not begin:
                                score(u - 1, 1)
                                pe.wait_ge(s["dv"], CHUNKS * g + c)
                            product(g, V_AT, psum[:, 1, :], dT_hi, dT_lo, c, "dv_done")
                        if not (begin and r < 2):
                            pe.wait_ge(s["prod"], u - 1)
                        product(g, Q_AT + r, psum[:, 2 + r % 2, :], xT_hi, xT_lo, c, "q_done")
                        if r == 1 and not begin:
                            if c == 1:
                                pe.wait_ge(s["w_lo"], PIECES * g + PIECES)
                            project(CHUNKS * g + c - 1, first and c == 1)
                        if r:
                            score(u - 1, (r - 1) % 2, not (begin and r < 3))

            group(0, True)
            with pe.Fori(1, KVB) as g:
                group(g, False)
            score(UNITS * KVB - 1, 1)
            project(CHUNKS * KVB - 1, False)



def layer(nc, dram, out):
    with ExitStack() as ctx:
        x_sb = ctx.enter_context(nc.sbuf_tensor("x_sb", [P, TILES, DM], F32))
        ident = ctx.enter_context(nc.sbuf_tensor("ident", [P, P], F32))
        psum = ctx.enter_context(nc.psum_tensor("psum", [P, 8, 512], F32))

        def sem(name):
            return ctx.enter_context(nc.semaphore(name))

        def lasting(name, shape, dt=F32):
            return ctx.enter_context(nc.sbuf_tensor(name, shape, dt))

        entry = FfnEntry(lasting, sem, x_sb, dram)
        with ExitStack() as first:
            def buf(name, shape, dt=F32):
                return first.enter_context(nc.sbuf_tensor(name, shape, dt))

            qkvT = buf("qkvT", [P, 3, TOK])
            pre = {
                "wqk": buf("p_wqk", [P, 2, HA * EA]), "wvT": buf("p_wvT", [P, HEAD_TILES, W]),
                "wo": buf("p_wo", [P, HEAD_TILES, W]), "bq": buf("p_bq", [P, HEAD_TILES]),
                "bk": buf("p_bk", [P, HEAD_TILES]), "bv": buf("p_bv", [P, HEAD_TILES]), "bo": buf("p_bo", [P, 1]),
                "proj_w": buf("p_proj_w", [P, DM]), "proj_b": buf("p_proj_b", [P, DM]), "mask": buf("p_mask", [P, HPS * P]),
            }
            loads = [(pre[n][:], dram[n]) for n in pre]
            pre["loads"], pre["total"], pre["in"] = loads, 16 * len(loads), sem("p_in")
            conv_stage(nc, psum, sem, x_sb, ident, qkvT, pre, entry, dram)
            attention_a_stage(nc, psum, sem, x_sb, ident, qkvT, pre, entry, dram)
        with nc.sbuf_tensor("wsum", [P, KVB, DM], F32) as wsum:
            ffn_stage(nc, psum, entry, ident, dram, 0, None, wsum)
            attention_b_stage(nc, psum, sem, x_sb, ident, wsum, entry, dram)
        ffn_stage(nc, psum, entry, ident, dram, 1, out, None)



def kernel(L0_attn_a_inputs, L0_attn_a_conv_w, L0_attn_a_conv_b, L0_attn_a_wq, L0_attn_a_bq, L0_attn_a_wk, L0_attn_a_bk,
           L0_attn_a_wv, L0_attn_a_bv, L0_attn_a_wo, L0_attn_a_bo, L0_attn_a_proj_w, L0_attn_a_proj_b,
           L0_attn_b_weight_qkv, L0_attn_b_weight_proj, L0_ffn_gate_w, L0_ffn_u, L0_ffn_g, L0_ffn_d):
    import numpy as np
    import concourse.bacc as bacc
    from concourse.bass_utils import run_bass_kernel_spmd

    def rows(a, n):
        return a.reshape(n, P, -1).transpose(1, 0, 2)

    def column(a):
        return a.reshape(-1, P).T

    def inner(a):
        return np.asarray(a).reshape(FT, P, KT, P).transpose(3, 0, 2, 1).reshape(P, FT, KT * P)

    wqkv = np.asarray(L0_attn_b_weight_qkv)
    wqkv_g = wqkv.reshape(KVB, ROWS_G // EB, EB, KT, P)
    pieces = wqkv_g.transpose(0, 1, 4, 3, 2).reshape(KVB, ROWS_G // EB, P, KT * EB)
    wprojT = np.asarray(L0_attn_b_weight_proj).T.reshape(KVB, QPG, EB, DM)
    order = [QPG, QPG + 1, *range(QPG)]
    spread = np.zeros((2 * EXPERTS, FF), np.float32)
    for e in range(EXPERTS):
        spread[e, e * INTER:(e + 1) * INTER] = 1
        spread[EXPERTS + e, e * INTER:(e + 1) * INTER] = 1
    arrays = {
        "x": np.asarray(L0_attn_a_inputs).reshape(TOK, DM),
        "conv_w": rows(np.asarray(L0_attn_a_conv_w).reshape(TAPS * DM, 3 * W), TAPS * KT),
        "conv_b": column(np.asarray(L0_attn_a_conv_b)),
        "wqk": np.stack([np.asarray(L0_attn_a_wq).reshape(W, HA * EA), np.asarray(L0_attn_a_wk).reshape(W, HA * EA)], 1),
        "wvT": rows(np.asarray(L0_attn_a_wv).reshape(W, HA * EA).T, HEAD_TILES),
        "wo": rows(np.asarray(L0_attn_a_wo).reshape(HA * EA, W), HEAD_TILES),
        "bq": column(np.asarray(L0_attn_a_bq)), "bk": column(np.asarray(L0_attn_a_bk)),
        "bv": column(np.asarray(L0_attn_a_bv)), "bo": column(np.asarray(L0_attn_a_bo)),
        "proj_w": np.asarray(L0_attn_a_proj_w),
        "proj_b": np.broadcast_to(np.asarray(L0_attn_a_proj_b)[None, :], (P, DM)),
        "mask": np.tile(np.triu(np.full((P, P), MASKED, np.float32), 1), (1, HPS)),
        "ident": np.eye(P, dtype=np.float32),
        "gate_w": rows(np.asarray(L0_ffn_gate_w).T, KT),
        "ffn_w": np.stack([inner(L0_ffn_g), inner(L0_ffn_u), rows(np.asarray(L0_ffn_d).T, FT)], 2),
        "spread": spread,
        "rank": np.tile(np.arange(EXPERTS, 0, -1, dtype=np.float32), (P, 1)),
        "wB": np.concatenate([pieces[:, order], wprojT], 1).reshape(KVB * (2 + 2 * QPG), P, DM),
        "wv": wqkv.reshape(KVB, QPG + 2, EB, DM)[:, QPG + 1].transpose(1, 0, 2),
        "wpT": wprojT.transpose(0, 2, 1, 3),
    }
    nc = bacc.Bacc("TRN2", target_bir_lowering=False, num_devices=1)
    dram, sent = {}, {}
    for name, a in arrays.items():
        a = np.ascontiguousarray(a)
        sent["in_" + name] = a
        dram[name] = nc.dram_tensor("in_" + name, a.shape, mybir.dt.from_np(a.dtype), kind="ExternalInput").ap()
    out = nc.dram_tensor("out", (TOK, DM), F32, kind="ExternalOutput").ap()
    layer(nc, dram, out)
    r = run_bass_kernel_spmd(nc, [sent], core_ids=[0])
    return r.results[0]["out"].reshape(SEQS, LEN, DM)
```

```python
from contextlib import ExitStack

import concourse.bass as bass
from concourse import mybir

F32 = mybir.dt.float32
F32R = mybir.dt.float32r
BF16 = mybir.dt.bfloat16
ACT = mybir.ActivationFunctionType
ALU = mybir.AluOpType
AX_X = mybir.AxisListType.X

P = 128
SEQS, LEN, DM = 2, 1024, 512
TOK = SEQS * LEN
TILES = TOK // P
KT = DM // P
GROUP = 512
GT = GROUP // P
GROUPS = TOK // GROUP
ST = LEN // P
EPS = 1e-5

TAPS, W, HA, EA = 3, 128, 16, 64
PADDED = LEN + TAPS - 1
HEAD_TILES = HA * EA // P
HPS = 4
BLOCK_STEPS = HA // HPS
STEPS = GT * BLOCK_STEPS
SCALE_A = EA ** -0.5
MASKED = -1e30

HB, KVB, EB = 32, 8, 128
QPG = HB // KVB
ROWS_G = (QPG + 2) * EB
SCALE_B = EB ** -0.5
PIECES_B = 2 + 2 * QPG
RING_B = PIECES_B // 2

EXPERTS, INTER = 16, 56
FF = EXPERTS * INTER
FT = FF // P

ds = bass.ds


def heads_of(step):
    return [8 * (step // 2) + 2 * m + step % 2 for m in range(HPS)]


def product3(pe, out, w_hi, w_lo, x_hi, x_lo, first, last):
    pe.matmul(out, w_hi, x_hi, start=first, stop=False)
    pe.matmul(out, w_hi, x_lo, start=False, stop=False)
    return pe.matmul(out, w_lo, x_hi, start=False, stop=last)


def wait_on_cell(eng, cell, sem, value):
    eng.wait_ge(sem, value)
    eng.tensor_tensor(cell[:, 0:1], cell[:, 1:2], cell[:, 1:2], ALU.mult)


def pool_copy(pool, out, src, zero):
    return pool.tensor_tensor(out, src, zero, ALU.add)


def take_hi(act, hi, src):
    return act.activation(hi, src, ACT.Copy)


def take_lo(eng, lo, src, hi):
    return eng.tensor_tensor(lo, src, hi.bitcast(F32), ALU.subtract)



def conv_stage(nc, psum, sem, x_sb, ident, qkvT, prefetch, entry, dram):
    with ExitStack() as ctx:
        def buf(name, shape, dt=F32):
            return ctx.enter_context(nc.sbuf_tensor("c_" + name, shape, dt))

        xnT_hi = buf("xnT_hi", [P, KT, SEQS * PADDED], F32R)
        xnT_lo = buf("xnT_lo", [P, KT, SEQS * PADDED], F32R)
        both = entry.raw[:, :, :, :].rearrange("p a b n -> p a (b n)")
        w_raw = [both[:, t, 0:KT * 3 * W].rearrange("p (k w) -> p k w", k=KT) for t in range(2)]
        w_raw.append(buf("w_raw", [P, KT, 3 * W])[:, :, :])
        warm = buf("warm", [P, 1])
        w_hi = buf("w_hi", [P, TAPS * KT, 3 * W], F32R)
        w_lo = buf("w_lo", [P, TAPS * KT, 3 * W], F32R)
        conv_b = buf("b", [P, 3])
        eps = buf("eps", [P, 1])
        stats = buf("stats", [P, TILES, 6])
        mv = buf("mv", [P, TILES, 2])
        std = buf("std", [P, TILES])
        rstd = buf("rstd", [P, TILES])
        xn = entry.xn

        names = ("warmed b_in eps_set pads w_hi_ready w_lo_ready stats var std rstd xn turned hi lo conv_done conv_out")
        s = {n: sem("c_" + n) for n in names.split()}
        x_in = {g: sem(f"c_x_in{g}") for g in range(1, GROUPS)}
        first_in = [sem(f"c_first_in{t}") for t in range(GT)]
        w_in = [sem(f"c_w_in{t}") for t in range(TAPS)]
        TURNS = 4
        turn_ps = [psum[:, b, :].rearrange("p (k n) -> p k n", k=KT) for b in (0, 1, 4, 5)]
        conv_ps = [psum[:, b, :] for b in (2, 3)]

        units = [(n, half, o) for n in range(SEQS) for half in range(2) for o in range(3)]
        tiles_for = {(0, 0): GT + 1, (0, 1): ST, (1, 0): ST + GT + 1, (1, 1): TILES}
        AHEAD, AFTER = GT + 1, 2

        def at(t):
            return (t // ST) * PADDED + 1 + (t % ST) * P

        block = ctx.enter_context(nc.Block())

        @block.sync
        def _(sp):
            xv = dram["x"].rearrange("(t p) n -> p t n", p=P)

            def load_x(g):
                sp.dma_start(x_sb[:, GT * g:GT * (g + 1), :], xv[:, GT * g:GT * (g + 1), :]).then_inc(x_in[g], 16)

            def load_w(t):
                sp.dma_start(w_raw[t], dram["conv_w"][:, KT * t:KT * (t + 1), :]).then_inc(w_in[t], 16)

            for t in range(GT):
                sp.dma_start(x_sb[:, t:t + 1, :], xv[:, t:t + 1, :]).then_inc(first_in[t], 16)
            sp.dma_start(ident[:, :], dram["ident"]).then_inc(s["b_in"], 16)
            sp.dma_start(conv_b[:, :], dram["conv_b"]).then_inc(s["b_in"], 16)
            load_w(0)
            load_x(1)
            load_w(1)
            load_w(2)
            load_x(2)
            load_x(3)
            entry.load_router(sp)
            for dst, src in prefetch["loads"]:
                sp.dma_start(dst, src).then_inc(prefetch["in"], 16)

        @block.gpsimd
        def _(pool):
            pool.memset(eps[:, :], EPS).then_inc(s["eps_set"], 1)
            entry.clear(pool)
            for t in (xnT_hi, xnT_lo):
                ends = t[:, :, :].bitcast(F32).rearrange("p k (s n) -> p k s n", s=SEQS)
                for col in (0, PADDED - 1):
                    pool.memset(ends[:, :, :, col:col + 1], 0.0).then_inc(s["pads"], 1)
            for t in range(TAPS):
                pool.wait_ge(s["w_hi_ready"], t + 1)
                for k in range(KT) if t == 0 else [slice(0, KT)]:
                    part = slice(k, k + 1) if t == 0 else k
                    taps = slice(KT * t + part.start, KT * t + part.stop)
                    take_lo(pool, w_lo[:, taps, :], w_raw[t][:, part, :], w_hi[:, taps, :]).then_inc(s["w_lo_ready"], 1)

        @block.vector
        def _(dve):
            def stats_of(g):
                if g:
                    dve.wait_ge(x_in[g], 16)
                for t in range(GT * g, GT * g + GT):
                    if g == 0:
                        dve.wait_ge(first_in[t], 16)
                    dve.bn_stats(stats[:, t, :], x_sb[:, t, :]).then_inc(s["stats"], 1)
                dve.wait_ge(s["stats"], GT * g + GT)
                for t in range(GT * g, GT * g + GT):
                    dve.bn_aggr(mv[:, t, :], stats[:, t, :]).then_inc(s["var"], 1)

            def norm(t):
                if t % GT == 0:
                    g = t // GT
                    cols = slice(t, t + GT)
                    dve.wait_ge(s["std"], g + 1)
                    dve.reciprocal(rstd[:, cols], std[:, cols]).then_inc(s["rstd"], 1)
                    dve.wait_ge(s["rstd"], g + 1)
                if t >= TURNS:
                    dve.wait_ge(s["turned"], t - TURNS + 1)
                dve.tensor_scalar(xn[:, t % TURNS, :], x_sb[:, t, :], mv[:, t, 0:1], rstd[:, t:t + 1],
                                  ALU.subtract, ALU.mult).then_inc(s["xn"], 1)

            stats_of(0)
            for t in range(GT):
                norm(t)

            def low(t):
                dve.wait_ge(s["hi"], t + 1)
                cols = slice(at(t), at(t) + P)
                take_lo(dve, xnT_lo[:, :, cols], turn_ps[t % TURNS], xnT_hi[:, :, cols]).then_inc(s["lo"], 1)

            for t in range(GT):
                low(t)
            stats_of(1)
            norm(GT)
            for t in range(GT, TILES):
                if t % GT == 1 and t // GT + 1 < GROUPS:
                    stats_of(t // GT + 1)
                if t + 1 < TILES:
                    norm(t + 1)
                low(t)

        @block.scalar
        def _(act):
            act.wait_ge(s["eps_set"], 1)
            act.activation(warm[:, :], eps[:, :], ACT.Sqrt).then_inc(s["warmed"], 1)
            act.wait_ge(s["b_in"], 32)

            def root(g):
                act.wait_ge(s["var"], GT * g + GT)
                cols = slice(GT * g, GT * g + GT)
                act.activation(std[:, cols], mv[:, cols, 1], ACT.Sqrt, bias=eps[:, 0:1]).then_inc(s["std"], 1)

            def high(t):
                act.wait_ge(s["turned"], t + 1)
                take_hi(act, xnT_hi[:, :, at(t):at(t) + P], turn_ps[t % TURNS]).then_inc(s["hi"], 1)
                if t > GT and t % GT == 1 and t // GT + 1 < GROUPS:
                    root(t // GT + 1)

            def high_w(t):
                act.wait_ge(w_in[t], 16)
                take_hi(act, w_hi[:, KT * t:KT * (t + 1), :], w_raw[t]).then_inc(s["w_hi_ready"], 1)

            root(0)
            high_w(0)
            high(0)
            high(1)
            high(2)
            high(3)
            high_w(1)
            root(1)
            high_w(2)
            high(GT)
            for c, (n, half, o) in enumerate(units):
                act.wait_ge(s["conv_done"], c + 1)
                first = n * LEN + half * GROUP
                act.activation(qkvT[:, o, first:first + GROUP], conv_ps[c % 2], ACT.Identity,
                               bias=conv_b[:, o:o + 1]).then_inc(s["conv_out"], 1)
                for t in range(AHEAD + AFTER * c, min(AHEAD + AFTER * (c + 1), TILES)):
                    high(t)

        @block.tensor
        def _(pe):
            pe.wait_ge(s["b_in"], 32)
            pe.wait_ge(s["pads"], 4)

            def turn(t):
                pe.wait_ge(s["xn"], t + 1)
                if t >= TURNS:
                    pe.wait_ge(s["lo"], t - TURNS + 1)
                for k in range(KT):
                    ins = pe.transpose(turn_ps[t % TURNS][:, k, :], xn[:, t % TURNS, k * P:(k + 1) * P], ident[:, :])
                ins.then_inc(s["turned"], 1)

            for t in range(GT):
                turn(t)
            for c, (n, half, o) in enumerate(units):
                pe.wait_ge(s["lo"], GT if c == 0 else tiles_for[n, half])
                if c >= 2:
                    pe.wait_ge(s["conv_out"], c - 1)
                for tap in range(TAPS):
                    if c == 0:
                        if tap == TAPS - 2:
                            turn(GT)
                        if tap == TAPS - 1:
                            pe.wait_ge(s["lo"], GT + 1)
                        if tap:
                            pe.wait_ge(s["w_lo_ready"], KT + tap)
                    for k in range(KT):
                        if c == 0 and tap == 0:
                            pe.wait_ge(s["w_lo_ready"], k + 1)
                        first = n * PADDED + half * GROUP + tap
                        kk, cols = tap * KT + k, slice(o * W, (o + 1) * W)
                        ins = product3(pe, conv_ps[c % 2], w_hi[:, kk, cols], w_lo[:, kk, cols],
                                       xnT_hi[:, k, first:first + GROUP], xnT_lo[:, k, first:first + GROUP],
                                       kk == 0, kk == TAPS * KT - 1)
                ins.then_inc(s["conv_done"], 1)
                for t in range(AHEAD + AFTER * c, min(AHEAD + AFTER * (c + 1), TILES)):
                    turn(t)



def attention_a_stage(nc, psum, sem, x_sb, ident, qkvT, pre, entry, dram):
    with ExitStack() as ctx:
        def buf(name, shape, dt=F32):
            return ctx.enter_context(nc.sbuf_tensor("a_" + name, shape, dt))

        wqk_hi = buf("wqk_hi", [P, 2, HA * EA], F32R)
        wqk_lo = buf("wqk_lo", [P, 2, HA * EA], F32R)
        vo_hi = buf("vo_hi", [P, BLOCK_STEPS, HPS * W], F32R)
        vo_lo = buf("vo_lo", [P, BLOCK_STEPS, HPS * W], F32R)
        obias = buf("obias", [P, 1])
        s_hi = buf("split_hi", [P, 3, GROUP], F32R)
        s_lo = buf("split_lo", [P, 3, GROUP], F32R)
        qh = buf("qh", [P, HEAD_TILES, GROUP])
        kh = buf("kh", [P, HEAD_TILES, GROUP])
        vo = buf("vo", [P, 4, HPS * W])
        mx = buf("mx", [P, 2, HPS])
        shift = buf("shift", [P, 2, HPS])
        prob = buf("prob", [P, 4, HPS, P])
        sums = buf("sums", [P, 2, HPS])
        rsum = buf("rsum", [P, 2, HPS])
        probT = buf("probT", [P, 2, HPS * P])
        oT = buf("oT", [P, 2, P])

        names = ("w_hi w_lo vo_made vo_hi vo_lo bias_made bias_ready hi lo vhi vlo projected qh kh scored "
                 "masked max_ready shift exp_done rsum_ready normed vo_done vo_ready probs_turned probT_ready "
                 "pv_done oT_ready y_done y_added pb_added")
        s = {n: sem("a_" + n) for n in names.split()}

        block = ctx.enter_context(nc.Block())

        @block.sync
        def _(sp):
            for j in range(2):
                entry.load_piece(sp, 0, j)

        score_ps = [psum[:, b, :] for b in (0, 1)]
        vo_ps = [psum[:, b, :] for b in (2, 3)]
        turn_ps = [psum[:, b, :] for b in (4, 5)]
        out_ps = [psum[:, b, :] for b in (6, 7)]
        N_PROJ = 2 * HEAD_TILES
        TURN = 3
        PV, Y = TURN + 1, TURN + 3
        DRAIN = Y
        proj_at = {STEPS + d: range(4 * d, 4 * d + 4) for d in range(N_PROJ // 4)}

        def proj_ps(n):
            return (vo_ps, score_ps)[n % 2][n // 2 % 2]

        def is_block_end(u):
            return u % BLOCK_STEPS == BLOCK_STEPS - 1

        @block.scalar
        def _(act):
            act.wait_ge(pre["in"], pre["total"])
            def split(i, o):
                src = qkvT[:, o, ds(i * GROUP, GROUP)]
                take_hi(act, s_hi[:, o, :], src).then_inc(s["vhi"] if o == 2 else s["hi"], 1)

            for w in range(2):
                take_hi(act, wqk_hi[:, w, :], pre["wqk"][:, w, :]).then_inc(s["w_hi"], 1)
            split(0, 0)
            split(0, 1)
            act.wait_ge(s["bias_made"], 1)
            act.activation(obias[:, :], psum[:, 0, 0:1], ACT.Identity, bias=pre["bo"][:, 0:1]).then_inc(s["bias_ready"], 1)

            def q_out(i, n):
                t = n // 2
                act.wait_ge(s["projected"], N_PROJ * i + n + 1)
                act.activation(qh[:, t, :], proj_ps(n), ACT.Identity, bias=pre["bq"][:, t:t + 1]).then_inc(s["qh"], 1)

            def group(i, last):
                for u in range(STEPS + DRAIN):
                    if u < STEPS:
                        act.wait_ge(s["vo_done"], STEPS * i + u + 1)
                        if u >= 4:
                            act.wait_ge(s["pv_done"], STEPS * i + u - 3)
                        act.activation(vo[:, u % 4, :], vo_ps[u % 2], ACT.Copy).then_inc(s["vo_ready"], 1)
                    if u in proj_at and not last:
                        q_out(i + 1, proj_at[u][0])
                    if TURN <= u < STEPS + TURN:
                        t = u - TURN
                        act.wait_ge(s["probs_turned"], STEPS * i + t + 1)
                        if t >= 2:
                            act.wait_ge(s["pv_done"], STEPS * i + t - 1)
                        act.activation(probT[:, t % 2, :], turn_ps[t % 2], ACT.Copy).then_inc(s["probT_ready"], 1)
                    if u < STEPS:
                        act.wait_ge(s["shift"], STEPS * i + u + 1)
                        if u >= 2:
                            act.wait_ge(s["rsum_ready"], STEPS * i + u - 1)
                        for m in range(HPS):
                            p = prob[:, u % 4, m, :]
                            act.activation(p, p, ACT.Exp, bias=shift[:, u % 2, m:m + 1], scale=SCALE_A,
                                           accum_out=sums[:, u % 2, m:m + 1]).then_inc(s["exp_done"], 1)
                    if u == STEPS - 3 and not last:
                        split(i + 1, 0)
                        split(i + 1, 1)
                    if u == STEPS + 1 and not last:
                        act.wait_ge(s["vo_done"], STEPS * i + STEPS)
                        split(i + 1, 2)
                    if u >= PV and is_block_end(u - PV):
                        b = (u - PV) // BLOCK_STEPS
                        act.wait_ge(s["pv_done"], STEPS * i + u - PV + 1)
                        if b >= 2:
                            act.wait_ge(s["y_done"], GT * i + b - 1)
                        act.activation(oT[:, b % 2, :], out_ps[b % 2][:, 0:P], ACT.Identity,
                                       bias=obias[:, 0:1]).then_inc(s["oT_ready"], 1)
                    if u in proj_at and not last:
                        q_out(i + 1, proj_at[u][2])
                    if u == GT + 2 and last:
                        entry.root(act, 0)

            for n in range(0, N_PROJ, 2):
                q_out(0, n)
                if n < 2 * BLOCK_STEPS:
                    c = n // 2
                    act.wait_ge(s["vo_made"], c + 1)
                    take_hi(act, vo_hi[:, c, :], psum[:, GT + c, :]).then_inc(s["vo_hi"], 1)
            split(0, 2)
            with act.Fori(0, GROUPS - 1) as i:
                group(i, False)
            group(GROUPS - 1, True)

        @block.vector
        def _(dve):
            dve.wait_ge(pre["in"], pre["total"])
            for w in range(2):
                dve.wait_ge(s["w_hi"], w + 1)
                take_lo(dve, wqk_lo[:, w, :], pre["wqk"][:, w, :], wqk_hi[:, w, :]).then_inc(s["w_lo"], 1)
            def split(i, o):
                dve.wait_ge(s["vhi"] if o == 2 else s["hi"], i + 1 if o == 2 else 2 * i + o + 1)
                src = qkvT[:, o, ds(i * GROUP, GROUP)]
                take_lo(dve, s_lo[:, o, :], src, s_hi[:, o, :]).then_inc(s["vlo"] if o == 2 else s["lo"], 1)

            mask = pre["mask"][:, :].rearrange("p (h k) -> p h k", h=HPS)

            def k_out(i, n):
                t = n // 2
                dve.wait_ge(s["projected"], N_PROJ * i + n + 1)
                dve.tensor_scalar(kh[:, t, :], proj_ps(n), pre["bk"][:, t:t + 1], None, ALU.add).then_inc(s["kh"], 1)

            def group(i, last):
                for u in range(STEPS + DRAIN + 1):
                    if u < STEPS:
                        scores = score_ps[u % 2].rearrange("p (h k) -> p h k", h=HPS)
                        if u >= 4:
                            dve.wait_ge(s["probs_turned"], STEPS * i + u - 3)
                        dve.wait_ge(s["scored"], STEPS * i + u + 1)
                        dve.tensor_tensor(prob[:, u % 4, :, :], scores, mask, ALU.add).then_inc(s["masked"], 1)
                        dve.wait_ge(s["masked"], STEPS * i + u + 1)
                        dve.tensor_reduce(mx[:, u % 2, :], prob[:, u % 4, :, :], AX_X, ALU.max).then_inc(s["max_ready"], 1)
                    if 1 <= u < STEPS + 1:
                        t = u - 1
                        dve.wait_ge(s["exp_done"], HPS * (STEPS * i + t + 1))
                        if t >= 2:
                            dve.wait_ge(s["normed"], STEPS * i + t - 1)
                        dve.reciprocal(rsum[:, t % 2, :], sums[:, t % 2, :]).then_inc(s["rsum_ready"], 1)
                    if u < STEPS:
                        dve.wait_ge(s["max_ready"], STEPS * i + u + 1)
                        dve.tensor_scalar(shift[:, u % 2, :], mx[:, u % 2, :], -SCALE_A, None, ALU.mult).then_inc(s["shift"], 1)
                    if u == STEPS - 2 and not last:
                        split(i + 1, 0)
                        split(i + 1, 1)
                    if u == STEPS + 1 and not last:
                        split(i + 1, 2)
                    if u in proj_at and not last:
                        k_out(i + 1, proj_at[u][1])
                        k_out(i + 1, proj_at[u][3])
                    if last:
                        if 1 <= u <= GT:
                            entry.stat(dve, 0, u - 1)
                        elif u == GT + 1:
                            entry.moments(dve, 0)
                        elif u == GT + 3:
                            entry.reciprocal(dve, 0)
                        elif GT + 4 <= u < 2 * GT + 4:
                            entry.norm(dve, 0, u - GT - 4)
                    if u > Y and is_block_end(u - Y - 1):
                        b = (u - Y - 1) // BLOCK_STEPS
                        dve.wait_ge(s["y_done"], GT * i + b + 1)
                        if b == 0:
                            dve.wait_ge(s["pb_added"], i + 1)
                        xt = x_sb[:, ds(GT * i + b, 1), :]
                        dve.tensor_tensor(xt, xt, out_ps[b % 2].unsqueeze(1), ALU.add).then_inc(s["y_added"], 1)
                dve.wait_ge(s["y_added"], GT * i + GT)

            split(0, 0)
            split(0, 1)
            for n in range(1, N_PROJ, 2):
                k_out(0, n)
                if n < 2 * BLOCK_STEPS:
                    c = n // 2
                    dve.wait_ge(s["vo_hi"], c + 1)
                    take_lo(dve, vo_lo[:, c, :], psum[:, GT + c, :], vo_hi[:, c, :]).then_inc(s["vo_lo"], 1)
            split(0, 2)
            with dve.Fori(0, GROUPS - 1) as i:
                group(i, False)
            group(GROUPS - 1, True)

        @block.gpsimd
        def _(pool):
            pool.wait_ge(pre["in"], pre["total"])
            with pool.Fori(0, GROUPS) as i:
                xg = x_sb[:, ds(GT * i, GT), :]
                pool.tensor_tensor(xg, xg, pre["proj_b"][:, :].unsqueeze(1).broadcast_to([P, GT, DM]), ALU.add).then_inc(s["pb_added"], 1)
                for u in range(STEPS):
                    pool.wait_ge(s["rsum_ready"], STEPS * i + u + 1)
                    p = prob[:, u % 4, :, :]
                    pool.tensor_tensor(p, p, rsum[:, u % 2, :].unsqueeze(2).broadcast_to([P, HPS, P]), ALU.mult).then_inc(s["normed"], 1)

        @block.tensor
        def _(pe):
            pe.wait_ge(pre["in"], pre["total"])
            for c in range(BLOCK_STEPS):
                for m, h in enumerate(heads_of(c)):
                    rows = slice(EA * (h % 2), EA * (h % 2) + EA)
                    ins = pe.matmul(psum[:, GT + c, m * W:(m + 1) * W], pre["wvT"][rows, h // 2, :], pre["wo"][rows, h // 2, :],
                                    start=True, stop=True)
                ins.then_inc(s["vo_made"], 1)
            for t in range(HEAD_TILES):
                ins = pe.matmul(psum[:, 0, 0:1], pre["wo"][:, t, :], pre["bv"][:, t:t + 1],
                                start=t == 0, stop=t == HEAD_TILES - 1)
            ins.then_inc(s["bias_made"], 1)
            pe.wait_ge(s["bias_ready"], 1)
            pe.wait_ge(s["w_lo"], 2)

            def project(i, n):
                w, t = n % 2, n // 2
                if n < 2:
                    pe.wait_ge(s["lo"], 2 * i + w + 1)
                elif n >= 4:
                    pe.wait_ge(s["kh"] if w else s["qh"], HEAD_TILES * i + t - 1)
                cols = slice(t * P, (t + 1) * P)
                product3(pe, proj_ps(n), wqk_hi[:, w, cols], wqk_lo[:, w, cols], s_hi[:, w, :], s_lo[:, w, :],
                         True, True).then_inc(s["projected"], 1)

            def group(i, last):
                for u in range(STEPS + DRAIN + 1):
                    if u < STEPS:
                        b, c = u // BLOCK_STEPS, u % BLOCK_STEPS
                        cols = slice(b * P, (b + 1) * P)
                        if u == 0:
                            pe.wait_ge(s["qh"], HEAD_TILES * i + HEAD_TILES)
                            pe.wait_ge(s["kh"], HEAD_TILES * i + HEAD_TILES)
                            pe.wait_ge(s["vlo"], i + 1)
                        else:
                            if u >= 2:
                                pe.wait_ge(s["masked"], STEPS * i + u - 1)
                                pe.wait_ge(s["vo_ready"], STEPS * i + u - 1)
                        for m, h in enumerate(heads_of(c)):
                            rows = slice(EA * (h % 2), EA * (h % 2) + EA)
                            ins = pe.matmul(score_ps[u % 2][:, m * P:(m + 1) * P], qh[rows, h // 2, cols], kh[rows, h // 2, cols],
                                            start=True, stop=True)
                        ins.then_inc(s["scored"], 1)
                        product3(pe, vo_ps[u % 2], s_hi[:, 2, cols], s_lo[:, 2, cols], vo_hi[:, c, :], vo_lo[:, c, :],
                                 True, True).then_inc(s["vo_done"], 1)
                    if u in proj_at and not last:
                        if u == STEPS:
                            pe.wait_ge(s["vo_ready"], STEPS * i + STEPS - 1)
                            pe.wait_ge(s["masked"], STEPS * i + STEPS - 1)
                        project(i + 1, proj_at[u][0])
                        project(i + 1, proj_at[u][1])
                    if TURN <= u < STEPS + TURN:
                        t = u - TURN
                        pe.wait_ge(s["normed"], STEPS * i + t + 1)
                        if t >= 2:
                            pe.wait_ge(s["probT_ready"], STEPS * i + t - 1)
                        for m in range(HPS):
                            ins = pe.transpose(turn_ps[t % 2][:, m * P:(m + 1) * P], prob[:, t % 4, m, :], ident[:, :])
                        ins.then_inc(s["probs_turned"], 1)
                    if PV <= u < STEPS + PV:
                        t = u - PV
                        b, c = t // BLOCK_STEPS, t % BLOCK_STEPS
                        pe.wait_ge(s["probT_ready"], STEPS * i + t + 1)
                        pe.wait_ge(s["vo_ready"], STEPS * i + t + 1)
                        if c == 0 and b >= 2:
                            pe.wait_ge(s["y_added"], GT * i + b - 1)
                        for m in range(HPS):
                            ins = pe.matmul(out_ps[b % 2][:, 0:P], vo[:, t % 4, m * W:(m + 1) * W], probT[:, t % 2, m * P:(m + 1) * P],
                                            start=c == 0 and m == 0, stop=c == BLOCK_STEPS - 1 and m == HPS - 1)
                        ins.then_inc(s["pv_done"], 1)
                    if u in proj_at and not last:
                        if u == STEPS:
                            pe.wait_ge(s["vo_ready"], STEPS * i + STEPS)
                            pe.wait_ge(s["masked"], STEPS * i + STEPS)
                        project(i + 1, proj_at[u][2])
                        project(i + 1, proj_at[u][3])
                    if u >= Y and is_block_end(u - Y):
                        b = (u - Y) // BLOCK_STEPS
                        pe.wait_ge(s["oT_ready"], GT * i + b + 1)
                        pe.matmul(out_ps[b % 2], oT[:, b % 2, :], pre["proj_w"][:, :], start=True, stop=True).then_inc(s["y_done"], 1)

            for n in range(N_PROJ):
                project(0, n)
            pe.wait_ge(s["vo_lo"], BLOCK_STEPS)
            with pe.Fori(0, GROUPS - 1) as i:
                group(i, False)
            group(GROUPS - 1, True)



class FfnEntry:

    SEMS = ("set r_in c_in consts eps stats var std rstd xn turned hi lo logitsT lgT logits routed routed2 shifted exped rstep "
            "w wT_turned wT g_done u_done w_done silu up hid h_hi h_lo d_done y_added out w_hi w_lo piece_in0 piece_in1 "
            "wp_in wsum1 wsum").split()
    USES = (FT + 1) // 2, FT // 2

    def __init__(self, buf, sem, x_sb, dram):
        self.s = {n: sem("f_" + n) for n in self.SEMS}
        self.x_sb, self.dram = x_sb, dram
        self.raw = buf("f_raw", [P, 2, 3, DM])
        self.eps = buf("f_eps", [P, 1])
        self.cell = buf("f_cell", [P, 2])
        self.stats = buf("f_stats", [P, GT, 6])
        self.mv = buf("f_mv", [P, GT, 2])
        self.std = buf("f_std", [P, GT])
        self.rstd = buf("f_rstd", [P, GT])
        self.xn = buf("f_xn", [P, GT, DM])
        self.r_raw = buf("f_r_raw", [P, KT, EXPERTS])
        self.rank = buf("f_rank", [P, EXPERTS])

    def tile(self, i, t):
        return self.x_sb[:, ds(GT * i + t, 1), :]

    def landed(self, run, j):
        return self.s[f"piece_in{j % 2}"], 16 * (self.USES[j % 2] * run + j // 2 + 1)

    def load_piece(self, sp, run, j):
        sp.dma_start(self.raw[:, j % 2, :, :], self.dram["ffn_w"][:, j, :, :]).then_inc(self.landed(run, j)[0], 16)

    def load_router(self, sp):
        sp.dma_start(self.r_raw[:, :, :], self.dram["gate_w"]).then_inc(self.s["r_in"], 16)
        sp.dma_start(self.rank[:, :], self.dram["rank"]).then_inc(self.s["r_in"], 16)

    def clear(self, pool):
        pool.memset(self.eps[:, :], EPS).then_inc(self.s["set"], 1)
        pool.memset(self.cell[:, :], 0.0).then_inc(self.s["set"], 1)

    def stat(self, dve, at, t):
        dve.bn_stats(self.stats[:, t, :], self.tile(at, t)).then_inc(self.s["stats"], 1)

    def moments(self, dve, i):
        wait_on_cell(dve, self.cell, self.s["stats"], GT * i + GT)
        for t in range(GT):
            dve.bn_aggr(self.mv[:, t, :], self.stats[:, t, :]).then_inc(self.s["var"], 1)

    def root(self, act, i):
        act.wait_ge(self.s["var"], GT * i + GT)
        act.activation(self.std[:, :], self.mv[:, :, 1], ACT.Sqrt, bias=self.eps[:, 0:1]).then_inc(self.s["std"], 1)

    def reciprocal(self, dve, i):
        dve.wait_ge(self.s["std"], i + 1)
        dve.reciprocal(self.rstd[:, :], self.std[:, :]).then_inc(self.s["rstd"], 1)
        dve.wait_ge(self.s["rstd"], i + 1)

    def norm(self, dve, at, t):
        dve.tensor_scalar(self.xn[:, t, :], self.tile(at, t), self.mv[:, t, 0:1], self.rstd[:, t:t + 1],
                          ALU.subtract, ALU.mult).then_inc(self.s["xn"], 1)


def ffn_stage(nc, psum, entry, ident, dram, run, out, wsum, wv_in):
    s, raw, xn, x_sb = entry.s, entry.raw, entry.xn, entry.x_sb
    FIRST, LAST = GROUPS * run, GROUPS * run + GROUPS - 1
    PARTS = 3
    W_BEFORE = PARTS * FT * run
    D_BEFORE = (GT - 1) * run
    G_PART, U_PART, D_PART = range(PARTS)
    with ExitStack() as ctx:
        def buf(name, shape, dt=F32):
            return ctx.enter_context(nc.sbuf_tensor(f"f{run}_{name}", shape, dt))

        w_hi = buf("w_hi", [P, FT, PARTS, DM], F32R)
        w_lo = buf("w_lo", [P, FT, PARTS, DM], F32R)
        r_raw, rank = entry.r_raw, entry.rank
        r_hi = buf("r_hi", [P, KT, P], F32R)
        r_lo = buf("r_lo", [P, KT, P], F32R)
        spread = buf("spread", [2 * EXPERTS, FF], F32R)
        xT_hi = buf("xT_hi", [P, KT, GROUP], F32R)
        xT_lo = buf("xT_lo", [P, KT, GROUP], F32R)
        lgT = buf("lgT", [P, GROUP])
        row = buf("row", [P, 3, GT])
        lg = buf("lg", [P, 6, GT, EXPERTS])
        wsplit = buf("wsplit", [P, GT, 2 * EXPERTS])
        wT = buf("wT", [2 * EXPERTS, GROUP], F32R)
        silu = buf("silu", [P, 2, GROUP])
        up = buf("up", [P, 2, GROUP])
        hid = buf("hid", [P, 2, GROUP])
        hT_hi = buf("hT_hi", [P, 3, GROUP], F32R)
        hT_lo = buf("hT_lo", [P, 3, GROUP], F32R)
        spread_raw = silu[0:2 * EXPERTS, :, :].rearrange("e a n -> e (a n)")[:, 0:FF]

        y_ps = [psum[:, b, :] for b in range(GT)]
        g_ps, u_ps, w_ps, m_ps = (psum[:, GT + b, :] for b in range(4))
        turn_ps = [m_ps, g_ps, u_ps, w_ps]

        block = ctx.enter_context(nc.Block())

        @block.sync
        def _(sp):
            sp.dma_start(spread_raw, dram["spread"]).then_inc(s["c_in"], 16)
            for j in range(2, FT):
                sp.wait_ge(s["w_lo"], W_BEFORE + PARTS * (j - 1))
                entry.load_piece(sp, run, j)
            if wsum is not None:
                sp.wait_ge(s["w_lo"], W_BEFORE + PARTS * FT)
                wp = raw[:, :, :, :].rearrange("p a b n -> p (a b) n")[:, 0:QPG, :]
                sp.dma_start(wp, dram["wpT"][0, :, :, :]).then_inc(s["wp_in"], 16)
                with sp.Fori(1, KVB) as g:
                    sp.wait_ge(s["wsum"], g)
                    sp.dma_start(wp, dram["wpT"][ds(g, 1), :, :, :].rearrange("a p q n -> (a p) q n")).then_inc(s["wp_in"], 16)
                sp.wait_ge(s["turned"], GT * (LAST + 1))
                for k in range(2):
                    load_wv(sp, xn, wv_in, dram, k, k)
            if out is not None:
                out_tiles = out.rearrange("(t p) n -> p t n", p=P)
                with sp.Fori(FIRST, LAST) as i:
                    sp.wait_ge(s["y_added"], GT * i + GT)
                    group = ds(GT * (i - FIRST), GT)
                    sp.dma_start(out_tiles[:, group, :], x_sb[:, group, :]).then_inc(s["out"], 16)
                for t in range(GT):
                    sp.wait_ge(s["y_added"], GT * LAST + t + 1)
                    one = slice(TILES - GT + t, TILES - GT + t + 1)
                    sp.dma_start(out_tiles[:, one, :], x_sb[:, one, :]).then_inc(s["out"], 16)
                sp.wait_ge(s["out"], 16 * (GROUPS - 1 + GT))

        @block.gpsimd
        def _(pool):
            def low_w(j):
                for part in range(PARTS):
                    pool.wait_ge(s["w_hi"], W_BEFORE + PARTS * j + part + 1)
                    take_lo(pool, w_lo[:, j, part, :], raw[:, j % 2, part, :], w_hi[:, j, part, :]).then_inc(s["w_lo"], 1)

            def head_sum(g):
                wp = raw[:, :, :, :].rearrange("p a b n -> p (a b) n")
                pool.wait_ge(s["wp_in"], 16 * g + 16)
                pool.tensor_tensor(wp[:, 0:2, :], wp[:, 0:2, :], wp[:, 2:4, :], ALU.add).then_inc(s["wsum1"], 1)
                pool.wait_ge(s["wsum1"], g + 1)
                pool.tensor_tensor(wsum[:, ds(g, 1), :], wp[:, 0:1, :], wp[:, 1:2, :], ALU.add).then_inc(s["wsum"], 1)

            def group(i, first=False, sums=()):
                for j in range(FT):
                    if first and j + 2 < FT:
                        low_w(j + 2)
                    pool.wait_ge(s["h_hi"], FT * i + j + 1)
                    take_lo(pool, hT_lo[:, j % 3, :], hid[:, j % 2, :], hT_hi[:, j % 3, :]).then_inc(s["h_lo"], 1)
                    if wsum is not None and j in sums:
                        head_sum(3 * (i - 1) + sums.index(j))

            for r in (r_hi, r_lo):
                pool.memset(r[:, :, :].bitcast(F32), 0.0).then_inc(s["consts"], 1)
            low_w(0)
            low_w(1)
            group(FIRST, first=True)
            with pool.Fori(FIRST + 1, LAST) as i:
                group(i, sums=(1, 3, 5))
            group(LAST, sums=(1, 3))

        CONSTS = 5 * run

        @block.scalar
        def _(act):
            def high_w(j):
                act.wait_ge(*entry.landed(run, j))
                for part in range(PARTS):
                    take_hi(act, w_hi[:, j, part, :], raw[:, j % 2, part, :]).then_inc(s["w_hi"], 1)

            def turn(i, t):
                act.wait_ge(s["turned"], GT * i + t + 1)
                take_hi(act, xT_hi[:, :, t * P:(t + 1) * P],
                        turn_ps[t].rearrange("p (k n) -> p k n", k=KT)).then_inc(s["hi"], 1)

            def route(i):
                act.wait_ge(s["logitsT"], i + 1)
                act.activation(lgT[:, :], m_ps, ACT.Copy).then_inc(s["lgT"], 1)
                act.wait_ge(s["shifted"], i + 1)
                act.activation(lg[:, 1, :, :], lg[:, 0, :, :], ACT.Exp).then_inc(s["exped"], 1)

            def gate(i, j):
                act.wait_ge(s["g_done"], FT * i + j + 1)
                if j >= 2:
                    act.wait_ge(s["up"], FT * i + j - 1)
                act.activation(silu[:, j % 2, :], g_ps, ACT.Silu).then_inc(s["silu"], 1)

            def high(i, j):
                act.wait_ge(s["hid"], FT * i + j + 1)
                if j >= 3:
                    act.wait_ge(s["d_done"], FT * i + D_BEFORE + j - 2)
                take_hi(act, hT_hi[:, j % 3, :], hid[:, j % 2, :]).then_inc(s["h_hi"], 1)

            def main(i, last=False, first=False):
                for j in range(FT + 1):
                    if j < FT:
                        gate(i, j)
                    if j == 1:
                        act.wait_ge(s["wT_turned"], i + 1)
                        act.activation(wT[:, :], m_ps[0:2 * EXPERTS, :], ACT.Copy).then_inc(s["wT"], 1)
                    if j >= 1:
                        high(i, j - 1)
                    if first and j + 2 < FT:
                        high_w(j + 2)
                    if j == 3 and not last:
                        entry.root(act, i + 1)
                if not last:
                    for t in range(GT):
                        turn(i + 1, t)
                    route(i + 1)

            for t in range(2):
                turn(FIRST, t)
            act.wait_ge(s["consts"], CONSTS + 2)
            act.wait_ge(s["r_in"], 32)
            take_hi(act, r_hi[:, :, 0:EXPERTS], r_raw[:, :, :]).then_inc(s["consts"], 1)
            for t in range(2, GT):
                turn(FIRST, t)
            high_w(0)
            act.wait_ge(s["c_in"], 16 * (run + 1))
            act.wait_ge(s["consts"], CONSTS + 4)
            act.activation(spread[:, :], spread_raw, ACT.Copy).then_inc(s["consts"], 1)
            high_w(1)
            route(FIRST)
            main(FIRST, first=True)
            with act.Fori(FIRST + 1, LAST) as i:
                main(i)
            main(LAST, last=True)

        @block.vector
        def _(dve):
            def low(i, t):
                dve.wait_ge(s["hi"], GT * i + t + 1)
                cols = slice(t * P, (t + 1) * P)
                take_lo(dve, xT_lo[:, :, cols], turn_ps[t].rearrange("p (k n) -> p k n", k=KT),
                        xT_hi[:, :, cols]).then_inc(s["lo"], 1)

            def gate_up(i, j):
                dve.wait_ge(s["silu"], FT * i + j + 1)
                dve.wait_ge(s["u_done"], FT * i + j + 1)
                dve.tensor_tensor(up[:, j % 2, :], silu[:, j % 2, :], u_ps, ALU.mult).then_inc(s["up"], 1)

            def weigh(i, j):
                dve.wait_ge(s["w_done"], FT * i + j + 1)
                if j >= 2:
                    dve.wait_ge(s["h_lo"], FT * i + j - 1)
                dve.wait_ge(s["up"], FT * i + j + 1)
                dve.tensor_tensor(hid[:, j % 2, :], up[:, j % 2, :], w_ps, ALU.mult).then_inc(s["hid"], 1)

            R_STEPS = 16

            def route(i):
                at = [0]

                def done(ins):
                    at[0] += 1
                    ins.then_inc(s["rstep"], 1)
                    dve.wait_ge(s["rstep"], R_STEPS * i + at[0])

                def wide(r):
                    return r.unsqueeze(2).broadcast_to([P, GT, EXPERTS])

                ranks = rank[:, :].unsqueeze(1).broadcast_to([P, GT, EXPERTS])
                logits = w_ps.rearrange("p (t e) -> p t e", t=GT)[:, :, 0:EXPERTS]
                a, e, c, one1, one2, left = (lg[:, k, :, :] for k in range(6))
                m, first, second = (row[:, k, :] for k in range(3))
                dve.wait_ge(s["logits"], i + 1)
                done(dve.tensor_reduce(m, logits, AX_X, ALU.max))
                dve.tensor_tensor(a, logits, wide(m), ALU.subtract).then_inc(s["shifted"], 1)
                dve.wait_ge(s["exped"], i + 1)
                done(dve.tensor_reduce(m, e, AX_X, ALU.add))
                done(dve.reciprocal(m, m))
                done(dve.tensor_tensor(a, e, wide(m), ALU.mult))
                for held, one, best in ((a, one1, first), (left, one2, second)):
                    done(dve.tensor_reduce(best, held, AX_X, ALU.max))
                    done(dve.tensor_tensor(c, held, wide(best), ALU.is_equal))
                    done(dve.tensor_tensor(c, c, ranks, ALU.mult))
                    done(dve.tensor_reduce(m, c, AX_X, ALU.max))
                    dve.tensor_tensor(one, ranks, wide(m), ALU.is_equal).then_inc(s["routed"], 1)
                    if one is one1:
                        dve.wait_ge(s["routed"], 2 * i + 1)
                        done(dve.scalar_tensor_tensor(left, one1, -2.0, a, ALU.mult, ALU.add))
                done(dve.tensor_tensor(first, first, second, ALU.add))
                done(dve.reciprocal(first, first))
                dve.wait_ge(s["routed"], 2 * i + 2)
                done(dve.tensor_tensor(one1, one1, one2, ALU.add))
                assert at[0] == R_STEPS
                dve.tensor_tensor(a, a, one1, ALU.mult).then_inc(s["routed2"], 1)
                dve.wait_ge(s["routed2"], 3 * i + 1)
                dve.tensor_tensor(a, a, wide(first), ALU.mult).then_inc(s["routed2"], 1)
                dve.wait_ge(s["routed2"], 3 * i + 2)
                dve.tensor_copy(wsplit[:, :, 0:EXPERTS].bitcast(F32R), a).then_inc(s["routed2"], 1)
                dve.wait_ge(s["routed2"], 3 * i + 3)
                dve.tensor_tensor(wsplit[:, :, EXPERTS:], a, wsplit[:, :, 0:EXPERTS], ALU.subtract).then_inc(s["w"], 1)

            def add(i, by_tile=False):
                if not by_tile:
                    dve.wait_ge(s["d_done"], FT * i + FT + D_BEFORE)
                for t in range(GT):
                    if by_tile:
                        dve.wait_ge(s["d_done"], FT * i + FT + D_BEFORE + t)
                    xt = entry.tile(i - FIRST, t)
                    dve.tensor_tensor(xt, xt, y_ps[t].unsqueeze(1), ALU.add).then_inc(s["y_added"], 1)

            def main(i, last=False):
                gate_up(i, 1)
                weigh(i, 0)
                for j in range(2, FT):
                    weigh(i, j - 1)
                    gate_up(i, j)
                    if j == 2 and not last:
                        for t in range(GT):
                            entry.stat(dve, i + 1 - FIRST, t)
                        entry.moments(dve, i + 1)
                    if j == 4 and not last:
                        entry.reciprocal(dve, i + 1)
                        for t in range(GT):
                            entry.norm(dve, i + 1 - FIRST, t)
                weigh(i, FT - 1)
                if last:
                    add(i, True)
                else:
                    for t in range(GT):
                        low(i + 1, t)
                    route(i + 1)
                    gate_up(i + 1, 0)
                    add(i)

            for t in range(2):
                low(FIRST, t)
            dve.wait_ge(s["consts"], CONSTS + 3)
            take_lo(dve, r_lo[:, :, 0:EXPERTS], r_raw[:, :, :], r_hi[:, :, 0:EXPERTS]).then_inc(s["consts"], 1)
            for t in range(2, GT):
                low(FIRST, t)
            route(FIRST)
            gate_up(FIRST, 0)
            main(FIRST)
            with dve.Fori(FIRST + 1, LAST) as i:
                main(i)
            main(LAST, last=True)

        @block.tensor
        def _(pe):
            def turn(i, t, first=False):
                pe.wait_ge(s["xn"], GT * i + t + 1)
                if t and not first:
                    pe.wait_ge(s[("silu", "up", "hid")[t - 1]], FT * i)
                for k in range(KT):
                    ins = pe.transpose(turn_ps[t][:, k * P:(k + 1) * P], xn[:, t, k * P:(k + 1) * P], ident[:, :])
                ins.then_inc(s["turned"], 1)

            def router(i):
                pe.wait_ge(s["lo"], GT * i + GT)
                for k in range(KT):
                    ins = product3(pe, m_ps, r_hi[:, k, :], r_lo[:, k, :], xT_hi[:, k, :], xT_lo[:, k, :], k == 0, k == KT - 1)
                ins.then_inc(s["logitsT"], 1)

            def turn_logits(i):
                pe.wait_ge(s["lgT"], i + 1)
                for t in range(GT):
                    ins = pe.transpose(w_ps[:, t * P:(t + 1) * P], lgT[:, t * P:(t + 1) * P], ident[:, :])
                ins.then_inc(s["logits"], 1)

            def hidden(out, part, j, name):
                pe.wait_ge(s["w_lo"], W_BEFORE + PARTS * j + part + 1)
                for k in range(KT):
                    cols = slice(k * P, (k + 1) * P)
                    ins = product3(pe, out, w_hi[:, j, part, cols], w_lo[:, j, part, cols], xT_hi[:, k, :], xT_lo[:, k, :],
                                   k == 0, k == KT - 1)
                ins.then_inc(s[name], 1)

            def down(i, j, by_tile=False):
                pe.wait_ge(s["w_lo"], W_BEFORE + PARTS * j + D_PART + 1)
                pe.wait_ge(s["h_lo"], FT * i + j + 1)
                for t in range(GT):
                    cols = slice(t * P, (t + 1) * P)
                    ins = product3(pe, y_ps[t], hT_hi[:, j % 3, cols], hT_lo[:, j % 3, cols],
                                   w_hi[:, j, D_PART, :], w_lo[:, j, D_PART, :], j == 0, j == FT - 1)
                    if by_tile or t == GT - 1:
                        ins.then_inc(s["d_done"], 1)

            def expert_weights(i):
                pe.wait_ge(s["w"], i + 1)
                for t in range(GT):
                    ins = pe.transpose(m_ps[0:2 * EXPERTS, t * P:(t + 1) * P], wsplit[:, t, :], ident[:, :])
                ins.then_inc(s["wT_turned"], 1)

            def spread_weights(i, j):
                if j:
                    pe.wait_ge(s["hid"], FT * i + j)
                else:
                    pe.wait_ge(s["wT"], i + 1)
                    pe.wait_ge(s["consts"], CONSTS + 5)
                pe.matmul(w_ps, spread[:, j * P:(j + 1) * P], wT[:, :], start=True, stop=True).then_inc(s["w_done"], 1)

            def main(i, first=False, last=False):
                for j in range(FT):
                    if j:
                        pe.wait_ge(s["silu"], FT * i + j)
                    hidden(g_ps, G_PART, j, "g_done")
                    if first and j == 0:
                        turn_logits(i)
                    if j == 1:
                        expert_weights(i)
                    if j >= 2:
                        spread_weights(i, j - 1)
                    if j:
                        pe.wait_ge(s["up"], FT * i + j)
                    hidden(u_ps, U_PART, j, "u_done")
                    if j == 1:
                        spread_weights(i, 0)
                    if j >= 2:
                        if j == FT - 1:
                            spread_weights(i, j)
                        down(i, j - 2)
                if last:
                    down(i, FT - 2)
                    down(i, FT - 1, True)
                else:
                    for t in range(GT):
                        turn(i + 1, t)
                    down(i, FT - 2)
                    router(i + 1)
                    down(i, FT - 1)
                    turn_logits(i + 1)

            for t in range(GT):
                turn(FIRST, t, True)
            pe.wait_ge(s["consts"], CONSTS + 4)
            router(FIRST)
            main(FIRST, first=True)
            with pe.Fori(FIRST + 1, LAST) as i:
                main(i)
            main(LAST, last=True)



def attention_b_stage(nc, psum, sem, x_sb, ident, wsum, wv_in, entry, dram):
    with ExitStack() as ctx:
        def pair(name):
            return [ctx.enter_context(nc.sbuf_tensor(f"b_{name}_{part}", [P, KT, LEN], F32R)) for part in ("hi", "lo")]

        xT, dT = pair("xT"), pair("dT")
        raw = entry.raw[:, :, :, :].rearrange("p a b n -> p (a b) n")
        piece_in = [sem(f"b_piece_in{k}") for k in range(RING_B)]
        direct_part(nc, psum, sem, x_sb, ident, xT, dT, wsum, wv_in, raw, piece_in, entry, dram)
        head_part(nc, psum, sem, x_sb, ident, xT, dT, wsum, raw, piece_in, entry, dram)


def load_piece_b(sp, raw, piece_in, dram, g, p):
    src = dram["wB"][ds(g * PIECES_B + p, 1), :, :].rearrange("a p n -> (a p) n")
    sp.dma_start(raw[:, p % RING_B, :], src).then_inc(piece_in[p % RING_B], 16)


def load_wv(sp, wv, wv_in, dram, g, k):
    sp.dma_start(wv[:, k, :], dram["wv"][:, ds(g, 1), :]).then_inc(wv_in[k], 16)


def direct_part(nc, psum, sem, x_sb, ident, xT, dT, wsum, w_in, raw, piece_in, entry, dram):
    with ExitStack() as ctx:
        def buf(name, shape, dt=F32):
            return ctx.enter_context(nc.sbuf_tensor("m_" + name, shape, dt))

        zero16 = buf("zero16", [P, DM], BF16)
        M_hi = buf("M_hi", [P, KT, DM], F32R)
        M_lo = buf("M_lo", [P, KT, DM], F32R)
        x0T = buf("x0T_hi", [P, KT, LEN], F32R), buf("x0T_lo", [P, KT, LEN], F32R)
        stats = buf("stats", [P, TILES, 6])
        mv = buf("mv", [P, TILES, 2])
        std = buf("std", [P, TILES])
        rstd = buf("rstd", [P, TILES])
        xn = buf("xn", [P, 2, 3, DM])
        wv = entry.xn
        names = "set M_done M_made M_hi M_lo stats var std rstd xn dx turned hi lo y_done y_added"
        s = {n: sem("m_" + n) for n in names.split()}
        XN0, XN1, DX = range(3)
        turn_ps = [psum[:, b, :].rearrange("p (k n) -> p k n", k=KT) for b in range(3)]
        M_ps = [psum[:, 4 + c, :] for c in range(KT)]
        Y_BANKS = 4
        into = (x0T, xT, dT)

        block = ctx.enter_context(nc.Block())

        @block.sync
        def _(sp):
            for p in range(RING_B):
                load_piece_b(sp, raw, piece_in, dram, 0, p)
            with sp.Fori(1, KVB // 2) as j:
                for k in range(2):
                    sp.wait_ge(s["M_done"], 2 * j + k - 1)
                    load_wv(sp, wv, w_in, dram, 2 * j + k, k)

        def of_half(a, half):
            return a[:, :].rearrange("p (place h t) -> p place h t", place=SEQS, h=2)[:, :, half, :]

        def pairs(eng, unit):
            for t in range(4):
                unit(t, t % 2, t < 2)
            with eng.Fori(2, ST // 2) as j:
                unit(2 * j, 0, False)
                unit(2 * j + 1, 1, False)

        @block.gpsimd
        def _(pool):
            pool.memset(zero16[:, :], 0.0).then_inc(s["set"], 1)

            def diff(t, k, first):
                pool.wait_ge(s["xn"], 2 * t + 2)
                pool.tensor_tensor(xn[:, k, DX, :], xn[:, k, XN0, :], xn[:, k, XN1, :], ALU.subtract).then_inc(s["dx"], 1)

            pairs(pool, diff)

        @block.scalar
        def _(act):
            def root(half):
                act.wait_ge(s["var"], TILES // 2 * (half + 1))
                act.activation(of_half(std, half), of_half(mv[:, :, 1], half), ACT.Sqrt,
                               bias=entry.eps[:, 0:1]).then_inc(s["std"], 1)

            root(0)

            def high(t, k, first):
                for a in range(3):
                    act.wait_ge(s["turned"], 3 * t + a + 1)
                    take_hi(act, into[a][0][:, :, ds(t * P, P)], turn_ps[a]).then_inc(s["hi"], 1)
                if isinstance(t, int) and t == 2:
                    root(1)

            pairs(act, high)
            act.wait_ge(s["M_made"], 1)
            for c in range(KT):
                take_hi(act, M_hi[:, c, :], M_ps[c]).then_inc(s["M_hi"], 1)

        @block.vector
        def _(dve):
            def tiles_of(half, place):
                return [ST * place + ST // 2 * half + t for t in range(ST // 2)]

            def stats_of(half, place):
                for t in tiles_of(half, place):
                    dve.bn_stats(stats[:, t, :], x_sb[:, t, :]).then_inc(s["stats"], 1)

            def moments(half):
                dve.wait_ge(s["stats"], TILES // 2 * (half + 1))
                for place in range(SEQS):
                    for t in tiles_of(half, place):
                        dve.bn_aggr(mv[:, t, :], stats[:, t, :]).then_inc(s["var"], 1)

            def reciprocal(half):
                dve.wait_ge(s["std"], half + 1)
                dve.reciprocal(of_half(rstd, half), of_half(std, half)).then_inc(s["rstd"], 1)
                dve.wait_ge(s["rstd"], half + 1)

            for place in range(SEQS):
                stats_of(0, place)
            moments(0)
            reciprocal(0)

            def norm(t, k, first):
                if not first:
                    dve.wait_ge(s["turned"], 3 * t - 3)
                for a in range(2):
                    at = t + ST * a
                    dve.tensor_scalar(xn[:, k, a, :], x_sb[:, ds(at, 1), :], mv[:, ds(at, 1), 0:1].squeeze(1),
                                      rstd[:, ds(at, 1)], ALU.subtract, ALU.mult).then_inc(s["xn"], 1)

            def low(t):
                for a in range(3):
                    dve.wait_ge(s["hi"], 3 * t + a + 1)
                    cols = ds(t * P, P)
                    take_lo(dve, into[a][1][:, :, cols], turn_ps[a], into[a][0][:, :, cols]).then_inc(s["lo"], 1)

            norm(0, 0, True)
            norm(1, 1, True)
            low(0)
            norm(2, 0, False)
            low(1)
            stats_of(1, 0)
            norm(3, 1, False)
            low(2)
            stats_of(1, 1)
            moments(1)
            reciprocal(1)
            with dve.Fori(2, ST // 2) as j:
                norm(2 * j, 0, False)
                low(2 * j - 1)
                norm(2 * j + 1, 1, False)
                low(2 * j)
            low(ST - 1)
            for c in range(KT):
                dve.wait_ge(s["M_hi"], c + 1)
                take_lo(dve, M_lo[:, c, :], M_ps[c], M_hi[:, c, :]).then_inc(s["M_lo"], 1)
            for t in range(TILES):
                dve.wait_ge(s["y_done"], t + 1)
                dve.tensor_tensor(x_sb[:, t, :], x_sb[:, t, :], psum[:, t % Y_BANKS, :], ALU.add).then_inc(s["y_added"], 1)

        @block.tensor
        def _(pe):
            def share(t, k, start=False):
                pe.wait_ge(w_in[k], 8 * t + 16 - 8 * k)
                for c in range(KT):
                    ins = pe.matmul(M_ps[c], wv[:, k, c * P:(c + 1) * P], wsum[:, ds(t, 1), :].squeeze(1),
                                    start=start, stop=False, skip_group_check=True)
                ins.then_inc(s["M_done"], 1)

            def unit(t, k, first):
                if not first:
                    share(t, k)
                for a in range(3):
                    if a == DX:
                        pe.wait_ge(s["dx"], t + 1)
                    else:
                        pe.wait_ge(s["xn"], 2 * t + a + 1)
                    if not (first and k == 0):
                        pe.wait_ge(s["lo"], 3 * t - 2 + a)
                    for c in range(KT):
                        ins = pe.transpose(turn_ps[a][:, c, :], xn[:, k, a, c * P:(c + 1) * P], ident[:, :])
                    ins.then_inc(s["turned"], 1)

            for k in range(2):
                share(k, k, k == 0)
            pairs(pe, unit)
            pe.wait_ge(s["set"], 1)
            for c in range(KT):
                ins = pe.matmul(M_ps[c], zero16[:, 0:P], zero16[:, :], start=False, stop=True, skip_group_check=True)
            ins.then_inc(s["M_made"], 1)
            pe.wait_ge(s["lo"], 3 * ST)
            for t in range(TILES):
                hi, lo = (x0T, xT)[t // ST]
                cols = slice((t % ST) * P, (t % ST + 1) * P)
                if t >= Y_BANKS:
                    pe.wait_ge(s["y_added"], t - Y_BANKS + 1)
                for c in range(KT):
                    if t == 0:
                        pe.wait_ge(s["M_lo"], c + 1)
                    ins = product3(pe, psum[:, t % Y_BANKS, :], hi[:, c, cols], lo[:, c, cols], M_hi[:, c, :], M_lo[:, c, :],
                                   c == 0, c == KT - 1)
                ins.then_inc(s["y_done"], 1)


def head_part(nc, psum, sem, x_sb, ident, xT, dT, spare, raw, piece_in, entry, dram):
    xT_hi, xT_lo = xT
    dT_hi, dT_lo = dT
    with ExitStack() as ctx:
        def buf(name, shape, dt=F32):
            return ctx.enter_context(nc.sbuf_tensor("h_" + name, shape, dt))

        PIECES, RING = PIECES_B, RING_B
        K_AT, V_AT, Q_AT, O_AT = 0, 1, 2, 2 + QPG
        CHUNKS = LEN // GROUP
        UNITS = ST
        ONCE = O_AT + 2
        kv_w = buf("kv_hi", [P, 2, DM], F32R), buf("kv_lo", [P, 2, DM], F32R)
        q_w = buf("q_hi", [P, 2, QPG, DM], F32R), buf("q_lo", [P, 2, QPG, DM], F32R)
        o_w = buf("o_hi", [P, 2, ONCE - O_AT, DM], F32R), buf("o_lo", [P, 2, ONCE - O_AT, DM], F32R)
        once_w = buf("once_hi", [P, PIECES - ONCE, DM], F32R), buf("once_lo", [P, PIECES - ONCE, DM], F32R)
        small = buf("small", [P, 4 * QPG + 1])
        dk = spare[:, 0:CHUNKS, :].rearrange("p c (t e) -> p c t e", t=GT)
        prod = spare[:, 2:4, :].rearrange("p b (h e) -> p b h e", h=QPG)
        dv_hi = buf("dv_hi", [P, CHUNKS, GROUP], F32R)
        dv_lo = buf("dv_lo", [P, CHUNKS, GROUP], F32R)
        dkT = spare[:, 4, :]
        diff = small[:, 0:2 * QPG].rearrange("p (b h) -> p b h", b=2)
        prob = small[:, 2 * QPG:4 * QPG].rearrange("p (b h) -> p b h", b=2)
        warm = small[:, 4 * QPG:4 * QPG + 1]
        names = ("warmed w_hi w_lo dk_done dkT dk_turned dk dv_done dv_hi dv_lo q_done prod diff prob o_done o_added")
        s = {n: sem("h_" + n) for n in names.split()}
        k_ps, v_ps = psum[:, 0, :], psum[:, 1, :]

        def part(a, slot, p):
            if p < Q_AT:
                return kv_w[a][:, p, :]
            if p < O_AT:
                return q_w[a][:, slot, p - Q_AT, :]
            if p < ONCE:
                return o_w[a][:, slot, p - O_AT, :]
            return once_w[a][:, p - ONCE, :]

        def groups(eng, group):
            group(0, 0)
            group(1, 1)
            with eng.Fori(1, KVB // 2 - 1) as j:
                group(2 * j, 0)
                group(2 * j + 1, 1)
            group(KVB - 2, 0)
            group(KVB - 1, 1)

        def is_first(g):
            return isinstance(g, int) and g == 0

        def is_last(g):
            return isinstance(g, int) and g == KVB - 1

        def early(n, least):
            return isinstance(n, int) and n < least

        block = ctx.enter_context(nc.Block())

        @block.sync
        def _(sp):
            def load(g, first):
                for p in range(RING if first else 0, PIECES):
                    sp.wait_ge(s["w_lo"], PIECES * g + p - RING + 1)
                    load_piece_b(sp, raw, piece_in, dram, g, p)

            load(0, True)
            with sp.Fori(1, KVB) as g:
                load(g, False)
            sp.wait_ge(s["w_lo"], PIECES * KVB)
            for j in range(2):
                entry.load_piece(sp, 1, j)

        @block.gpsimd
        def _(pool):
            def low_w(g, slot):
                for p in range(PIECES):
                    pool.wait_ge(s["w_hi"], PIECES * g + p + 1)
                    take_lo(pool, part(1, slot, p), raw[:, p % RING, :], part(0, slot, p)).then_inc(s["w_lo"], 1)

            groups(pool, lambda g, slot: None if is_first(g) else low_w(g, slot))

        @block.scalar
        def _(act):
            def high_w(g, slot, p):
                if p == K_AT and not early(g, 1):
                    act.wait_ge(s["dk_done"], CHUNKS * g)
                if p == V_AT and not early(g, 1):
                    act.wait_ge(s["dv_done"], CHUNKS * g)
                if Q_AT <= p < O_AT and not early(g, 2):
                    act.wait_ge(s["q_done"], UNITS * (g - 1))
                if O_AT <= p < ONCE and not early(g, 2):
                    act.wait_ge(s["o_done"], QPG * UNITS * (g - 1))
                if ONCE <= p and not early(g, 1):
                    act.wait_ge(s["o_done"], QPG * UNITS * g)
                act.wait_ge(piece_in[p % RING], 16 * (2 * g + p // RING + 1))
                take_hi(act, part(0, slot, p), raw[:, p % RING, :]).then_inc(s["w_hi"], 1)

            def keys(n):
                if not early(n, 1):
                    act.wait_ge(s["dk_turned"], n)
                act.wait_ge(s["dk_done"], n + 1)
                act.activation(dkT, k_ps, ACT.Copy).then_inc(s["dkT"], 1)

            def values(n, c):
                if not early(n, 2):
                    act.wait_ge(s["o_done"], QPG * GT * (n - 1))
                act.wait_ge(s["dv_done"], n + 1)
                take_hi(act, dv_hi[:, c, :], v_ps).then_inc(s["dv_hi"], 1)

            def turned_keys(n, c):
                if not early(n, 2):
                    act.wait_ge(s["prod"], GT * (n - 1))
                act.wait_ge(s["dk_turned"], n + 1)
                act.activation(dk[:, c, :, :], k_ps.rearrange("p (t e) -> p t e", t=GT), ACT.Copy).then_inc(s["dk"], 1)

            def weight(u, b):
                if not early(u, 2):
                    act.wait_ge(s["o_added"], QPG * (u - 1))
                act.wait_ge(s["diff"], u + 1)
                act.activation(prob[:, b, :], diff[:, b, :], ACT.Sigmoid, scale=SCALE_B).then_inc(s["prob"], 1)

            PER_UNIT = 2

            def group(g, slot):
                for t in range(UNITS):
                    u, n, c = UNITS * g + t, CHUNKS * g + t // GT + 1, (t // GT + 1) % CHUNKS
                    has_next = not (is_last(g) and t >= GT)
                    if t == 0 and not is_first(g):
                        for p in range(ONCE, PIECES):
                            high_w(g, slot, p)
                    weight(u, t % 2)
                    if t % GT == 1 and has_next:
                        keys(n)
                        values(n, c)
                    if t % GT == 2 and has_next:
                        turned_keys(n, c)
                    at = PER_UNIT * (t - 2)
                    if 0 <= at < ONCE and not is_last(g):
                        for p in range(at, at + PER_UNIT):
                            high_w(g + 1, 1 - slot, p)

            for p in range(PIECES):
                high_w(0, 0, p)
                if p == Q_AT:
                    keys(0)
                if p == Q_AT + 2:
                    values(0, 0)
            turned_keys(0, 0)
            entry.root(act, GROUPS)
            act.activation(warm, entry.eps[:, 0:1], ACT.Sigmoid).then_inc(s["warmed"], 1)
            groups(act, group)

        @block.vector
        def _(dve):
            def low_values(n, c):
                dve.wait_ge(s["dv_hi"], n + 1)
                take_lo(dve, dv_lo[:, c, :], v_ps, dv_hi[:, c, :]).then_inc(s["dv_lo"], 1)

            def differ(u, t):
                b = t % 2
                if not early(u, 2):
                    dve.wait_ge(s["prob"], u - 1)
                dve.wait_ge(s["q_done"], u + 1)
                q = psum[:, 2 + b, :].rearrange("p (h e) -> p h e", h=QPG)
                keys = dk[:, t // GT, t % GT, :].unsqueeze(1).broadcast_to([P, QPG, EB])
                dve.tensor_tensor(prod[:, b, :, :], q, keys, ALU.mult).then_inc(s["prod"], 1)
                dve.wait_ge(s["prod"], u + 1)
                dve.tensor_reduce(diff[:, b, :], prod[:, b, :, :], AX_X, ALU.add).then_inc(s["diff"], 1)

            def add(u, t):
                dve.wait_ge(s["prob"], u + 1)
                xt = x_sb[:, ST + t, :]
                for r in range(QPG):
                    if not early(u, 1) or r:
                        dve.wait_ge(s["o_added"], QPG * u + r)
                    dve.wait_ge(s["o_done"], QPG * u + r + 1)
                    dve.scalar_tensor_tensor(xt, psum[:, 4 + r, :], prob[:, t % 2, r:r + 1], xt,
                                             ALU.mult, ALU.add).then_inc(s["o_added"], 1)

            def group(g, slot):
                for t in range(UNITS):
                    u, n, c = UNITS * g + t, CHUNKS * g + t // GT + 1, (t // GT + 1) % CHUNKS
                    if t % GT == 0:
                        dve.wait_ge(s["dk"], n)
                    differ(u, t)
                    if not (is_first(g) and t == 0):
                        add(u - 1, (t - 1) % UNITS)
                    if t % GT == 1 and not (is_last(g) and t >= GT):
                        low_values(n, c)

            for p in range(PIECES):
                dve.wait_ge(s["w_hi"], p + 1)
                take_lo(dve, part(1, 0, p), raw[:, p % RING, :], part(0, 0, p)).then_inc(s["w_lo"], 1)
                if p == Q_AT + 2:
                    low_values(0, 0)
            for t in range(GT):
                entry.stat(dve, 0, t)
            entry.moments(dve, GROUPS)
            entry.reciprocal(dve, GROUPS)
            for t in range(GT):
                entry.norm(dve, 0, t)
            groups(dve, group)
            add(UNITS * KVB - 1, UNITS - 1)

        @block.tensor
        def _(pe):
            def product(g, n, c, p, out, name):
                pe.wait_ge(s["w_lo"], PIECES * g + p + 1)
                cols = slice(c * GROUP, (c + 1) * GROUP)
                for k in range(KT):
                    w = slice(k * P, (k + 1) * P)
                    ins = product3(pe, out, kv_w[0][:, p, w], kv_w[1][:, p, w], dT_hi[:, k, cols], dT_lo[:, k, cols],
                                   k == 0, k == KT - 1)
                ins.then_inc(s[name], 1)

            def keys_values(g, n, c):
                if not early(n, 1):
                    pe.wait_ge(s["dk"], n)
                product(g, n, c, K_AT, k_ps, "dk_done")
                if not early(n, 1):
                    pe.wait_ge(s["dv_lo"], n)
                product(g, n, c, V_AT, v_ps, "dv_done")

            def turn_keys(n):
                pe.wait_ge(s["dkT"], n + 1)
                for t in range(GT):
                    ins = pe.transpose(k_ps[:, t * P:(t + 1) * P], dkT[:, t * P:(t + 1) * P], ident[:, :])
                ins.then_inc(s["dk_turned"], 1)

            def queries(g, u, t, slot):
                pe.wait_ge(s["w_lo"], PIECES * g + O_AT)
                if not early(u, 2):
                    pe.wait_ge(s["prod"], u - 1)
                out = psum[:, 2 + t % 2, :].rearrange("p (h e) -> p h e", h=QPG)
                cols = slice(t * P, (t + 1) * P)
                for k in range(KT):
                    w = slice(k * P, (k + 1) * P)
                    ins = product3(pe, out, xT_hi[:, k, cols], xT_lo[:, k, cols], q_w[0][:, slot, :, w], q_w[1][:, slot, :, w],
                                   k == 0, k == KT - 1)
                ins.then_inc(s["q_done"], 1)

            def project(g, u, t, slot):
                if t % GT == 0:
                    pe.wait_ge(s["dv_lo"], CHUNKS * g + t // GT + 1)
                c, cols = t // GT, slice(t % GT * P, (t % GT + 1) * P)
                for r in range(QPG):
                    if t == 0:
                        pe.wait_ge(s["w_lo"], PIECES * g + O_AT + r + 1)
                    if not early(u, 1):
                        pe.wait_ge(s["o_added"], QPG * (u - 1) + r + 1)
                    product3(pe, psum[:, 4 + r, :], dv_hi[:, c, cols], dv_lo[:, c, cols],
                             part(0, slot, O_AT + r), part(1, slot, O_AT + r), True, True).then_inc(s["o_done"], 1)

            def group(g, slot):
                for t in range(UNITS):
                    u, n, c = UNITS * g + t, CHUNKS * g + t // GT + 1, (t // GT + 1) % CHUNKS
                    has_next = not (is_last(g) and t >= GT)
                    queries(g, u, t, slot)
                    if t:
                        project(g, u - 1, t - 1, slot)
                    elif not is_first(g):
                        project(g - 1, u - 1, UNITS - 1, 1 - slot)
                    if t % GT == 1 and has_next:
                        keys_values(g + (t // GT), n, c)
                    if t % GT == 2 and has_next:
                        turn_keys(n)

            keys_values(0, 0, 0)
            turn_keys(0)
            groups(pe, group)
            project(KVB - 1, UNITS * KVB - 1, UNITS - 1, 1)



def layer(nc, dram, out):
    with ExitStack() as ctx:
        x_sb = ctx.enter_context(nc.sbuf_tensor("x_sb", [P, TILES, DM], F32))
        ident = ctx.enter_context(nc.sbuf_tensor("ident", [P, P], F32))
        psum = ctx.enter_context(nc.psum_tensor("psum", [P, 8, 512], F32))

        def sem(name):
            return ctx.enter_context(nc.semaphore(name))

        def lasting(name, shape, dt=F32):
            return ctx.enter_context(nc.sbuf_tensor(name, shape, dt))

        entry = FfnEntry(lasting, sem, x_sb, dram)
        with ExitStack() as first:
            def buf(name, shape, dt=F32):
                return first.enter_context(nc.sbuf_tensor(name, shape, dt))

            qkvT = buf("qkvT", [P, 3, TOK])
            pre = {
                "wqk": buf("p_wqk", [P, 2, HA * EA]), "wvT": buf("p_wvT", [P, HEAD_TILES, W]),
                "wo": buf("p_wo", [P, HEAD_TILES, W]), "bq": buf("p_bq", [P, HEAD_TILES]),
                "bk": buf("p_bk", [P, HEAD_TILES]), "bv": buf("p_bv", [P, HEAD_TILES]), "bo": buf("p_bo", [P, 1]),
                "proj_w": buf("p_proj_w", [P, DM]), "proj_b": buf("p_proj_b", [P, DM]), "mask": buf("p_mask", [P, HPS * P]),
            }
            loads = [(pre[n][:], dram[n]) for n in pre]
            pre["loads"], pre["total"], pre["in"] = loads, 16 * len(loads), sem("p_in")
            conv_stage(nc, psum, sem, x_sb, ident, qkvT, pre, entry, dram)
            attention_a_stage(nc, psum, sem, x_sb, ident, qkvT, pre, entry, dram)
        with nc.sbuf_tensor("wsum", [P, KVB, DM], F32) as wsum:
            wv_in = [sem(f"wv_in{k}") for k in range(2)]
            ffn_stage(nc, psum, entry, ident, dram, 0, None, wsum, wv_in)
            attention_b_stage(nc, psum, sem, x_sb, ident, wsum, wv_in, entry, dram)
        ffn_stage(nc, psum, entry, ident, dram, 1, out, None, None)



def kernel(L0_attn_a_inputs, L0_attn_a_conv_w, L0_attn_a_conv_b, L0_attn_a_wq, L0_attn_a_bq, L0_attn_a_wk, L0_attn_a_bk,
           L0_attn_a_wv, L0_attn_a_bv, L0_attn_a_wo, L0_attn_a_bo, L0_attn_a_proj_w, L0_attn_a_proj_b,
           L0_attn_b_weight_qkv, L0_attn_b_weight_proj, L0_ffn_gate_w, L0_ffn_u, L0_ffn_g, L0_ffn_d):
    import numpy as np
    import concourse.bacc as bacc
    from concourse.bass_utils import run_bass_kernel_spmd

    def rows(a, n):
        return a.reshape(n, P, -1).transpose(1, 0, 2)

    def column(a):
        return a.reshape(-1, P).T

    def inner(a):
        return np.asarray(a).reshape(FT, P, KT, P).transpose(3, 0, 2, 1).reshape(P, FT, KT * P)

    wqkv = np.asarray(L0_attn_b_weight_qkv)
    wqkv_g = wqkv.reshape(KVB, ROWS_G // EB, EB, KT, P)
    pieces = wqkv_g.transpose(0, 1, 4, 3, 2).reshape(KVB, ROWS_G // EB, P, KT * EB)
    wprojT = np.asarray(L0_attn_b_weight_proj).T.reshape(KVB, QPG, EB, DM)
    order = [QPG, QPG + 1, *range(QPG)]
    spread = np.zeros((2 * EXPERTS, FF), np.float32)
    for e in range(EXPERTS):
        spread[e, e * INTER:(e + 1) * INTER] = 1
        spread[EXPERTS + e, e * INTER:(e + 1) * INTER] = 1
    arrays = {
        "x": np.asarray(L0_attn_a_inputs).reshape(TOK, DM),
        "conv_w": rows(np.asarray(L0_attn_a_conv_w).reshape(TAPS * DM, 3 * W), TAPS * KT),
        "conv_b": column(np.asarray(L0_attn_a_conv_b)),
        "wqk": np.stack([np.asarray(L0_attn_a_wq).reshape(W, HA * EA), np.asarray(L0_attn_a_wk).reshape(W, HA * EA)], 1),
        "wvT": rows(np.asarray(L0_attn_a_wv).reshape(W, HA * EA).T, HEAD_TILES),
        "wo": rows(np.asarray(L0_attn_a_wo).reshape(HA * EA, W), HEAD_TILES),
        "bq": column(np.asarray(L0_attn_a_bq)), "bk": column(np.asarray(L0_attn_a_bk)),
        "bv": column(np.asarray(L0_attn_a_bv)), "bo": column(np.asarray(L0_attn_a_bo)),
        "proj_w": np.asarray(L0_attn_a_proj_w),
        "proj_b": np.broadcast_to(np.asarray(L0_attn_a_proj_b)[None, :], (P, DM)),
        "mask": np.tile(np.triu(np.full((P, P), MASKED, np.float32), 1), (1, HPS)),
        "ident": np.eye(P, dtype=np.float32),
        "gate_w": rows(np.asarray(L0_ffn_gate_w).T, KT),
        "ffn_w": np.stack([inner(L0_ffn_g), inner(L0_ffn_u), rows(np.asarray(L0_ffn_d).T, FT)], 2),
        "spread": spread,
        "rank": np.tile(np.arange(EXPERTS, 0, -1, dtype=np.float32), (P, 1)),
        "wB": np.concatenate([pieces[:, order], wprojT], 1).reshape(KVB * (2 + 2 * QPG), P, DM),
        "wv": wqkv.reshape(KVB, QPG + 2, EB, DM)[:, QPG + 1].transpose(1, 0, 2),
        "wpT": wprojT.transpose(0, 2, 1, 3),
    }
    nc = bacc.Bacc("TRN2", target_bir_lowering=False, num_devices=1)
    dram, sent = {}, {}
    for name, a in arrays.items():
        a = np.ascontiguousarray(a)
        sent["in_" + name] = a
        dram[name] = nc.dram_tensor("in_" + name, a.shape, mybir.dt.from_np(a.dtype), kind="ExternalInput").ap()
    out = nc.dram_tensor("out", (TOK, DM), F32, kind="ExternalOutput").ap()
    layer(nc, dram, out)
    r = run_bass_kernel_spmd(nc, [sent], core_ids=[0])
    return r.results[0]["out"].reshape(SEQS, LEN, DM)
```
